# Optimizing a Trainium2 kernel written in Bass

```python
import numpy as np
import jax
import jax.numpy as jnp

def _softmax(x, axis=-1):
    return jax.nn.softmax(x, axis=axis)

def _gelu(x):
    return jax.nn.gelu(x, approximate=True)

def _silu(x):
    return jax.nn.silu(x)

def _sigmoid(x):
    return jax.nn.sigmoid(x)

def _layernorm(x, axis=-1, eps=1e-05):
    m = jnp.mean(x, axis=axis, keepdims=True)
    v = jnp.var(x, axis=axis, keepdims=True)
    return (x - m) / jnp.sqrt(v + eps)

def _scatter_add(tgt, idx, src, axis=0):
    return tgt.at[idx].add(src)

def _segment_sum(src, seg, n):
    return jax.ops.segment_sum(src, seg, n)
kernel_name = 'mk_xattn_ffn_d4_seqx_r8_908b7e'

def setup_inputs(seed: int=0):
    np.random.seed(seed)
    _w = jnp.asarray

    def _rec_inputs():
        import jax
        import jax.numpy as jnp
        _rk = jax.random.key(seed)
        x = -0.0002928 + 1 * jax.random.normal(jax.random.fold_in(_rk, 1), (4, 256, 128), jnp.float32)
        _lenS = 256 - jax.random.randint(jax.random.fold_in(_rk, 7), (4,), 0, max(1, 256 // 4) + 1, jnp.int32)
        _lenS2 = 256 - jax.random.randint(jax.random.fold_in(_rk, 8), (4,), 0, max(1, 256 // 4) + 1, jnp.int32)
        _ctx_1024P = jax.random.normal(jax.random.fold_in(_rk, 11), (4, 16, 128), jnp.float32)
        _ctx_1024c = jax.random.dirichlet(jax.random.fold_in(_rk, 511), 0.3 * jnp.ones((16,), jnp.float32), (4, 256))
        _ctx_1024t = jnp.einsum('bsk,bkd->bsd', _ctx_1024c, _ctx_1024P)
        _ctx_1024t = _ctx_1024t * jax.lax.rsqrt(jnp.mean(jnp.square(_ctx_1024t)) + 1e-12) * 0.953939
        ctx_1024 = -1.39393e-06 + 0.999914 * (_ctx_1024t + 0.3 * jax.random.normal(jax.random.fold_in(_rk, 611), (4, 256, 128), jnp.float32))
        itok_BxS_0_7 = jax.random.randint(jax.random.fold_in(_rk, 14), (4, 256), 0, 8, jnp.int32)
        itok_BxS_0_4092 = jax.random.randint(jax.random.fold_in(_rk, 15), (4, 256), 0, 4093, jnp.int32)
        _validS = jnp.arange(256)[None, :] < _lenS[:, None]
        _validS2 = jnp.arange(256)[None, :] < _lenS2[:, None]
        _causal = jnp.tril(jnp.ones((256, 256), dtype=bool))
        mask_1x1xSxS2_bk1 = jnp.broadcast_to(_validS2[0:1, None, None, :], (1, 1, 256, 256))
        mask_BxS2_bf1 = jnp.ones((4, 256), dtype=bool)
        return (x, ctx_1024, itok_BxS_0_7, itok_BxS_0_4092, mask_1x1xSxS2_bk1, mask_BxS2_bf1)
    x, ctx_1024, itok_BxS_0_7, itok_BxS_0_4092, mask_1x1xSxS2_bk1, mask_BxS2_bf1 = _rec_inputs()

    def _L0_xattn_setup():
        import jax, jax.numpy as jnp
        import numpy as np
        import math
        B, S, D_MODEL = (2, 256, 128)
        NUM_HEADS, D_KEY, D_VALUE = (16, 64, 64)
        key = jax.random.key(seed)
        ks = jax.random.split(key, 7)
        query = jax.random.normal(ks[0], (B, S, D_MODEL), dtype=jnp.float32)
        k_in = jax.random.normal(ks[1], (B, S, D_MODEL), dtype=jnp.float32)
        v_in = jax.random.normal(ks[2], (B, S, D_MODEL), dtype=jnp.float32)
        mask = jnp.triu(jnp.ones((S, S), dtype=bool), k=1)[None, None, :, :]
        scale = 1.0 / math.sqrt(D_MODEL)
        w_q = jax.random.normal(ks[3], (D_MODEL, NUM_HEADS * D_KEY), dtype=jnp.float32) * scale
        w_k = jax.random.normal(ks[4], (D_MODEL, NUM_HEADS * D_KEY), dtype=jnp.float32) * scale
        w_v = jax.random.normal(ks[5], (D_MODEL, NUM_HEADS * D_VALUE), dtype=jnp.float32) * scale
        w_o = jax.random.normal(ks[6], (NUM_HEADS * D_VALUE, D_MODEL), dtype=jnp.float32) * scale
        return {'query': query, 'key': k_in, 'value': v_in, 'mask': mask, 'w_q': w_q, 'w_k': w_k, 'w_v': w_v, 'w_o': w_o}
    _L0_xattn_all = _L0_xattn_setup()
    _L0_xattn_in = {k: v for k, v in _L0_xattn_all.items() if k in ('w_q', 'w_k', 'w_v', 'w_o')}
    del _L0_xattn_all

    def _L0_ffn_setup():
        import jax, jax.numpy as jnp
        import numpy as np
        DIM = 128
        DEPTH = 2
        HEADS = 8
        DIM_HEAD = 64
        WINDOW = 64
        INNER = HEADS * DIM_HEAD
        HID = int(DIM * 4 * 2 / 3)
        B, N = (2, 1024)
        QK_SCALE = 8.0

        def shift_token(t):
            t1, t2 = jnp.split(t, 2, axis=-1)
            t2 = jnp.pad(t2, ((0, 0), (1, 0), (0, 0)))[:, :-1]
            return jnp.concatenate([t1, t2], axis=-1)

        def l2norm(t):
            return t / jnp.clip(jnp.linalg.norm(t, axis=-1, keepdims=True), 1e-12)

        def rotate_half(x):
            x1, x2 = jnp.split(x, 2, axis=-1)
            return jnp.concatenate([-x2, x1], axis=-1)

        def rotary_xpos(q, k):
            n = q.shape[-2]
            half_idx = jnp.arange(0, DIM_HEAD, 2, dtype=jnp.float32)
            inv_freq = 1.0 / 10000.0 ** (half_idx / DIM_HEAD)
            t = jnp.arange(n, dtype=jnp.float32)
            freqs = t[:, None] * inv_freq[None, :]
            freqs = jnp.concatenate([freqs, freqs], axis=-1)
            base = (half_idx + 0.4 * DIM_HEAD) / (1.4 * DIM_HEAD)
            power = (t - n // 2) / float(WINDOW // 2)
            scale = base[None, :] ** power[:, None]
            scale = jnp.concatenate([scale, scale], axis=-1)
            cos, sin = (jnp.cos(freqs), jnp.sin(freqs))
            q = q * cos * scale + rotate_half(q) * sin * scale
            k = k * cos / scale + rotate_half(k) * sin / scale
            return (q, k)

        def local_attention(q, k, v):
            b, h, n, d = q.shape
            w = n // WINDOW
            bq = q.reshape(b, h, w, WINDOW, d) * QK_SCALE
            bk = k.reshape(b, h, w, WINDOW, d)
            bv = v.reshape(b, h, w, WINDOW, d)

            def look_around(t):
                p = jnp.pad(t, ((0, 0), (0, 0), (1, 0), (0, 0), (0, 0)))
                return jnp.concatenate([p[:, :, :w], p[:, :, 1:]], axis=3)
            bk, bv = (look_around(bk), look_around(bv))
            bt = jnp.arange(n).reshape(w, WINDOW)
            btp = jnp.pad(bt, ((1, 0), (0, 0)), constant_values=-1)
            btk = jnp.concatenate([btp[:w], btp[1:]], axis=1)
            sim = jnp.einsum('bhwid,bhwjd->bhwij', bq, bk)
            i = bt[:, :, None]
            j = btk[:, None, :]
            mask = (i < j) | (i > j + WINDOW) | (j == -1)
            sim = jnp.where(mask, -jnp.finfo(sim.dtype).max, sim)
            attn = jax.nn.softmax(sim, axis=-1)
            out = jnp.einsum('bhwij,bhwjd->bhwid', attn, bv)
            return out.reshape(b, h, n, d)

        def _layer(x, wqkv, qs, ksc, wo, lg, lb, w1, b1, w2, b2):
            b, n, _ = x.shape
            h = shift_token(x)
            qkv = h @ wqkv
            q, k, v = jnp.split(qkv, 3, axis=-1)
            to_heads = lambda t: t.reshape(b, n, HEADS, DIM_HEAD).transpose(0, 2, 1, 3)
            q, k, v = (to_heads(q), to_heads(k), to_heads(v))
            q = l2norm(q) * qs
            k = l2norm(k) * ksc
            q, k = rotary_xpos(q, k)
            o = local_attention(q, k, v)
            o = o.transpose(0, 2, 1, 3).reshape(b, n, INNER)
            x = x + o @ wo
            h = shift_token(x)
            mu = h.mean(-1, keepdims=True)
            var = h.var(-1, keepdims=True)
            h = (h - mu) / jnp.sqrt(var + 1e-05) * lg + lb
            h = h @ w1 + b1
            a, g = jnp.split(h, 2, axis=-1)
            h = a * jax.nn.gelu(g, approximate=False)
            x = x + h @ w2 + b2
            return x
        key = jax.random.key(seed)
        ks = jax.random.split(key, 6)
        return {'x': jax.random.normal(ks[0], (B, N, DIM), jnp.float32), 'wqkv': jax.random.normal(ks[1], (DEPTH, DIM, 3 * INNER), jnp.float32) * 0.02, 'q_scale': jnp.ones((DEPTH, DIM_HEAD), jnp.float32), 'k_scale': jnp.ones((DEPTH, DIM_HEAD), jnp.float32), 'wo': jax.random.normal(ks[2], (DEPTH, INNER, DIM), jnp.float32) * 0.02, 'ln_g': jnp.ones((DEPTH, DIM), jnp.float32), 'ln_b': jnp.zeros((DEPTH, DIM), jnp.float32), 'w1': jax.random.normal(ks[3], (DEPTH, DIM, 2 * HID), jnp.float32) * 0.02, 'b1': jnp.zeros((DEPTH, 2 * HID), jnp.float32), 'w2': jax.random.normal(ks[4], (DEPTH, HID, DIM), jnp.float32) * 0.02, 'b2': jnp.zeros((DEPTH, DIM), jnp.float32)}
    _L0_ffn_all = _L0_ffn_setup()
    _L0_ffn_in = {k: v for k, v in _L0_ffn_all.items() if k in ('wqkv', 'q_scale', 'k_scale', 'wo', 'ln_g', 'ln_b', 'w1', 'b1', 'w2', 'b2')}
    del _L0_ffn_all

    def _L1_xattn_setup():
        import jax, jax.numpy as jnp
        import numpy as np
        DIM = 128
        HEADS = 16
        DIM_HEAD = 64
        INNER = HEADS * DIM_HEAD
        EPS = 1e-05

        def layer_norm(x, gamma, beta):
            mu = jnp.mean(x, axis=-1, keepdims=True)
            var = jnp.var(x, axis=-1, keepdims=True)
            return (x - mu) * jax.lax.rsqrt(var + EPS) * gamma + beta
        key = jax.random.key(seed)
        ks = jax.random.split(key, 8)
        b, n, m = (8, 512, 64)
        x = jax.random.normal(ks[0], (b, n, DIM), dtype=jnp.float32)
        latents = jax.random.normal(ks[1], (b, m, DIM), dtype=jnp.float32)
        mask = jnp.ones((b, n), dtype=bool)
        s = 0.02
        Wq = jax.random.normal(ks[2], (DIM, INNER), dtype=jnp.float32) * s
        Wkv = jax.random.normal(ks[3], (DIM, 2 * INNER), dtype=jnp.float32) * s
        Wout = jax.random.normal(ks[4], (INNER, DIM), dtype=jnp.float32) * s
        g_x = jnp.ones((DIM,), jnp.float32)
        b_x = jnp.zeros((DIM,), jnp.float32)
        g_l = jnp.ones((DIM,), jnp.float32)
        b_l = jnp.zeros((DIM,), jnp.float32)
        g_o = jnp.ones((DIM,), jnp.float32)
        b_o = jnp.zeros((DIM,), jnp.float32)
        return {'x': x, 'latents': latents, 'mask': mask, 'g_x': g_x, 'b_x': b_x, 'g_l': g_l, 'b_l': b_l, 'Wq': Wq, 'Wkv': Wkv, 'Wout': Wout, 'g_o': g_o, 'b_o': b_o}
    _L1_xattn_all = _L1_xattn_setup()
    _L1_xattn_in = {k: v for k, v in _L1_xattn_all.items() if k in ('g_x', 'b_x', 'g_l', 'b_l', 'Wq', 'Wkv', 'Wout', 'g_o', 'b_o')}
    del _L1_xattn_all

    def _L1_ffn_setup():
        import jax, jax.numpy as jnp
        import numpy as np
        TOP_K = 2

        def _mlp(x, w_fc, w_proj):
            return jnp.square(jax.nn.relu(x @ w_fc.T)) @ w_proj.T
        key = jax.random.key(seed)
        ks = jax.random.split(key, 6)
        B, S, D, E = (4, 256, 128, 8)
        d_ff = 4 * D
        x = jax.random.normal(ks[0], (B, S, D), dtype=jnp.float32)
        router_w = jax.random.normal(ks[1], (E, D), dtype=jnp.float32) * 0.02
        w_fc = jax.random.normal(ks[2], (E, d_ff, D), dtype=jnp.float32) * 0.02
        w_proj = jax.random.normal(ks[3], (E, D, d_ff), dtype=jnp.float32) * 0.02
        shared_fc = jax.random.normal(ks[4], (d_ff, D), dtype=jnp.float32) * 0.02
        shared_proj = jax.random.normal(ks[5], (D, d_ff), dtype=jnp.float32) * 0.02
        return {'x': x, 'router_w': router_w, 'w_fc': w_fc, 'w_proj': w_proj, 'shared_fc': shared_fc, 'shared_proj': shared_proj}
    _L1_ffn_all = _L1_ffn_setup()
    _L1_ffn_in = {k: v for k, v in _L1_ffn_all.items() if k in ('router_w', 'w_fc', 'w_proj', 'shared_fc', 'shared_proj')}
    del _L1_ffn_all

    def _L2_xattn_setup():
        import math
        import jax, jax.numpy as jnp
        import numpy as np
        B, T, L, H = (4, 512, 512, 128)

        def _forward(hidden_states, advisor_states, advisor_ids, pointer_ids, Wqj, Wkj, Wvj, Wqi, Wki, Wvi, Wout, gain, council_weights):
            b, t, h = hidden_states.shape
            l = advisor_states.shape[1]
            inv_sqrt_h = 1.0 / math.sqrt(float(h))
            p = pointer_ids[:, :, None]
            indices = jnp.clip(jnp.concatenate([p, p + 1, p + 2], axis=-1), 0, l - 1)
            win_states = jax.vmap(lambda a, idx: a[idx])(advisor_states, indices)
            win_ids = jax.vmap(lambda a, idx: a[idx])(advisor_ids, indices)
            qj = hidden_states @ Wqj.T
            kj = win_states @ Wkj.T
            vj = win_states @ Wvj.T
            sj = jnp.einsum('bth,btwh->btw', qj, kj) * inv_sqrt_h
            l_rel, l_v1, l_v2 = (sj[:, :, 0], sj[:, :, 1], sj[:, :, 2])
            rel_ids = win_ids[:, :, 0]
            is_and = (rel_ids == 0).astype(sj.dtype)
            is_or = (rel_ids == 1).astype(sj.dtype)
            is_not = (rel_ids == 2).astype(sj.dtype)
            is_implies = (rel_ids == 3).astype(sj.dtype)
            is_xor = (rel_ids == 4).astype(sj.dtype)
            l_new = is_and * (l_v1 + l_v2) + is_or * jnp.maximum(l_v1, l_v2) + is_not * -l_v1 + is_implies * jnp.maximum(-l_v1, l_v2) + is_xor * jnp.abs(l_v1 - l_v2)
            mask_any = jnp.clip(is_and + is_or + is_not + is_implies + is_xor, 0.0, 1.0)
            l_final = mask_any * l_new + (1.0 - mask_any) * l_rel
            sj = jnp.stack([l_final, l_v1, l_v2], axis=-1)
            aj = jax.nn.softmax(sj, axis=-1)
            cj = jnp.einsum('btw,btwh->bth', aj, vj)
            qi = hidden_states @ Wqi.T
            ki = win_states @ Wki.T
            vi = win_states @ Wvi.T
            si = jnp.einsum('bth,btwh->btw', qi, ki) * inv_sqrt_h
            ai = jax.nn.softmax(si, axis=-1)
            ci = jnp.einsum('btw,btwh->bth', ai, vi)
            w = jax.nn.softmax(council_weights, axis=0)
            context = w[0] * cj + w[1] * ci
            return context @ Wout.T * gain
        key = jax.random.key(seed)
        ks = jax.random.split(key, 12)
        inp = {'hidden_states': jax.random.normal(ks[0], (B, T, H), jnp.float32), 'advisor_states': jax.random.normal(ks[1], (B, L, H), jnp.float32), 'advisor_ids': jax.random.randint(ks[2], (B, L), 0, 8, jnp.int32), 'pointer_ids': jax.random.randint(ks[3], (B, T), 0, L - 2, jnp.int32)}
        s = 1.0 / math.sqrt(H)
        names = ['Wqj', 'Wkj', 'Wvj', 'Wqi', 'Wki', 'Wvi', 'Wout']
        for i, n in enumerate(names):
            inp[n] = jax.random.normal(ks[4 + i], (H, H), jnp.float32) * s
        inp['gain'] = jnp.asarray(0.1, jnp.float32)
        inp['council_weights'] = jnp.ones((2,), jnp.float32)
        return inp
    _L2_xattn_all = _L2_xattn_setup()
    _L2_xattn_in = {k: v for k, v in _L2_xattn_all.items() if k in ('Wqj', 'Wkj', 'Wvj', 'Wqi', 'Wki', 'Wvi', 'Wout', 'gain', 'council_weights')}
    del _L2_xattn_all

    def _L2_ffn_setup():
        import jax, jax.numpy as jnp
        import numpy as np
        EPS_LN = 1e-05
        EPS_GATE = 1e-08

        def layer_norm(x, gamma, beta):
            mu = jnp.mean(x, axis=-1, keepdims=True)
            var = jnp.mean(jnp.square(x - mu), axis=-1, keepdims=True)
            return (x - mu) * jax.lax.rsqrt(var + EPS_LN) * gamma + beta
        key = jax.random.key(seed)
        ks = jax.random.split(key, 8)
        B, S, D, E, H = (4, 512, 128, 4, 256)
        s_in = 1.0 / np.sqrt(D)
        s_h = 1.0 / np.sqrt(H)
        return {'h': jax.random.normal(ks[0], (B, S, D), dtype=jnp.float32), 'router_w': jax.random.uniform(ks[1], (E, D), jnp.float32, -s_in, s_in), 'rn_g': jnp.ones((D,), jnp.float32), 'rn_b': jnp.zeros((D,), jnp.float32), 'w1': jax.random.uniform(ks[2], (E, D, H), jnp.float32, -s_in, s_in), 'ln_g': jnp.ones((E, H), jnp.float32), 'ln_b': jnp.zeros((E, H), jnp.float32), 'w2': jax.random.uniform(ks[3], (E, H, D), jnp.float32, -s_h, s_h), 'on_g': jnp.ones((D,), jnp.float32), 'on_b': jnp.zeros((D,), jnp.float32)}
    _L2_ffn_all = _L2_ffn_setup()
    _L2_ffn_in = {k: v for k, v in _L2_ffn_all.items() if k in ('router_w', 'rn_g', 'rn_b', 'w1', 'ln_g', 'ln_b', 'w2', 'on_g', 'on_b')}
    del _L2_ffn_all

    def _L3_xattn_setup():
        import jax, jax.numpy as jnp
        import numpy as np
        INF = 10000000000.0
        D_KEY = 128
        key = jax.random.key(seed)
        k1, k2, k3 = jax.random.split(key, 3)
        B, S, D = (8, 256, D_KEY)
        return {'query': jax.random.normal(k1, (B, S, D), dtype=jnp.float32), 'key': jax.random.normal(k2, (B, S, D), dtype=jnp.float32), 'value': jax.random.normal(k3, (B, S, D), dtype=jnp.float32)}
    _L3_xattn_all = _L3_xattn_setup()
    _L3_xattn_in = {k: v for k, v in _L3_xattn_all.items() if k in ()}
    del _L3_xattn_all

    def _L3_ffn_setup():
        import math
        import jax, jax.numpy as jnp
        import numpy as np
        HIDDEN = 128
        INTER = 512
        EXPERTS = 8
        B, T = (4, 256)
        EPS = 1e-12
        CAP_FACTOR = 1.0
        MIN_CAP = 4

        def layer_norm(x, g, b, eps=EPS):
            m = jnp.mean(x, axis=-1, keepdims=True)
            v = jnp.var(x, axis=-1, keepdims=True)
            return (x - m) * jax.lax.rsqrt(v + eps) * g + b

        def top1_gate(x, wg, capacity):
            logits = x @ wg
            gates = jax.nn.softmax(logits, axis=-1)
            E = wg.shape[-1]
            idx = jnp.argmax(gates, axis=-1)
            mask1 = jax.nn.one_hot(idx, E, dtype=gates.dtype)
            locations = jnp.cumsum(mask1, axis=0) - mask1
            mask1 = mask1 * (locations < capacity).astype(gates.dtype)
            gates1_s = jnp.sum(gates * mask1, axis=-1)
            loc_s = jnp.sum(locations * mask1, axis=-1).astype(jnp.int32)
            loc_oh = jax.nn.one_hot(loc_s, capacity, dtype=gates.dtype)
            combine = gates1_s[:, None, None] * mask1[:, :, None] * loc_oh[:, None, :]
            dispatch = jax.lax.stop_gradient((combine > 0).astype(x.dtype))
            return (combine, dispatch)
        key = jax.random.key(seed)
        ks = jax.random.split(key, 8)
        s = 0.02
        return {'x': jax.random.normal(ks[0], (B, T, HIDDEN), jnp.float32), 'attn_nw': jnp.ones((HIDDEN,), jnp.float32), 'attn_nb': jnp.zeros((HIDDEN,), jnp.float32), 'wg': jax.random.normal(ks[1], (HIDDEN, EXPERTS), jnp.float32) * s, 'inter_w': jax.random.normal(ks[2], (EXPERTS, HIDDEN, INTER), jnp.float32) * s, 'inter_b': jnp.zeros((EXPERTS, INTER), jnp.float32), 'output_w': jax.random.normal(ks[3], (EXPERTS, INTER, HIDDEN), jnp.float32) * s, 'output_b': jnp.zeros((EXPERTS, HIDDEN), jnp.float32), 'res_inter_w': jax.random.normal(ks[4], (HIDDEN, INTER), jnp.float32) * s, 'res_inter_b': jnp.zeros((INTER,), jnp.float32), 'res_output_w': jax.random.normal(ks[5], (INTER, HIDDEN), jnp.float32) * s, 'res_output_b': jnp.zeros((HIDDEN,), jnp.float32), 'res_coef': jax.random.normal(ks[6], (HIDDEN, 2), jnp.float32) * s}
    _L3_ffn_all = _L3_ffn_setup()
    _L3_ffn_in = {k: v for k, v in _L3_ffn_all.items() if k in ('attn_nw', 'attn_nb', 'wg', 'inter_w', 'inter_b', 'output_w', 'output_b', 'res_inter_w', 'res_inter_b', 'res_output_w', 'res_output_b', 'res_coef')}
    del _L3_ffn_all
    return {'x': x, 'ctx_1024': ctx_1024, 'itok_BxS_0_7': itok_BxS_0_7, 'itok_BxS_0_4092': itok_BxS_0_4092, 'mask_1x1xSxS2_bk1': mask_1x1xSxS2_bk1, 'mask_BxS2_bf1': mask_BxS2_bf1, 'L0_xattn_w_q': _L0_xattn_in['w_q'], 'L0_xattn_w_k': _L0_xattn_in['w_k'], 'L0_xattn_w_v': _L0_xattn_in['w_v'], 'L0_xattn_w_o': _L0_xattn_in['w_o'], 'L0_ffn_wqkv': _L0_ffn_in['wqkv'], 'L0_ffn_q_scale': _L0_ffn_in['q_scale'], 'L0_ffn_k_scale': _L0_ffn_in['k_scale'], 'L0_ffn_wo': _L0_ffn_in['wo'], 'L0_ffn_ln_g': _L0_ffn_in['ln_g'], 'L0_ffn_ln_b': _L0_ffn_in['ln_b'], 'L0_ffn_w1': _L0_ffn_in['w1'], 'L0_ffn_b1': _L0_ffn_in['b1'], 'L0_ffn_w2': _L0_ffn_in['w2'], 'L0_ffn_b2': _L0_ffn_in['b2'], 'L1_xattn_g_x': _L1_xattn_in['g_x'], 'L1_xattn_b_x': _L1_xattn_in['b_x'], 'L1_xattn_g_l': _L1_xattn_in['g_l'], 'L1_xattn_b_l': _L1_xattn_in['b_l'], 'L1_xattn_Wq': _L1_xattn_in['Wq'], 'L1_xattn_Wkv': _L1_xattn_in['Wkv'], 'L1_xattn_Wout': _L1_xattn_in['Wout'], 'L1_xattn_g_o': _L1_xattn_in['g_o'], 'L1_xattn_b_o': _L1_xattn_in['b_o'], 'L1_ffn_router_w': _L1_ffn_in['router_w'], 'L1_ffn_w_fc': _L1_ffn_in['w_fc'], 'L1_ffn_w_proj': _L1_ffn_in['w_proj'], 'L1_ffn_shared_fc': _L1_ffn_in['shared_fc'], 'L1_ffn_shared_proj': _L1_ffn_in['shared_proj'], 'L2_xattn_Wqj': _L2_xattn_in['Wqj'], 'L2_xattn_Wkj': _L2_xattn_in['Wkj'], 'L2_xattn_Wvj': _L2_xattn_in['Wvj'], 'L2_xattn_Wqi': _L2_xattn_in['Wqi'], 'L2_xattn_Wki': _L2_xattn_in['Wki'], 'L2_xattn_Wvi': _L2_xattn_in['Wvi'], 'L2_xattn_Wout': _L2_xattn_in['Wout'], 'L2_xattn_gain': _L2_xattn_in['gain'], 'L2_xattn_council_weights': _L2_xattn_in['council_weights'], 'L2_ffn_router_w': _L2_ffn_in['router_w'], 'L2_ffn_rn_g': _L2_ffn_in['rn_g'], 'L2_ffn_rn_b': _L2_ffn_in['rn_b'], 'L2_ffn_w1': _L2_ffn_in['w1'], 'L2_ffn_ln_g': _L2_ffn_in['ln_g'], 'L2_ffn_ln_b': _L2_ffn_in['ln_b'], 'L2_ffn_w2': _L2_ffn_in['w2'], 'L2_ffn_on_g': _L2_ffn_in['on_g'], 'L2_ffn_on_b': _L2_ffn_in['on_b'], 'L3_ffn_attn_nw': _L3_ffn_in['attn_nw'], 'L3_ffn_attn_nb': _L3_ffn_in['attn_nb'], 'L3_ffn_wg': _L3_ffn_in['wg'], 'L3_ffn_inter_w': _L3_ffn_in['inter_w'], 'L3_ffn_inter_b': _L3_ffn_in['inter_b'], 'L3_ffn_output_w': _L3_ffn_in['output_w'], 'L3_ffn_output_b': _L3_ffn_in['output_b'], 'L3_ffn_res_inter_w': _L3_ffn_in['res_inter_w'], 'L3_ffn_res_inter_b': _L3_ffn_in['res_inter_b'], 'L3_ffn_res_output_w': _L3_ffn_in['res_output_w'], 'L3_ffn_res_output_b': _L3_ffn_in['res_output_b'], 'L3_ffn_res_coef': _L3_ffn_in['res_coef']}

def reference(x, ctx_1024, itok_BxS_0_7, itok_BxS_0_4092, mask_1x1xSxS2_bk1, mask_BxS2_bf1, L0_xattn_w_q, L0_xattn_w_k, L0_xattn_w_v, L0_xattn_w_o, L0_ffn_wqkv, L0_ffn_q_scale, L0_ffn_k_scale, L0_ffn_wo, L0_ffn_ln_g, L0_ffn_ln_b, L0_ffn_w1, L0_ffn_b1, L0_ffn_w2, L0_ffn_b2, L1_xattn_g_x, L1_xattn_b_x, L1_xattn_g_l, L1_xattn_b_l, L1_xattn_Wq, L1_xattn_Wkv, L1_xattn_Wout, L1_xattn_g_o, L1_xattn_b_o, L1_ffn_router_w, L1_ffn_w_fc, L1_ffn_w_proj, L1_ffn_shared_fc, L1_ffn_shared_proj, L2_xattn_Wqj, L2_xattn_Wkj, L2_xattn_Wvj, L2_xattn_Wqi, L2_xattn_Wki, L2_xattn_Wvi, L2_xattn_Wout, L2_xattn_gain, L2_xattn_council_weights, L2_ffn_router_w, L2_ffn_rn_g, L2_ffn_rn_b, L2_ffn_w1, L2_ffn_ln_g, L2_ffn_ln_b, L2_ffn_w2, L2_ffn_on_g, L2_ffn_on_b, L3_ffn_attn_nw, L3_ffn_attn_nb, L3_ffn_wg, L3_ffn_inter_w, L3_ffn_inter_b, L3_ffn_output_w, L3_ffn_output_b, L3_ffn_res_inter_w, L3_ffn_res_inter_b, L3_ffn_res_output_w, L3_ffn_res_output_b, L3_ffn_res_coef):
    import jax
    import jax.numpy as jnp

    def _L0_xattn_ref(query, key, value, mask, w_q, w_k, w_v, w_o):
        import jax, jax.numpy as jnp
        import numpy as np
        import math
        B, S, D_MODEL = (2, 256, 128)
        NUM_HEADS, D_KEY, D_VALUE = (16, 64, 64)
        b, sq, _ = query.shape
        sk = key.shape[1]
        q = (query @ w_q).reshape(b, sq, NUM_HEADS, D_KEY).transpose(0, 2, 1, 3)
        k = (key @ w_k).reshape(b, sk, NUM_HEADS, D_KEY).transpose(0, 2, 1, 3)
        v = (value @ w_v).reshape(b, sk, NUM_HEADS, D_VALUE).transpose(0, 2, 1, 3)
        scores = jnp.einsum('bhqd,bhkd->bhqk', q, k) / math.sqrt(D_KEY)
        scores = jnp.where(mask, -jnp.inf, scores)
        attn = jax.nn.softmax(scores, axis=-1)
        out = jnp.einsum('bhqk,bhkd->bhqd', attn, v)
        out = out.transpose(0, 2, 1, 3).reshape(b, sq, NUM_HEADS * D_VALUE)
        return out @ w_o

    def _L0_ffn_ref(x, wqkv, q_scale, k_scale, wo, ln_g, ln_b, w1, b1, w2, b2):
        import jax, jax.numpy as jnp
        import numpy as np
        DIM = 128
        DEPTH = 2
        HEADS = 8
        DIM_HEAD = 64
        WINDOW = 64
        INNER = HEADS * DIM_HEAD
        HID = int(DIM * 4 * 2 / 3)
        B, N = (2, 1024)
        QK_SCALE = 8.0

        def shift_token(t):
            t1, t2 = jnp.split(t, 2, axis=-1)
            t2 = jnp.pad(t2, ((0, 0), (1, 0), (0, 0)))[:, :-1]
            return jnp.concatenate([t1, t2], axis=-1)

        def l2norm(t):
            return t / jnp.clip(jnp.linalg.norm(t, axis=-1, keepdims=True), 1e-12)

        def rotate_half(x):
            x1, x2 = jnp.split(x, 2, axis=-1)
            return jnp.concatenate([-x2, x1], axis=-1)

        def rotary_xpos(q, k):
            n = q.shape[-2]
            half_idx = jnp.arange(0, DIM_HEAD, 2, dtype=jnp.float32)
            inv_freq = 1.0 / 10000.0 ** (half_idx / DIM_HEAD)
            t = jnp.arange(n, dtype=jnp.float32)
            freqs = t[:, None] * inv_freq[None, :]
            freqs = jnp.concatenate([freqs, freqs], axis=-1)
            base = (half_idx + 0.4 * DIM_HEAD) / (1.4 * DIM_HEAD)
            power = (t - n // 2) / float(WINDOW // 2)
            scale = base[None, :] ** power[:, None]
            scale = jnp.concatenate([scale, scale], axis=-1)
            cos, sin = (jnp.cos(freqs), jnp.sin(freqs))
            q = q * cos * scale + rotate_half(q) * sin * scale
            k = k * cos / scale + rotate_half(k) * sin / scale
            return (q, k)

        def local_attention(q, k, v):
            b, h, n, d = q.shape
            w = n // WINDOW
            bq = q.reshape(b, h, w, WINDOW, d) * QK_SCALE
            bk = k.reshape(b, h, w, WINDOW, d)
            bv = v.reshape(b, h, w, WINDOW, d)

            def look_around(t):
                p = jnp.pad(t, ((0, 0), (0, 0), (1, 0), (0, 0), (0, 0)))
                return jnp.concatenate([p[:, :, :w], p[:, :, 1:]], axis=3)
            bk, bv = (look_around(bk), look_around(bv))
            bt = jnp.arange(n).reshape(w, WINDOW)
            btp = jnp.pad(bt, ((1, 0), (0, 0)), constant_values=-1)
            btk = jnp.concatenate([btp[:w], btp[1:]], axis=1)
            sim = jnp.einsum('bhwid,bhwjd->bhwij', bq, bk)
            i = bt[:, :, None]
            j = btk[:, None, :]
            mask = (i < j) | (i > j + WINDOW) | (j == -1)
            sim = jnp.where(mask, -jnp.finfo(sim.dtype).max, sim)
            attn = jax.nn.softmax(sim, axis=-1)
            out = jnp.einsum('bhwij,bhwjd->bhwid', attn, bv)
            return out.reshape(b, h, n, d)

        def _layer(x, wqkv, qs, ksc, wo, lg, lb, w1, b1, w2, b2):
            b, n, _ = x.shape
            h = shift_token(x)
            qkv = h @ wqkv
            q, k, v = jnp.split(qkv, 3, axis=-1)
            to_heads = lambda t: t.reshape(b, n, HEADS, DIM_HEAD).transpose(0, 2, 1, 3)
            q, k, v = (to_heads(q), to_heads(k), to_heads(v))
            q = l2norm(q) * qs
            k = l2norm(k) * ksc
            q, k = rotary_xpos(q, k)
            o = local_attention(q, k, v)
            o = o.transpose(0, 2, 1, 3).reshape(b, n, INNER)
            x = x + o @ wo
            h = shift_token(x)
            mu = h.mean(-1, keepdims=True)
            var = h.var(-1, keepdims=True)
            h = (h - mu) / jnp.sqrt(var + 1e-05) * lg + lb
            h = h @ w1 + b1
            a, g = jnp.split(h, 2, axis=-1)
            h = a * jax.nn.gelu(g, approximate=False)
            x = x + h @ w2 + b2
            return x
        for l in range(DEPTH):
            x = _layer(x, wqkv[l], q_scale[l], k_scale[l], wo[l], ln_g[l], ln_b[l], w1[l], b1[l], w2[l], b2[l])
        return x

    def _L1_xattn_ref(x, latents, mask, g_x, b_x, g_l, b_l, Wq, Wkv, Wout, g_o, b_o):
        import jax, jax.numpy as jnp
        import numpy as np
        DIM = 128
        HEADS = 16
        DIM_HEAD = 64
        INNER = HEADS * DIM_HEAD
        EPS = 1e-05

        def layer_norm(x, gamma, beta):
            mu = jnp.mean(x, axis=-1, keepdims=True)
            var = jnp.var(x, axis=-1, keepdims=True)
            return (x - mu) * jax.lax.rsqrt(var + EPS) * gamma + beta
        scale = DIM_HEAD ** (-0.5)
        xn = layer_norm(x, g_x, b_x)
        ln = layer_norm(latents, g_l, b_l)
        b, m = (ln.shape[0], ln.shape[1])
        q = jnp.einsum('bnd,de->bne', ln, Wq)
        kv_in = jnp.concatenate([xn, ln], axis=1)
        kv = jnp.einsum('bnd,de->bne', kv_in, Wkv)
        k, v = jnp.split(kv, 2, axis=-1)

        def split_heads(t):
            return t.reshape(t.shape[0], t.shape[1], HEADS, DIM_HEAD).transpose(0, 2, 1, 3)
        q, k, v = (split_heads(q), split_heads(k), split_heads(v))
        q = q * scale
        sim = jnp.einsum('bhid,bhjd->bhij', q, k)
        full_mask = jnp.concatenate([mask, jnp.ones((b, m), dtype=bool)], axis=1)
        max_neg = -jnp.finfo(sim.dtype).max
        sim = jnp.where(full_mask[:, None, None, :], sim, max_neg)
        attn = jax.nn.softmax(sim, axis=-1)
        out = jnp.einsum('bhij,bhjd->bhid', attn, v)
        out = out.transpose(0, 2, 1, 3).reshape(b, m, INNER)
        out = jnp.einsum('bne,ed->bnd', out, Wout)
        return layer_norm(out, g_o, b_o)

    def _L1_ffn_ref(x, router_w, w_fc, w_proj, shared_fc, shared_proj):
        import jax, jax.numpy as jnp
        import numpy as np
        TOP_K = 2

        def _mlp(x, w_fc, w_proj):
            return jnp.square(jax.nn.relu(x @ w_fc.T)) @ w_proj.T
        B, S, D = x.shape
        E = router_w.shape[0]
        T = B * S
        flat = x.reshape(T, D)
        logits = flat @ router_w.T
        probs = jax.nn.softmax(logits.astype(jnp.float32), axis=-1)
        topk_p, topk_i = jax.lax.top_k(probs, TOP_K)
        topk_w = (topk_p / jnp.maximum(topk_p.sum(-1, keepdims=True), 1e-09)).astype(flat.dtype)
        combine = jnp.zeros((T, E), dtype=flat.dtype)
        combine = combine.at[jnp.arange(T)[:, None], topk_i].add(topk_w)
        out = jnp.zeros_like(flat)
        for e in range(E):
            out = out + _mlp(flat, w_fc[e], w_proj[e]) * combine[:, e:e + 1]
        out = out + _mlp(flat, shared_fc, shared_proj)
        return out.reshape(B, S, D)

    def _L2_xattn_ref(hidden_states, advisor_states, advisor_ids, pointer_ids, Wqj, Wkj, Wvj, Wqi, Wki, Wvi, Wout, gain, council_weights):
        import math
        import jax, jax.numpy as jnp
        import numpy as np
        B, T, L, H = (4, 512, 512, 128)

        def _forward(hidden_states, advisor_states, advisor_ids, pointer_ids, Wqj, Wkj, Wvj, Wqi, Wki, Wvi, Wout, gain, council_weights):
            b, t, h = hidden_states.shape
            l = advisor_states.shape[1]
            inv_sqrt_h = 1.0 / math.sqrt(float(h))
            p = pointer_ids[:, :, None]
            indices = jnp.clip(jnp.concatenate([p, p + 1, p + 2], axis=-1), 0, l - 1)
            win_states = jax.vmap(lambda a, idx: a[idx])(advisor_states, indices)
            win_ids = jax.vmap(lambda a, idx: a[idx])(advisor_ids, indices)
            qj = hidden_states @ Wqj.T
            kj = win_states @ Wkj.T
            vj = win_states @ Wvj.T
            sj = jnp.einsum('bth,btwh->btw', qj, kj) * inv_sqrt_h
            l_rel, l_v1, l_v2 = (sj[:, :, 0], sj[:, :, 1], sj[:, :, 2])
            rel_ids = win_ids[:, :, 0]
            is_and = (rel_ids == 0).astype(sj.dtype)
            is_or = (rel_ids == 1).astype(sj.dtype)
            is_not = (rel_ids == 2).astype(sj.dtype)
            is_implies = (rel_ids == 3).astype(sj.dtype)
            is_xor = (rel_ids == 4).astype(sj.dtype)
            l_new = is_and * (l_v1 + l_v2) + is_or * jnp.maximum(l_v1, l_v2) + is_not * -l_v1 + is_implies * jnp.maximum(-l_v1, l_v2) + is_xor * jnp.abs(l_v1 - l_v2)
            mask_any = jnp.clip(is_and + is_or + is_not + is_implies + is_xor, 0.0, 1.0)
            l_final = mask_any * l_new + (1.0 - mask_any) * l_rel
            sj = jnp.stack([l_final, l_v1, l_v2], axis=-1)
            aj = jax.nn.softmax(sj, axis=-1)
            cj = jnp.einsum('btw,btwh->bth', aj, vj)
            qi = hidden_states @ Wqi.T
            ki = win_states @ Wki.T
            vi = win_states @ Wvi.T
            si = jnp.einsum('bth,btwh->btw', qi, ki) * inv_sqrt_h
            ai = jax.nn.softmax(si, axis=-1)
            ci = jnp.einsum('btw,btwh->bth', ai, vi)
            w = jax.nn.softmax(council_weights, axis=0)
            context = w[0] * cj + w[1] * ci
            return context @ Wout.T * gain
        return _forward(hidden_states, advisor_states, advisor_ids, pointer_ids, Wqj, Wkj, Wvj, Wqi, Wki, Wvi, Wout, gain, council_weights)

    def _L2_ffn_ref(h, router_w, rn_g, rn_b, w1, ln_g, ln_b, w2, on_g, on_b):
        import jax, jax.numpy as jnp
        import numpy as np
        EPS_LN = 1e-05
        EPS_GATE = 1e-08

        def layer_norm(x, gamma, beta):
            mu = jnp.mean(x, axis=-1, keepdims=True)
            var = jnp.mean(jnp.square(x - mu), axis=-1, keepdims=True)
            return (x - mu) * jax.lax.rsqrt(var + EPS_LN) * gamma + beta
        D = h.shape[-1]
        h_norm = layer_norm(h, rn_g, rn_b)
        g = jax.nn.softmax(jnp.einsum('bsd,ed->bse', h_norm, router_w), axis=-1)
        top2_w, top2_idx = jax.lax.top_k(g, 2)
        top2_w = top2_w / (jnp.sum(top2_w, axis=-1, keepdims=True) + EPS_GATE)
        hid = jnp.einsum('bsd,edh->bseh', h, w1)
        hid = jax.nn.relu(layer_norm(hid, ln_g, ln_b))
        expert_out = jnp.einsum('bseh,ehd->bsed', hid, w2)
        idx = jnp.broadcast_to(top2_idx[..., None], top2_idx.shape + (D,))
        top2_out = jnp.take_along_axis(expert_out, idx, axis=-2)
        out = jnp.sum(top2_out * top2_w[..., None], axis=-2)
        return layer_norm(out, on_g, on_b)

    def _L3_xattn_ref(query, key, value):
        import jax, jax.numpy as jnp
        import numpy as np
        INF = 10000000000.0
        D_KEY = 128
        scale = jnp.asarray(np.sqrt(D_KEY), dtype=query.dtype)
        dots = jnp.einsum('bqd,bkd->bqk', query, key)
        S = key.shape[1]
        tri = jnp.triu(jnp.ones((S, S), dtype=dots.dtype), k=1) * INF
        dots = dots - tri[None, :, :]
        attn = jax.nn.softmax(dots / scale, axis=-1)
        return jnp.einsum('bqk,bkd->bqd', attn, value)

    def _L3_ffn_ref(x, attn_nw, attn_nb, wg, inter_w, inter_b, output_w, output_b, res_inter_w, res_inter_b, res_output_w, res_output_b, res_coef):
        import math
        import jax, jax.numpy as jnp
        import numpy as np
        HIDDEN = 128
        INTER = 512
        EXPERTS = 8
        B, T = (4, 256)
        EPS = 1e-12
        CAP_FACTOR = 1.0
        MIN_CAP = 4

        def layer_norm(x, g, b, eps=EPS):
            m = jnp.mean(x, axis=-1, keepdims=True)
            v = jnp.var(x, axis=-1, keepdims=True)
            return (x - m) * jax.lax.rsqrt(v + eps) * g + b

        def top1_gate(x, wg, capacity):
            logits = x @ wg
            gates = jax.nn.softmax(logits, axis=-1)
            E = wg.shape[-1]
            idx = jnp.argmax(gates, axis=-1)
            mask1 = jax.nn.one_hot(idx, E, dtype=gates.dtype)
            locations = jnp.cumsum(mask1, axis=0) - mask1
            mask1 = mask1 * (locations < capacity).astype(gates.dtype)
            gates1_s = jnp.sum(gates * mask1, axis=-1)
            loc_s = jnp.sum(locations * mask1, axis=-1).astype(jnp.int32)
            loc_oh = jax.nn.one_hot(loc_s, capacity, dtype=gates.dtype)
            combine = gates1_s[:, None, None] * mask1[:, :, None] * loc_oh[:, None, :]
            dispatch = jax.lax.stop_gradient((combine > 0).astype(x.dtype))
            return (combine, dispatch)
        Bx, Tx, M = x.shape
        S = Bx * Tx
        E = wg.shape[-1]
        capacity = max(MIN_CAP, math.ceil(S / E * CAP_FACTOR))
        residual = x.reshape(S, M)
        attn_out = layer_norm(residual, attn_nw, attn_nb)
        combine, dispatch = top1_gate(attn_out, wg, capacity)
        dispatched = jnp.einsum('sec,sm->ecm', dispatch, attn_out)
        h = jax.nn.gelu(jnp.einsum('ecm,emi->eci', dispatched, inter_w) + inter_b[:, None, :], approximate=True)
        expert_out = jnp.einsum('eci,eim->ecm', h, output_w) + output_b[:, None, :]
        moe_out = jnp.einsum('sec,ecm->sm', combine, expert_out)
        rh = jax.nn.gelu(attn_out @ res_inter_w + res_inter_b, approximate=True)
        res_mlp_out = rh @ res_output_w + res_output_b
        coef = jax.nn.softmax(attn_out @ res_coef, axis=-1)
        out = res_mlp_out * coef[:, :1] + moe_out * coef[:, 1:]
        out = out + residual
        return out.reshape(Bx, Tx, M)
    x = x + _L0_xattn_ref(_layernorm(x, axis=-1), ctx_1024, ctx_1024, mask_1x1xSxS2_bk1, L0_xattn_w_q, L0_xattn_w_k, L0_xattn_w_v, L0_xattn_w_o)
    x = x + _L0_ffn_ref(_layernorm(x, axis=-1), L0_ffn_wqkv, L0_ffn_q_scale, L0_ffn_k_scale, L0_ffn_wo, L0_ffn_ln_g, L0_ffn_ln_b, L0_ffn_w1, L0_ffn_b1, L0_ffn_w2, L0_ffn_b2)
    x = x + _L1_xattn_ref(ctx_1024, _layernorm(x, axis=-1), mask_BxS2_bf1, L1_xattn_g_x, L1_xattn_b_x, L1_xattn_g_l, L1_xattn_b_l, L1_xattn_Wq, L1_xattn_Wkv, L1_xattn_Wout, L1_xattn_g_o, L1_xattn_b_o)
    x = x + _L1_ffn_ref(_layernorm(x, axis=-1), L1_ffn_router_w, L1_ffn_w_fc, L1_ffn_w_proj, L1_ffn_shared_fc, L1_ffn_shared_proj)
    x = x + _L2_xattn_ref(_layernorm(x, axis=-1), ctx_1024, itok_BxS_0_7, itok_BxS_0_4092, L2_xattn_Wqj, L2_xattn_Wkj, L2_xattn_Wvj, L2_xattn_Wqi, L2_xattn_Wki, L2_xattn_Wvi, L2_xattn_Wout, L2_xattn_gain, L2_xattn_council_weights)
    x = x + _L2_ffn_ref(_layernorm(x, axis=-1), L2_ffn_router_w, L2_ffn_rn_g, L2_ffn_rn_b, L2_ffn_w1, L2_ffn_ln_g, L2_ffn_ln_b, L2_ffn_w2, L2_ffn_on_g, L2_ffn_on_b)
    x = x + _L3_xattn_ref(_layernorm(x, axis=-1), ctx_1024, ctx_1024)
    x = x + _L3_ffn_ref(_layernorm(x, axis=-1), L3_ffn_attn_nw, L3_ffn_attn_nb, L3_ffn_wg, L3_ffn_inter_w, L3_ffn_inter_b, L3_ffn_output_w, L3_ffn_output_b, L3_ffn_res_inter_w, L3_ffn_res_inter_b, L3_ffn_res_output_w, L3_ffn_res_output_b, L3_ffn_res_coef)
    return x

_drawn_inputs = setup_inputs


def setup_inputs(seed=0):
    import zlib

    import numpy as np

    out = dict(_drawn_inputs(seed))
    spreads = {'L0_ffn_q_scale': (1.0, 0.6),
     'L0_ffn_k_scale': (1.0, 0.6),
     'L0_ffn_ln_g': (1.0, 0.6),
     'L0_ffn_ln_b': (0.0, 0.8),
     'L0_ffn_b1': (0.0, 0.8),
     'L0_ffn_b2': (0.0, 0.1),
     'L1_xattn_g_x': (1.0, 0.2),
     'L1_xattn_b_x': (0.0, 0.1),
     'L1_xattn_g_l': (1.0, 0.2),
     'L1_xattn_b_l': (0.0, 0.1),
     'L1_xattn_g_o': (1.0, 0.2),
     'L1_xattn_b_o': (0.0, 0.1),
     'L2_xattn_council_weights': (1.0, 0.6),
     'L2_ffn_rn_g': (1.0, 0.2),
     'L2_ffn_rn_b': (0.0, 0.1),
     'L2_ffn_ln_g': (1.0, 0.2),
     'L2_ffn_ln_b': (0.0, 0.1),
     'L2_ffn_on_g': (1.0, 0.2),
     'L2_ffn_on_b': (0.0, 0.1),
     'L3_ffn_attn_nw': (1.0, 0.6),
     'L3_ffn_attn_nb': (0.0, 0.8),
     'L3_ffn_inter_b': (0.0, 0.8),
     'L3_ffn_output_b': (0.0, 0.8),
     'L3_ffn_res_inter_b': (0.0, 0.8),
     'L3_ffn_res_output_b': (0.0, 0.719)}
    factors = {'L0_ffn_w1': 3.389,
     'L0_ffn_w2': 3.806,
     'L1_xattn_Wq': 2.997,
     'L1_ffn_router_w': 6.395,
     'L1_ffn_w_fc': 5.09,
     'L1_ffn_w_proj': 5.513,
     'L1_ffn_shared_fc': 3.491,
     'L1_ffn_shared_proj': 4.402,
     'L2_xattn_Wqj': 64.0,
     'L2_xattn_Wkj': 64.0,
     'L2_xattn_Wqi': 64.0,
     'L2_xattn_Wki': 64.0,
     'L3_ffn_wg': 8.0,
     'L3_ffn_inter_w': 8.0,
     'L3_ffn_output_w': 8.0,
     'L3_ffn_res_inter_w': 8.0,
     'L3_ffn_res_output_w': 7.726,
     'L3_ffn_res_coef': 8.0,
     'L2_xattn_Wvi': 8.0}
    for name, (base, spread) in spreads.items():
        noise = np.random.default_rng([zlib.crc32(name.encode()), seed]).standard_normal(out[name].shape)
        drawn = base * np.exp(spread * noise) if base else spread * noise
        out[name] = jnp.asarray(drawn.astype(out[name].dtype))
    for name, factor in factors.items():
        out[name] = (out[name] * factor).astype(out[name].dtype)
    return out
```

```python
import numpy as np
import concourse.bass as bass
from concourse import mybir
from contextlib import ExitStack

F32 = mybir.dt.float32
BF16 = mybir.dt.bfloat16
I32 = mybir.dt.int32
U32 = mybir.dt.uint32
U8 = mybir.dt.uint8
ALU = mybir.AluOpType
ACT = mybir.ActivationFunctionType
AX = mybir.AxisListType

B, S, D = 4, 256, 128
P = 128
NT = S // P
DH = 64
H16, H8 = 16, 8
BANK = 512
HID = 341
HC = [(0, 128), (128, 128), (256, HID - 256)]
NE1, FF = 8, 512
NE2, H2 = 4, 256
NE3, CAP = 8, B * S // 8
MASKED = -1.0e30


def linker(engine, sem):
    count = [0]

    def link(ins):
        count[0] += 1
        ins.then_inc(sem, 1)
        engine.wait_ge(sem, count[0])
    return link


class Net:

    def __init__(self, nc, es):
        self.nc, self.es = nc, es
        self.pool = [es.enter_context(nc.semaphore(f"phase_{i}")) for i in range(40)]

    def sb(self, name, shape, dt=F32):
        return self.es.enter_context(self.nc.sbuf_tensor(name, shape, dt))

    def sem(self, name):
        return self.es.enter_context(self.nc.semaphore(name))

    def signals(self, n):
        return self.pool[:n]

    def end_phase(self):
        self.nc.all_engine_barrier(sems_to_clear=range(self.pool[0].num, self.pool[-1].num + 1))



def dve_stats(nc, link, net, rows, n, eps, var_ready):
    for t in range(n):
        last = nc.vector.bn_stats(net.stats[:, t, :], rows(t))
    link(last)
    for t in range(n):
        last = nc.vector.bn_aggr(net.mv[:, t, :], net.stats[:, t, :])
    link(last)
    nc.vector.tensor_scalar(net.veps[:, 0:n], net.mv[:, 0:n, 1], eps, None, ALU.add).then_inc(var_ready, 1)


def act_rsqrt_seed(nc, act, link, net, n, var_ready, k, seed_ready):
    act.wait_ge(var_ready, k)
    link(nc.scalar.activation(net.lnv[:, 0:n], net.veps[:, 0:n], ACT.Ln))
    nc.scalar.activation(net.seed[:, 0:n], net.lnv[:, 0:n], ACT.Exp, scale=-0.5).then_inc(seed_ready, 1)


def dve_rsqrt(nc, dve, link, net, n, seed_ready, k, out, factor=1.0):
    dve.wait_ge(seed_ready, k)
    link(nc.vector.tensor_tensor(net.nwt[:, 0:n], net.seed[:, 0:n], net.seed[:, 0:n], ALU.mult))
    link(nc.vector.tensor_tensor(net.nwt[:, 0:n], net.nwt[:, 0:n], net.veps[:, 0:n], ALU.mult))
    link(nc.vector.tensor_scalar(net.nwt[:, 0:n], net.nwt[:, 0:n], -0.5 * factor, 1.5 * factor, ALU.mult, ALU.add))
    link(nc.vector.tensor_tensor(out, net.nwt[:, 0:n], net.seed[:, 0:n], ALU.mult))


def dve_normalise(nc, net, out, rows, n):
    for t in range(n):
        last = nc.vector.tensor_scalar(out(t), rows(t), net.mv[:, t, 0:1], net.rstd[:, t:t + 1],
                                       ALU.subtract, ALU.mult)
    return last



def pe_projections(nc, pe, net, tiles, banks, tile_ready, emptied):
    for j, products in enumerate(tiles):
        if j >= banks:
            pe.wait_ge(emptied[j % 2], (j - banks) // 2 + 1)
        for a, b, stationary, moving in products:
            last = nc.tensor.matmul(net.ps[:, j % banks, a:b], stationary, moving, start=True, stop=True)
        last.then_inc(tile_ready, 1)


def empty_projections(nc, engine, copy, net, outs, banks, which, tile_ready, emptied):
    for j, out in enumerate(outs):
        if j % 2 == which:
            engine.wait_ge(tile_ready, j + 1)
            copy(out, net.ps[:, j % banks, :]).then_inc(emptied[which], 1)


def evac_counts(n):
    return ((n + 1) // 2, n // 2)



class Attention:

    def __init__(self, net, units, nk, d, qT, kT, v, mask_l, mask_r, scale, scale_ap, sums, groups, sems):
        self.net, self.units, self.nk, self.d, self.qT, self.kT, self.v = net, units, nk, d, qT, kT, v
        self.mask_l, self.mask_r, self.scale, self.scale_ap = mask_l, mask_r, scale, scale_ap
        self.sums, self.groups = sums, groups
        (self.scores_ready, self.negmax_ready, self.probs_ready, self.turned,
         self.turned_copied, self.pv_done, self.group_done) = sems
        self.nq = len(units[0][1])
        self.kt = nk // P

    def pe(self, nc, pe):
        net, nq, kt, U = self.net, self.nq, self.kt, len(self.units)
        for step in range(U + 2):
            if step < U:
                u = step
                h, qts, _, _ = self.units[u]
                if u >= 2:
                    pe.wait_ge(self.probs_ready, nq * (u - 1))
                bank = net.ps[:, u % 2, :]
                nc.tensor.matmul(bank, self.mask_l, self.mask_r, start=True, stop=False)
                for i, qt in enumerate(qts):
                    last = nc.tensor.matmul(bank[:, i * self.nk:(i + 1) * self.nk], self.qT(h, qt), self.kT(h),
                                            start=False, stop=i == nq - 1)
                last.then_inc(self.scores_ready, 1)
            if 1 <= step <= U:
                u = step - 1
                pe.wait_ge(self.probs_ready, nq * (u + 1))
                if u >= 2:
                    pe.wait_ge(self.turned_copied, u - 1)
                for c in range(4):
                    last = nc.tensor.transpose(net.ps[:, 2 + u % 2, c * P:(c + 1) * P],
                                               net.probs[:, u % 2, c * P:(c + 1) * P], net.ident[:])
                last.then_inc(self.turned, 1)
            if step >= 2:
                u = step - 2
                h, qts, obanks, col = self.units[u]
                pe.wait_ge(self.turned_copied, u + 1)
                for i in range(nq):
                    for k in range(kt):
                        c = i * kt + k
                        last = nc.tensor.matmul(net.ps[:, obanks[i], col:col + self.d],
                                                net.probsT[:, u % 2, c * P:(c + 1) * P], self.v(h, k),
                                                start=k == 0, stop=k == kt - 1)
                last.then_inc(self.pv_done, 1)

    def act(self, nc, act):
        net, nq = self.net, self.nq
        for u, (h, qts, _, _) in enumerate(self.units):
            act.wait_ge(self.negmax_ready, u + 1)
            if u >= 2:
                act.wait_ge(self.turned, u - 1)
            for i, qt in enumerate(qts):
                scale = self.scale if self.scale_ap is None else self.scale_ap(h, qt)
                nc.scalar.activation(net.probs[:, u % 2, i * self.nk:(i + 1) * self.nk],
                                     net.ps[:, u % 2, i * self.nk:(i + 1) * self.nk], ACT.Exp,
                                     bias=net.negmax[:, u % 4, i:i + 1], scale=scale,
                                     accum_out=self.sums(h, qt)).then_inc(self.probs_ready, 1)

    def dve(self, nc, dve, link):
        net, nq, U = self.net, self.nq, len(self.units)

        def finish(g):
            last_unit, bank, sums, out = self.groups[g]
            dve.wait_ge(self.pv_done, last_unit + 1)
            n = sums.shape[-1]
            link(nc.vector.reciprocal(net.recip[:, g, 0:n], sums))
            nc.vector.tensor_tensor(out, net.ps[:, bank, 0:n * self.d].rearrange("p (h d) -> p h d", d=self.d),
                                    net.recip[:, g, 0:n].unsqueeze(2).to_broadcast([P, n, self.d]),
                                    ALU.mult).then_inc(self.group_done, 1)

        done = 0
        for step in range(U + 1):
            if step < U:
                u = step
                h, qts, _, _ = self.units[u]
                dve.wait_ge(self.scores_ready, u + 1)
                link(nc.vector.reduce_max(net.rowmax[:, u % 4, 0:nq],
                                          net.ps[:, u % 2, :].rearrange("p (q k) -> p q k", q=nq), AX.X))
                if self.scale_ap is None:
                    nc.vector.tensor_scalar(net.negmax[:, u % 4, 0:nq], net.rowmax[:, u % 4, 0:nq],
                                            -self.scale, None, ALU.mult).then_inc(self.negmax_ready, 1)
                else:
                    nc.vector.scalar_tensor_tensor(net.negmax[:, u % 4, 0:nq], net.rowmax[:, u % 4, 0:nq], -1.0,
                                                   self.scale_all(h), ALU.mult, ALU.mult).then_inc(self.negmax_ready, 1)
            if step >= 1:
                u = step - 1
                dve.wait_ge(self.turned, u + 1)
                if u >= 2:
                    dve.wait_ge(self.pv_done, u - 1)
                nc.vector.tensor_copy(net.probsT[:, u % 2, :], net.ps[:, 2 + u % 2, :]).then_inc(self.turned_copied, 1)
            while done < len(self.groups) and self.groups[done][0] + 3 <= step:
                finish(done)
                done += 1
        while done < len(self.groups):
            finish(done)
            done += 1


def head_rows(h):
    return slice(DH * (h % 2), DH * (h % 2) + DH)



def pe_out_projection(nc, pe, net, chunks, w, waits, turned, copied, result):
    for j in range(chunks // 2):
        for sem, val in waits if j == 0 else []:
            pe.wait_ge(sem, val)
        for m in range(2):
            for t in range(NT):
                last = nc.tensor.transpose(net.ps[:, j, (m * NT + t) * P:(m * NT + t + 1) * P],
                                           net.heads[:, t, (2 * j + m) * P:(2 * j + m + 1) * P], net.ident[:])
        last.then_inc(turned, 1)
    for t in range(NT):
        for c in range(chunks):
            if t == 0 and c % 2 == 0:
                j = c // 2
                pe.wait_ge(copied[j % 2], j // 2 + 1)
            last = nc.tensor.matmul(net.ps[:, 4, t * P:(t + 1) * P], net.qT[:, c, t * P:(t + 1) * P], w[:, c, :],
                                    start=c == 0, stop=c == chunks - 1)
    last.then_inc(result, 1)


def copy_out_chunks(nc, engine, copy, net, chunks, which, turned, copied):
    for j in range(chunks // 2):
        if j % 2 == which:
            engine.wait_ge(turned, j + 1)
            copy(net.qT[:, 2 * j:2 * j + 2, 0:S], net.ps[:, j, :].rearrange("p (m s) -> p m s", m=2)).then_inc(copied[which], 1)



def layer0_attention(net):
    nc = net.nc
    (loaded, dve_link, act_link, var_ready, seed_ready, rows_ready, zT_turned, zT_ready, tile_ready, act_emptied,
     dve_emptied, o_turned, act_copied, dve_copied, o_ready, *att) = net.signals(22)
    emptied, copied = (act_emptied, dve_emptied), (act_copied, dve_copied)
    w = net.w0
    tiles, outs = [], []
    for m in range(0, 8, 2):
        tiles.append([(i * S, (i + 1) * S, w["k"][:, (m + i) * P:(m + i + 1) * P], net.ctxT[:]) for i in range(2)])
        outs.append(net.kT[:, m:m + 2, 0:S])
    for t in range(NT):
        for half in range(2):
            tiles.append([(0, BANK, net.ctxT[:, t * P:(t + 1) * P], w["v"][:, half * BANK:(half + 1) * BANK])])
            outs.append(net.v[:, t, half * BANK:(half + 1) * BANK])
    n_ctx = len(tiles)
    for m in range(0, 8, 2):
        tiles.append([(i * S, (i + 1) * S, w["q"][:, (m + i) * P:(m + i + 1) * P], net.zT[:]) for i in range(2)])
        outs.append(net.qT[:, m:m + 2, :])
    counts = evac_counts(len(tiles))
    units = [(h, (0, 1), (4 + 2 * (h // 8), 5 + 2 * (h // 8)), DH * (h % 8)) for h in range(H16)]
    groups = [(8 * g + 7, 4 + 2 * g + t, net.sums[:, t, 8 * g:8 * g + 8],
               net.heads[:, t, g * BANK:(g + 1) * BANK].rearrange("p (h d) -> p h d", d=DH))
              for g in range(2) for t in range(NT)]
    attn = Attention(net, units, S, DH,
                     lambda h, qt: net.qT[head_rows(h), h // 2, qt * P:(qt + 1) * P],
                     lambda h: net.kT[head_rows(h), h // 2, 0:S],
                     lambda h, k: net.v[:, k, h * DH:(h + 1) * DH],
                     net.ident_b[:], net.mask0[:], DH ** -0.5, None, lambda h, qt: net.sums[:, qt, h:h + 1], groups, att)

    with nc.Block() as block:
        @block.sync
        def _(sp):
            b = net.batch
            sp.dma_start(net.ctxT[:], net.d["ctxT"][bass.ds(b, 1), :, :].rearrange("b d s -> d (b s)")).then_inc(loaded, 16)
            sp.dma_start(net.x[:], net.d["x"][bass.ds(b, 1), :, :].rearrange("b (t p) d -> p (b t) d", p=P)).then_inc(loaded, 16)
            sp.dma_start(net.ctx[:], net.d["ctx"][bass.ds(b, 1), :, :].rearrange("b (t p) d -> p (b t) d", p=P)).then_inc(loaded, 16)
            sp.dma_start(net.ptr_i[:], net.d["ptr"][bass.ds(b, 1), :, :].rearrange("b p t -> p (b t)")).then_inc(loaded, 16)
            sp.dma_start(net.ids_i[:], net.d["ids"][bass.ds(b, 1), :]).then_inc(loaded, 16)
            sp.dma_start(net.kmask_u[:], net.d["kmask"][bass.ds(b, 1), :]).then_inc(loaded, 16)
            sp.wait_ge(loaded, 96)

        @block.vector
        def _(dve):
            link = linker(dve, dve_link)
            dve.wait_ge(loaded, 96)
            dve_stats(nc, link, net, lambda t: net.x[:, t, :], NT, 1e-5, var_ready)
            dve_rsqrt(nc, dve, link, net, NT, seed_ready, 1, net.rstd[:, 0:NT])
            dve_normalise(nc, net, lambda t: net.z[:, t, :], lambda t: net.x[:, t, :], NT).then_inc(rows_ready, 1)
            empty_projections(nc, dve, nc.vector.tensor_copy, net, outs, 8, 1, tile_ready, emptied)
            attn.dve(nc, dve, link)
            copy_out_chunks(nc, dve, nc.vector.tensor_copy, net, 8, 1, o_turned, copied)
            dve.wait_ge(o_ready, 1)
            nc.vector.tensor_tensor(net.x[:], net.x[:], net.ps[:, 4, 0:S].rearrange("p (t d) -> p t d", d=D), ALU.add)

        @block.scalar
        def _(act):
            link = linker(act, act_link)
            act_rsqrt_seed(nc, act, link, net, NT, var_ready, 1, seed_ready)
            empty_projections(nc, act, nc.scalar.copy, net, outs[:n_ctx], 8, 0, tile_ready, emptied)
            act.wait_ge(zT_turned, 1)
            nc.scalar.copy(net.zT[:], net.ps[:, 0, 0:S]).then_inc(zT_ready, 1)
            for j in range(n_ctx, len(outs)):
                if j % 2 == 0:
                    act.wait_ge(tile_ready, j + 1)
                    nc.scalar.copy(outs[j], net.ps[:, j % 8, :]).then_inc(emptied[0], 1)
            attn.act(nc, act)
            copy_out_chunks(nc, act, nc.scalar.copy, net, 8, 0, o_turned, copied)

        @block.tensor
        def _(pe):
            pe.wait_ge(loaded, 96)
            pe.wait_ge(net.w0_loaded, net.w0_count)
            pe_projections(nc, pe, net, tiles[:n_ctx], 8, tile_ready, emptied)
            pe.wait_ge(rows_ready, 1)
            pe.wait_ge(emptied[0], 1)
            for t in range(NT):
                last = nc.tensor.transpose(net.ps[:, 0, t * P:(t + 1) * P], net.z[:, t, :], net.ident[:])
            last.then_inc(zT_turned, 1)
            pe.wait_ge(zT_ready, 1)
            for j in range(n_ctx, len(tiles)):
                pe.wait_ge(emptied[j % 2], (j - 8) // 2 + 1)
                for a, c, stationary, moving in tiles[j]:
                    last = nc.tensor.matmul(net.ps[:, j % 8, a:c], stationary, moving, start=True, stop=True)
                last.then_inc(tile_ready, 1)
            for which in range(2):
                pe.wait_ge(emptied[which], counts[which])
            attn.pe(nc, pe)
            pe_out_projection(nc, pe, net, 8, w["o"], [(attn.group_done, 4)], o_turned, copied, o_ready)
    net.end_phase()



def local_block(net, l):
    nc = net.nc
    (dve_link, act_link, pool_link, zT_turned, zT_ready, qkv_ready, rows_copied, squares_ready, v_copied, cos_used,
     sin_ready, rotated, qk_turned, qk_act, qk_dve, var_ready, seed_ready, o_turned, act_copied, dve_copied, o_ready,
     z_ready, shifted, rows_ready, hT_turned, hT_ready, gate_in, gated, hidden_ready, mlp_ready, link_z, *att) = net.signals(38)
    copied = (act_copied, dve_copied)
    w = net.wf[l]
    units = [(h, (0, 1), (4, 5), DH * h) for h in range(H8)]
    groups = [(H8 - 1, 4 + t, net.sums[:, t, 0:H8], net.heads[:, t, 0:BANK].rearrange("p (h d) -> p h d", d=DH))
              for t in range(NT)]
    attn = Attention(net, units, S, DH,
                     lambda h, qt: net.qT[head_rows(h), h // 2, qt * P:(qt + 1) * P],
                     lambda h: net.kT[head_rows(h), h // 2, 0:S],
                     lambda h, k: net.v[:, k, h * DH:(h + 1) * DH],
                     net.ident_b[:], net.band[:], 1.0, lambda h, qt: net.rnorm[:, qt, h:h + 1],
                     lambda h, qt: net.sums[:, qt, h:h + 1], groups, att)
    attn.scale_all = lambda h: net.rnorm[:, :, h]
    half = slice(D // 2, D)

    def rot(x, a, b):
        return x[:, :, :, a:b]

    with nc.Block() as block:
        @block.tensor
        def _(pe):
            for t in range(NT):
                last = nc.tensor.transpose(net.ps[:, 7, t * P:(t + 1) * P], net.z[:, t, :], net.ident[:])
            last.then_inc(zT_turned, 1)
            pe.wait_ge(zT_ready, 3)
            if l == 0:
                pe.wait_ge(net.wf_loaded, net.wf_count)
            for t in range(NT):
                if t >= 1:
                    pe.wait_ge(squares_ready, t)
                    pe.wait_ge(rows_copied, t)
                    pe.wait_ge(v_copied, t)
                for part in range(3):
                    last = nc.tensor.matmul(net.ps[:, part, :], net.hT[:, t * P:(t + 1) * P],
                                            w["qkv"][:, part * BANK:(part + 1) * BANK], start=True, stop=True)
                last.then_inc(qkv_ready, 1)
            for t in range(NT):
                pe.wait_ge(rotated, t + 1)
                for part in range(2):
                    for m in range(4):
                        last = nc.tensor.transpose(net.ps[:, 3 + 2 * t + part, m * P:(m + 1) * P],
                                                   net.qk_rot[:, t, part * BANK + m * P:part * BANK + (m + 1) * P],
                                                   net.ident[:])
                    last.then_inc(qk_turned, 1)
            pe.wait_ge(qk_act, 2)
            pe.wait_ge(qk_dve, 2)
            pe.wait_ge(v_copied, NT)
            attn.pe(nc, pe)
            pe_out_projection(nc, pe, net, 4, w["o"], [(attn.group_done, 2)], o_turned, copied, o_ready)
            pe.wait_ge(rows_ready, 1)
            for t in range(NT):
                last = nc.tensor.transpose(net.ps[:, 0, t * P:(t + 1) * P], net.hn[:, t, :], net.ident[:])
            last.then_inc(hT_turned, 1)
            pe.wait_ge(hT_ready, 1)
            for c, (c0, cn) in enumerate(HC):
                for part in range(2):
                    last = nc.tensor.matmul(net.ps[0:cn, 1 + c, part * S:(part + 1) * S],
                                            w["w1"][:, part * HID + c0:part * HID + c0 + cn], net.hnT[:],
                                            start=True, stop=True)
                last.then_inc(gate_in, 1)
            for t in range(NT):
                for c, (c0, cn) in enumerate(HC):
                    if t == 0:
                        pe.wait_ge(hidden_ready, c + 1)
                    last = nc.tensor.matmul(net.ps[:, 5, t * P:(t + 1) * P], net.hid[0:cn, c, t * P:(t + 1) * P],
                                            w["w2"][0:cn, c, :], start=c == 0, stop=c == len(HC) - 1)
            last.then_inc(mlp_ready, 1)

        @block.scalar
        def _(act):
            link = linker(act, act_link)
            act.wait_ge(zT_turned, 1)
            nc.scalar.copy(net.hT[0:D // 2, :], net.ps[0:D // 2, 7, 0:S]).then_inc(zT_ready, 1)
            for t in range(NT):
                act.wait_ge(qkv_ready, t + 1)
                nc.scalar.copy(net.qk[:, t, :], net.ps[:, 0:2, :]).then_inc(rows_copied, 1)
                if t >= 1:
                    act.wait_ge(cos_used, t)
                nc.scalar.activation(net.squares[:], net.ps[:, 0:2, :].rearrange("p b n -> p (b n)"), ACT.Square).then_inc(squares_ready, 1)
                nc.scalar.copy(net.v[:, t, 0:BANK], net.ps[:, 2, :]).then_inc(v_copied, 1)
            act_rsqrt_seed(nc, act, link, net, NT * 16, var_ready, 1, seed_ready)
            for t in range(NT):
                act.wait_ge(qk_turned, 2 * t + 1)
                nc.scalar.copy(net.qT[:, 0:4, t * P:(t + 1) * P],
                               net.ps[:, 3 + 2 * t, :].rearrange("p (m s) -> p m s", m=4)).then_inc(qk_act, 1)
            attn.act(nc, act)
            copy_out_chunks(nc, act, nc.scalar.copy, net, 4, 0, o_turned, copied)
            act_rsqrt_seed(nc, act, link, net, NT, var_ready, 2, seed_ready)
            act.wait_ge(hT_turned, 1)
            nc.scalar.activation(net.hnT[:], net.ps[:, 0, 0:S], ACT.Identity, scale=net.col("L0_ln_g", l),
                                 bias=net.col("L0_ln_b", l)).then_inc(hT_ready, 1)
            for c, (c0, cn) in enumerate(HC):
                act.wait_ge(gate_in, c + 1)
                nc.scalar.activation(net.gate[0:cn, c, :], net.ps[0:cn, 1 + c, S:2 * S], ACT.Gelu,
                                     bias=net.col("L0_b1", 6 * l + 3 + c)[0:cn]).then_inc(gated, 1)

        @block.gpsimd
        def _(pool):
            for t in range(NT):
                pool.wait_ge(rows_copied, t + 1)
                x = net.qk[:, t, :].rearrange("p (a h d) -> p a h d", a=2, d=DH)
                y = net.qk_sin[:, t, :].rearrange("p (a h d) -> p a h d", a=2, d=DH)
                sin = net.sin_t[:, l, t, :, :]
                for a, b in ((0, 32), (32, 0)):
                    last = nc.gpsimd.tensor_tensor(rot(y, a, a + 32), rot(x, b, b + 32),
                                                   sin[:, :, a:a + 32].unsqueeze(2).to_broadcast([P, 2, H8, 32]), ALU.mult)
                last.then_inc(sin_ready, 1)

        @block.sync
        def _(sp):
            sp.wait_ge(z_ready, 1)
            sp.dma_start(net.hs[1:P, :, half], net.z[0:P - 1, :, half]).then_inc(shifted, 16)
            sp.dma_start(net.hs[0:1, 1, half], net.z[P - 1:P, 0, half]).then_inc(shifted, 16)
            sp.wait_ge(shifted, 32)

        @block.vector
        def _(dve):
            link = linker(dve, dve_link)
            dve.wait_ge(zT_turned, 1)
            turned = net.ps[half, 7, 0:S - 1]
            nc.vector.tensor_copy(net.hT[half, 1:S], turned).then_inc(zT_ready, 1)
            nc.vector.memset(net.hT[half, 0:1], 0.0).then_inc(zT_ready, 1)
            for t in range(NT):
                dve.wait_ge(rows_copied, t + 1)
                x = net.qk[:, t, :].rearrange("p (a h d) -> p a h d", a=2, d=DH)
                y = net.qk_rot[:, t, :].rearrange("p (a h d) -> p a h d", a=2, d=DH)
                link(nc.vector.tensor_tensor(y, x, net.cos_t[:, l, t, :, :].unsqueeze(2).to_broadcast([P, 2, H8, DH]), ALU.mult))
                dve.wait_ge(squares_ready, t + 1)
                nc.vector.reduce_sum(net.ssq[:, t, :], net.squares[:].rearrange("p (h d) -> p h d", d=DH), AX.X).then_inc(cos_used, 1)
            dve.wait_ge(cos_used, NT)
            nc.vector.tensor_scalar(net.veps[:, 0:NT * 16], net.ssq[:].rearrange("p t h -> p (t h)"), 1e-24, 2.0 ** 30,
                                    ALU.max, ALU.mult).then_inc(var_ready, 1)
            dve_rsqrt(nc, dve, link, net, NT * 16, seed_ready, 1, net.rnorm[:].rearrange("p t h -> p (t h)"), 2.0 ** 15)
            for t in range(NT):
                dve.wait_ge(sin_ready, t + 1)
                link(nc.vector.tensor_tensor(net.qk_rot[:, t, :], net.qk_rot[:, t, :], net.qk_sin[:, t, :], ALU.add))
                k = net.qk_rot[:, t, BANK:2 * BANK].rearrange("p (h d) -> p h d", d=DH)
                nc.vector.tensor_tensor(k, k, net.rnorm[:, t, H8:16].unsqueeze(2).to_broadcast([P, H8, DH]),
                                        ALU.mult).then_inc(rotated, 1)
            link(nc.vector.tensor_scalar(net.rnorm[:, :, 0:H8], net.rnorm[:, :, 0:H8], 8.0, None, ALU.mult))
            for t in range(NT):
                dve.wait_ge(qk_turned, 2 * t + 2)
                nc.vector.tensor_copy(net.kT[:, 0:4, t * P:(t + 1) * P],
                                      net.ps[:, 4 + 2 * t, :].rearrange("p (m s) -> p m s", m=4)).then_inc(qk_dve, 1)
            attn.dve(nc, dve, link)
            copy_out_chunks(nc, dve, nc.vector.tensor_copy, net, 4, 1, o_turned, copied)
            dve.wait_ge(o_ready, 1)
            nc.vector.tensor_tensor(net.z[:], net.z[:], net.ps[:, 4, 0:S].rearrange("p (t d) -> p t d", d=D), ALU.add).then_inc(z_ready, 1)
            dve.wait_ge(z_ready, 1)
            link(nc.vector.tensor_copy(net.hs[:, :, 0:D // 2], net.z[:, :, 0:D // 2]))
            dve.wait_ge(shifted, 32)
            dve_stats(nc, link, net, lambda t: net.hs[:, t, :], NT, 1e-5, var_ready)
            dve_rsqrt(nc, dve, link, net, NT, seed_ready, 2, net.rstd[:, 0:NT])
            dve_normalise(nc, net, lambda t: net.hn[:, t, :], lambda t: net.hs[:, t, :], NT).then_inc(rows_ready, 1)
            link(nc.vector.tensor_tensor(net.z[:], net.z[:], net.row("L0_b2", l).unsqueeze(1).to_broadcast([P, NT, D]), ALU.add))
            for c, (c0, cn) in enumerate(HC):
                dve.wait_ge(gated, c + 1)
                nc.vector.scalar_tensor_tensor(net.hid[0:cn, c, :], net.ps[0:cn, 1 + c, 0:S],
                                               net.col("L0_b1", 6 * l + c)[0:cn], net.gate[0:cn, c, :],
                                               ALU.add, ALU.mult).then_inc(hidden_ready, 1)
            dve.wait_ge(mlp_ready, 1)
            link(nc.vector.tensor_tensor(net.z[:], net.z[:], net.ps[:, 5, 0:S].rearrange("p (t d) -> p t d", d=D), ALU.add))
            if l == 1:
                nc.vector.tensor_tensor(net.x[:], net.x[:], net.z[:], ALU.add)
    net.end_phase()


def norm_x(net):
    nc = net.nc
    dve_link, act_link, var_ready, seed_ready = net.signals(4)
    with nc.Block() as block:
        @block.vector
        def _(dve):
            link = linker(dve, dve_link)
            dve_stats(nc, link, net, lambda t: net.x[:, t, :], NT, 1e-5, var_ready)
            dve_rsqrt(nc, dve, link, net, NT, seed_ready, 1, net.rstd[:, 0:NT])
            dve_normalise(nc, net, lambda t: net.z[:, t, :], lambda t: net.x[:, t, :], NT)

        @block.scalar
        def _(act):
            act_rsqrt_seed(nc, act, linker(act, act_link), net, NT, var_ready, 1, seed_ready)
    net.end_phase()



def dve_norm_rows(nc, dve, link, net, src, out, n, eps, var_ready, seed_ready, k):
    dve_stats(nc, link, net, src, n, eps, var_ready)
    dve_rsqrt(nc, dve, link, net, n, seed_ready, k, net.rstd[:, 0:n])
    return dve_normalise(nc, net, out, src, n)


def spread(ap, n):
    return ap.unsqueeze(2).to_broadcast([P, ap.shape[1], n])


def dve_top2(nc, dve, link, net, logits, ne, probs, exp_in, exp_out, guard, comb):
    r = net.small
    mx, sm, top, idx, idxf = r["mx"][:, 0:NT], r["sm"][:, 0:NT], r["top"], r["idx"], r["idxf"]
    link(nc.vector.reduce_max(mx, logits, AX.X))
    nc.vector.tensor_tensor(r["e"][:, 0:NT, 0:ne], logits, spread(mx, ne), ALU.subtract).then_inc(exp_in, 1)
    dve.wait_ge(exp_out, 1)
    link(nc.vector.reduce_sum(sm, r["e"][:, 0:NT, 0:ne], AX.X))
    link(nc.vector.reciprocal(sm, sm))
    link(nc.vector.tensor_tensor(probs[:, 0:NT, 0:ne], r["e"][:, 0:NT, 0:ne], spread(sm, ne), ALU.mult))
    for t in range(NT):
        last = nc.vector.max(top[:, t, :], probs[:, t, :])
    link(last)
    for t in range(NT):
        last = nc.vector.max_index(idx[:, t, :], top[:, t, :], probs[:, t, :])
    link(last)
    link(nc.vector.tensor_copy(idxf[:, 0:NT, :], idx[:, 0:NT, :]))
    link(nc.vector.tensor_tensor(sm, top[:, 0:NT, 0], top[:, 0:NT, 1], ALU.add))
    link(nc.vector.tensor_scalar(sm, sm, guard[0], None, guard[1]))
    link(nc.vector.reciprocal(sm, sm))
    link(nc.vector.tensor_tensor(r["w2"], top[:, 0:NT, 0:2], spread(sm, 2), ALU.mult))
    iota = net.iota[:, 0:ne].unsqueeze(1).to_broadcast([P, NT, ne])
    for k in range(2):
        link(nc.vector.tensor_tensor(r["eq"][:, k, :, 0:ne], iota, spread(idxf[:, 0:NT, k], ne), ALU.is_equal))
        link(nc.vector.tensor_tensor(r["eq"][:, k, :, 0:ne], r["eq"][:, k, :, 0:ne], spread(r["w2"][:, :, k], ne), ALU.mult))
    link(nc.vector.tensor_tensor(comb, r["eq"][:, 0, :, 0:ne], r["eq"][:, 1, :, 0:ne], ALU.add))


def rows_of(ap):
    return lambda t: ap[:, t, :]



def layer1_attention(net):
    nc = net.nc
    (dve_link, act_link, var_ready, seed_ready, rows_ready, turned, cols_ready, mask_ready, tile_ready, act_emptied,
     dve_emptied, o_turned, act_copied, dve_copied, o_ready, *att) = net.signals(22)
    emptied, copied = (act_emptied, dve_emptied), (act_copied, dve_copied)
    w = net.w1
    tiles, outs = [], []
    for m in range(8):
        tiles.append([(0, BANK, w["kv"][:, m * P:(m + 1) * P], net.kv_in[:])])
        outs.append(net.kT[:, m, :])
    for t in range(4):
        for half in range(2):
            tiles.append([(0, BANK, net.kv_in[:, t * P:(t + 1) * P], w["kv"][:, 1024 + half * BANK:1024 + (half + 1) * BANK])])
            outs.append(net.v[:, t, half * BANK:(half + 1) * BANK])
    for m in range(0, 8, 2):
        tiles.append([(i * S, (i + 1) * S, w["q"][:, (m + i) * P:(m + i + 1) * P], net.kv_in[:, S:2 * S]) for i in range(2)])
        outs.append(net.qT[:, m:m + 2, :])
    counts = evac_counts(len(tiles))
    units = [(h, (t,), (4 + 2 * t + h // 8,), DH * (h % 8)) for t in range(NT) for h in range(H16)]
    groups = [(16 * t + 8 * g + 7, 4 + 2 * t + g, net.sums[:, t, 8 * g:8 * g + 8],
               net.heads[:, t, g * BANK:(g + 1) * BANK].rearrange("p (h d) -> p h d", d=DH))
              for t in range(NT) for g in range(2)]
    attn = Attention(net, units, 2 * S, DH,
                     lambda h, qt: net.qT[head_rows(h), h // 2, qt * P:(qt + 1) * P],
                     lambda h: net.kT[head_rows(h), h // 2, :],
                     lambda h, k: net.v[:, k, h * DH:(h + 1) * DH],
                     net.ones_b[0:1, :], net.kmask[:], DH ** -0.5, None, lambda h, qt: net.sums[:, qt, h:h + 1], groups, att)

    with nc.Block() as block:
        @block.tensor
        def _(pe):
            for k, (src, bank) in enumerate(((net.cn, 7), (net.hn, 6))):
                pe.wait_ge(rows_ready, k + 1)
                for t in range(NT):
                    last = nc.tensor.transpose(net.ps[:, bank, t * P:(t + 1) * P], src[:, t, :], net.ident[:])
                last.then_inc(turned, 1)
            pe.wait_ge(cols_ready, 2)
            pe.wait_ge(net.w1_loaded, net.w1_count)
            pe_projections(nc, pe, net, tiles, 6, tile_ready, emptied)
            for which in range(2):
                pe.wait_ge(emptied[which], counts[which])
            pe.wait_ge(mask_ready, 1)
            attn.pe(nc, pe)
            pe_out_projection(nc, pe, net, 8, w["o"], [(attn.group_done, 4)], o_turned, copied, o_ready)

        @block.scalar
        def _(act):
            link = linker(act, act_link)
            act_rsqrt_seed(nc, act, link, net, 2 * NT, var_ready, 1, seed_ready)
            act_rsqrt_seed(nc, act, link, net, NT, var_ready, 2, seed_ready)
            for k, (name, bank) in enumerate((("x", 7), ("l", 6))):
                act.wait_ge(turned, k + 1)
                nc.scalar.activation(net.kv_in[:, k * S:(k + 1) * S], net.ps[:, bank, 0:S], ACT.Identity,
                                     scale=net.col("L1_g_" + name, 0), bias=net.col("L1_b_" + name, 0)).then_inc(cols_ready, 1)
            empty_projections(nc, act, nc.scalar.copy, net, outs, 6, 0, tile_ready, emptied)
            attn.act(nc, act)
            copy_out_chunks(nc, act, nc.scalar.copy, net, 8, 0, o_turned, copied)
            act_rsqrt_seed(nc, act, link, net, NT, var_ready, 3, seed_ready)

        @block.vector
        def _(dve):
            link = linker(dve, dve_link)
            both = lambda a, b: lambda t: a[:, t, :] if t < NT else b[:, t - NT, :]
            dve_norm_rows(nc, dve, link, net, both(net.ctx, net.x), both(net.cn, net.z), 2 * NT, 1e-5,
                          var_ready, seed_ready, 1).then_inc(rows_ready, 1)
            dve.wait_ge(rows_ready, 1)
            dve_norm_rows(nc, dve, link, net, rows_of(net.z), rows_of(net.hn), NT, 1e-5,
                          var_ready, seed_ready, 2).then_inc(rows_ready, 1)
            nc.vector.tensor_scalar(net.kmask[0:1, 0:S], net.kmask_u[:].bitcast(U8), -MASKED, MASKED, ALU.mult, ALU.add).then_inc(mask_ready, 1)
            empty_projections(nc, dve, nc.vector.tensor_copy, net, outs, 6, 1, tile_ready, emptied)
            attn.dve(nc, dve, link)
            copy_out_chunks(nc, dve, nc.vector.tensor_copy, net, 8, 1, o_turned, copied)
            dve.wait_ge(o_ready, 1)
            out = net.ps[:, 4, 0:S].rearrange("p (t d) -> p t d", d=D)
            link(dve_norm_rows(nc, dve, link, net, rows_of(out), rows_of(net.hn), NT, 1e-5, var_ready, seed_ready, 3))
            both_rows = lambda name: net.row(name, 0).unsqueeze(1).to_broadcast([P, NT, D])
            link(nc.vector.tensor_tensor(net.hn[:], net.hn[:], both_rows("L1_g_o"), ALU.mult))
            link(nc.vector.tensor_tensor(net.hn[:], net.hn[:], both_rows("L1_b_o"), ALU.add))
            nc.vector.tensor_tensor(net.x[:], net.x[:], net.hn[:], ALU.add)
    net.end_phase()



def layer1_experts(net):
    nc = net.nc
    (dve_link, act_link, var_ready, seed_ready, rows_ready, turned, zT_ready, logits_ready, exp_in, exp_out,
     fc_ready, relu_ready, hid_ready, proj_ready, added) = net.signals(15)
    n = NE1 + 1
    relu = net.qT[:].rearrange("p m s -> p (m s)").rearrange("p (a n) -> p a n", a=2)
    hid = net.kT[:].rearrange("p m s -> p (m s)")[:, 0:2048].rearrange("p (a m s) -> p a m s", a=2, m=4)
    comb = net.comb[:, :, 0:NE1]

    with nc.Block() as block:
        @block.tensor
        def _(pe):
            pe.wait_ge(rows_ready, 1)
            for t in range(NT):
                last = nc.tensor.transpose(net.ps[:, 7, t * P:(t + 1) * P], net.z[:, t, :], net.ident[:])
            last.then_inc(turned, 1)
            pe.wait_ge(zT_ready, 1)
            pe.wait_ge(net.w1f_loaded, net.w1f_count)
            for t in range(NT):
                last = nc.tensor.matmul(net.ps[:, 6, t * NE1:(t + 1) * NE1], net.zT[:, t * P:(t + 1) * P], net.router1[:],
                                        start=True, stop=True)
            last.then_inc(logits_ready, 1)
            for e in range(n + 1):
                if e < n:
                    if e >= 2:
                        pe.wait_ge(hid_ready, e - 1)
                    for c in range(4):
                        last = nc.tensor.matmul(net.ps[:, 2 * (e % 2) + c // 2, (c % 2) * S:(c % 2 + 1) * S],
                                                net.fc[:, e, c * P:(c + 1) * P], net.zT[:], start=True, stop=True)
                    last.then_inc(fc_ready, 1)
                if e >= 1:
                    v = e - 1
                    pe.wait_ge(hid_ready, v + 1)
                    if v >= 2:
                        pe.wait_ge(added, v - 1)
                    for t in range(NT):
                        for c in range(4):
                            last = nc.tensor.matmul(net.ps[:, 4 + v % 2, t * P:(t + 1) * P], hid[:, v % 2, c, t * P:(t + 1) * P],
                                                    net.proj[:, v, c, :], start=c == 0, stop=c == 3)
                    last.then_inc(proj_ready, 1)

        @block.scalar
        def _(act):
            link = linker(act, act_link)
            act_rsqrt_seed(nc, act, link, net, NT, var_ready, 1, seed_ready)
            act.wait_ge(turned, 1)
            nc.scalar.copy(net.zT[:], net.ps[:, 7, 0:S]).then_inc(zT_ready, 1)
            act.wait_ge(exp_in, 1)
            e2 = net.small["e"][:, 0:NT, 0:NE1]
            nc.scalar.activation(e2, e2, ACT.Exp).then_inc(exp_out, 1)
            for e in range(n):
                act.wait_ge(fc_ready, e + 1)
                if e >= 2:
                    act.wait_ge(hid_ready, e - 1)
                nc.scalar.activation(relu[:, e % 2, :], net.ps[:, 2 * (e % 2):2 * (e % 2) + 2, :].rearrange("p b n -> p (b n)"),
                                     ACT.Relu).then_inc(relu_ready, 1)

        @block.vector
        def _(dve):
            link = linker(dve, dve_link)
            dve_norm_rows(nc, dve, link, net, rows_of(net.x), rows_of(net.z), NT, 1e-5, var_ready, seed_ready, 1).then_inc(rows_ready, 1)
            dve.wait_ge(logits_ready, 1)
            dve_top2(nc, dve, link, net, net.ps[:, 6, 0:NT * NE1].rearrange("p (t e) -> p t e", t=NT), NE1, net.small["p8"],
                     exp_in, exp_out, (1e-9, ALU.max), comb)
            for e in range(n + 1):
                if e < n:
                    dve.wait_ge(relu_ready, e + 1)
                    if e >= 2:
                        dve.wait_ge(proj_ready, e - 1)
                    nc.vector.scalar_tensor_tensor(hid[:, e % 2, :, :].rearrange("p m s -> p (m s)"),
                                                   net.ps[:, 2 * (e % 2):2 * (e % 2) + 2, :].rearrange("p b n -> p (b n)"), 0.0,
                                                   relu[:, e % 2, :], ALU.max, ALU.mult).then_inc(hid_ready, 1)
                if e >= 1:
                    v = e - 1
                    dve.wait_ge(proj_ready, v + 1)
                    out = net.ps[:, 4 + v % 2, 0:S].rearrange("p (t d) -> p t d", d=D)
                    if v < NE1:
                        for t in range(NT):
                            last = nc.vector.scalar_tensor_tensor(net.x[:, t, :], out[:, t, :], comb[:, t, v:v + 1],
                                                                  net.x[:, t, :], ALU.mult, ALU.add)
                    else:
                        last = nc.vector.tensor_tensor(net.x[:], out, net.x[:], ALU.add)
                    last.then_inc(added, 1)
                    dve.wait_ge(added, v + 1)
    net.end_phase()



def layer2_attention(net):
    nc = net.nc
    (dve_link, act_link, var_ready, seed_ready, rows_ready, turned, zT_ready, proj_ready, proj_copied, ids_ready, ids_bc,
     scores_ready, exp_in, exp_out, mixed, mix_turned, mix_copied, mean_ready, mean_copied, out_ready, o) = net.signals(21)
    w = net.w2x
    qk = net.heads[:, 0, :].rearrange("p (a n) -> p a n", a=2)
    v = net.heads[:, 1, 0:BANK].rearrange("p (t n) -> p t n", t=NT)
    hot = net.qT[:].rearrange("p m s -> p (m s)")[:, 0:3 * NT * S].rearrange("p (w t l) -> p w t l", w=3, t=NT)
    junk = net.kT[:].rearrange("p m s -> p (m s)").rearrange("p (a l) -> p a l", l=S)
    mix = net.v[:, 0, :].rearrange("p (a t l) -> p a t l", a=2, t=NT)
    mixT = net.v[:, 1, :].rearrange("p (a l q) -> p a l q", a=2, l=NT)
    meanT = net.v[:, 2, 0:S]
    s6, r = net.s6, net.small
    tiles = [[(a * S, (a + 1) * S, w["q"][:, a, :], net.zT[:]) for a in range(2)],
             [(a * S, (a + 1) * S, w["k"][:, a, :], net.ctxT[:]) for a in range(2)],
             [(t * S, (t + 1) * S, net.ctxT[:, t * P:(t + 1) * P], w["v"][:]) for t in range(NT)]]

    with nc.Block() as block:
        @block.tensor
        def _(pe):
            pe.wait_ge(ids_ready, 1)
            nc.tensor.matmul(net.ps[:, 5, 0:S], net.ones[0:1, :], net.ids_f[:], start=True, stop=True).then_inc(ids_bc, 1)
            pe.wait_ge(net.w2_loaded, net.w2_count)
            for j in (1, 2, 0):
                if j == 0:
                    pe.wait_ge(rows_ready, 1)
                    for t in range(NT):
                        last = nc.tensor.transpose(net.ps[:, 7, t * P:(t + 1) * P], net.z[:, t, :], net.ident[:])
                    last.then_inc(turned, 1)
                    pe.wait_ge(zT_ready, 1)
                for a, b, stationary, moving in tiles[j]:
                    last = nc.tensor.matmul(net.ps[:, j, a:b], stationary, moving, start=True, stop=True)
                last.then_inc(proj_ready, 1)
            pe.wait_ge(proj_copied, 3)
            for a in range(2):
                for t in range(NT):
                    last = nc.tensor.matmul(net.ps[:, 3 + a, t * S:(t + 1) * S], qk[:, 0, a * S + t * P:a * S + (t + 1) * P],
                                            qk[:, 1, a * S:(a + 1) * S], start=True, stop=True)
                last.then_inc(scores_ready, 1)
            for a in range(2):
                pe.wait_ge(mixed, a + 1)
                for l in range(NT):
                    for t in range(NT):
                        last = nc.tensor.transpose(net.ps[:, 6 + a, (l * NT + t) * P:(l * NT + t + 1) * P],
                                                   mix[:, a, t, l * P:(l + 1) * P], net.ident[:])
                last.then_inc(mix_turned, 1)
            pe.wait_ge(mix_copied, 2)
            for a in range(2):
                for l in range(NT):
                    last = nc.tensor.matmul(net.ps[:, 0, 0:S], v[:, l, a * P:(a + 1) * P], mixT[:, a, l, :],
                                            start=a == 0 and l == 0, stop=a == 1 and l == NT - 1)
            last.then_inc(mean_ready, 1)
            pe.wait_ge(mean_copied, 1)
            for t in range(NT):
                last = nc.tensor.matmul(net.ps[:, 1, t * P:(t + 1) * P], meanT[:, t * P:(t + 1) * P], w["o"][:], start=True, stop=True)
            last.then_inc(out_ready, 1)

        @block.scalar
        def _(act):
            link = linker(act, act_link)
            act_rsqrt_seed(nc, act, link, net, NT, var_ready, 1, seed_ready)
            act.wait_ge(proj_ready, 1)
            nc.scalar.copy(qk[:, 1, :], net.ps[:, 1, :]).then_inc(proj_copied, 1)
            act.wait_ge(proj_ready, 2)
            nc.scalar.copy(v.rearrange("p t n -> p (t n)"), net.ps[:, 2, :]).then_inc(proj_copied, 1)
            act.wait_ge(turned, 1)
            nc.scalar.copy(net.zT[:], net.ps[:, 7, 0:S]).then_inc(zT_ready, 1)
            act.wait_ge(proj_ready, 3)
            nc.scalar.copy(qk[:, 0, :], net.ps[:, 0, :]).then_inc(proj_copied, 1)
            act.wait_ge(exp_in, 1)
            nc.scalar.activation(s6[:], s6[:], ACT.Exp).then_inc(exp_out, 1)
            for a in range(2):
                act.wait_ge(mix_turned, a + 1)
                nc.scalar.copy(mixT[:, a, :, :].rearrange("p l q -> p (l q)"), net.ps[:, 6 + a, :]).then_inc(mix_copied, 1)
            act.wait_ge(mean_ready, 1)
            nc.scalar.copy(meanT, net.ps[:, 0, 0:S]).then_inc(mean_copied, 1)

        @block.vector
        def _(dve):
            link = linker(dve, dve_link)
            nc.vector.tensor_copy(net.ids_f[:], net.ids_i[:]).then_inc(ids_ready, 1)
            dve_norm_rows(nc, dve, link, net, rows_of(net.x), rows_of(net.z), NT, 1e-5, var_ready, seed_ready, 1).then_inc(rows_ready, 1)
            link(nc.vector.tensor_copy(r["ptr"][:, 3, :], net.ptr_i[:]))
            for k in range(3):
                last = nc.vector.tensor_scalar(r["ptr"][:, k, :], r["ptr"][:, 3, :], float(k), 0.0, ALU.add, ALU.max)
            link(last)
            link(nc.vector.tensor_scalar(r["ptr"][:, 0:3, :], r["ptr"][:, 0:3, :], float(S - 1), None, ALU.min))
            for k in range(3):
                for t in range(NT):
                    last = nc.vector.tensor_scalar(hot[:, k, t, :], net.iota[:, 0:S], r["ptr"][:, k, t:t + 1], None, ALU.is_equal)
            link(last)
            dve.wait_ge(ids_bc, 1)
            for t in range(NT):
                last = nc.vector.scalar_tensor_tensor(junk[:, t, :], net.ps[:, 5, 0:S], 1.0, hot[:, 0, t, :], ALU.mult, ALU.mult,
                                                      accum_out=r["rel"][:, t:t + 1])
            for a in range(2):
                dve.wait_ge(scores_ready, a + 1)
                for t in range(NT):
                    for k in range(3):
                        last = nc.vector.scalar_tensor_tensor(junk[:, 2 + 6 * a + 3 * t + k, :], net.ps[:, 3 + a, t * S:(t + 1) * S],
                                                              D ** -0.5, hot[:, k, t, :], ALU.mult, ALU.mult,
                                                              accum_out=s6[:, a, t, k:k + 1])
            link(last)
            v1, v2, val, eq = s6[:, 0, :, 1], s6[:, 0, :, 2], r["val"], r["is"]
            nc.vector.tensor_tensor(val[:, 0, :], v1, v2, ALU.add)
            nc.vector.tensor_tensor(val[:, 1, :], v1, v2, ALU.max)
            nc.vector.tensor_tensor(val[:, 4, :], v1, v2, ALU.subtract)
            for k in range(5):
                nc.vector.tensor_scalar(eq[:, k, :], r["rel"][:], float(k), None, ALU.is_equal)
            link(nc.vector.tensor_scalar(val[:, 2, :], v1, -1.0, None, ALU.mult))
            nc.vector.tensor_tensor(val[:, 3, :], val[:, 2, :], v2, ALU.max)
            link(nc.vector.tensor_scalar(val[:, 5, :], val[:, 4, :], -1.0, None, ALU.mult))
            link(nc.vector.tensor_tensor(val[:, 4, :], val[:, 4, :], val[:, 5, :], ALU.max))
            link(nc.vector.tensor_tensor(val[:, 0:5, :], val[:, 0:5, :], eq[:], ALU.mult))
            nc.vector.reduce_sum(r["new"][:], val[:, 0:5, :].rearrange("p k t -> p t k"), AX.X)
            link(nc.vector.reduce_sum(r["any"][:], eq[:].rearrange("p k t -> p t k"), AX.X))
            link(nc.vector.tensor_scalar(r["any"][:], r["any"][:], -1.0, 1.0, ALU.mult, ALU.add))
            link(nc.vector.tensor_tensor(r["any"][:], r["any"][:], s6[:, 0, :, 0], ALU.mult))
            link(nc.vector.tensor_tensor(s6[:, 0, :, 0], r["any"][:], r["new"][:], ALU.add))
            flat = s6[:].rearrange("p a t w -> p (a t) w")
            link(nc.vector.reduce_max(r["mx"][:, 0:4], flat, AX.X))
            nc.vector.tensor_tensor(flat, flat, spread(r["mx"][:, 0:4], 3), ALU.subtract).then_inc(exp_in, 1)
            dve.wait_ge(exp_out, 1)
            link(nc.vector.reduce_sum(r["sm"][:, 0:4], flat, AX.X))
            link(nc.vector.reciprocal(r["sm"][:, 0:4], r["sm"][:, 0:4]))
            link(nc.vector.tensor_tensor(r["sm"][:, 0:4].rearrange("p (a t) -> p a t", a=2),
                                         r["sm"][:, 0:4].rearrange("p (a t) -> p a t", a=2), spread(net.share[:], NT), ALU.mult))
            link(nc.vector.tensor_tensor(flat, flat, spread(r["sm"][:, 0:4], 3), ALU.mult))
            for a in range(2):
                for t in range(NT):
                    last = nc.vector.tensor_scalar(mix[:, a, t, :], hot[:, 0, t, :], s6[:, a, t, 0:1], None, ALU.mult)
                link(last)
                for k in (1, 2):
                    for t in range(NT):
                        last = nc.vector.scalar_tensor_tensor(mix[:, a, t, :], hot[:, k, t, :], s6[:, a, t, k:k + 1],
                                                              mix[:, a, t, :], ALU.mult, ALU.add)
                    link(last)
                dve.sem_inc(mixed, 1)
            dve.wait_ge(out_ready, 1)
            nc.vector.scalar_tensor_tensor(net.x[:], net.ps[:, 1, 0:S].rearrange("p (t d) -> p t d", d=D), net.row("gain", 0, 1),
                                           net.x[:], ALU.mult, ALU.add)
    net.end_phase()



def layer2_experts(net):
    nc = net.nc
    (dve_link, act_link, var_ready, seed_ready, rows_ready, turned, cols_ready, logits_ready, exp_in, exp_out,
     hid_in, hid_normed, hid_turned, hid_ready, out_ready) = net.signals(15)
    hidn = net.heads
    hidT = net.qT
    comb = net.comb[:, :, 0:NE2]
    sums = net.hs2

    def hidden(i):
        t, e = divmod(i, NE2)
        return net.ps[:, 2 * t + e // 2, (e % 2) * H2:(e % 2 + 1) * H2]

    with nc.Block() as block:
        @block.tensor
        def _(pe):
            for k, src in enumerate((net.z, net.hn)):
                pe.wait_ge(rows_ready, k + 1)
                for t in range(NT):
                    last = nc.tensor.transpose(net.ps[:, 6 + k, t * P:(t + 1) * P], src[:, t, :], net.ident[:])
                last.then_inc(turned, 1)
                pe.wait_ge(cols_ready, k + 1)
                if k == 0:
                    for t in range(NT):
                        for half in range(2):
                            last = nc.tensor.matmul(net.ps[:, 2 * t + half, :], net.zT[:, t * P:(t + 1) * P],
                                                    net.w2f["in"][:, half * BANK:(half + 1) * BANK], start=True, stop=True)
                    last.then_inc(hid_in, 1)
            for t in range(NT):
                last = nc.tensor.matmul(net.ps[:, 5, t * NE2:(t + 1) * NE2], net.hnT[:, t * P:(t + 1) * P], net.router2[:],
                                        start=True, stop=True)
            last.then_inc(logits_ready, 1)
            pe.wait_ge(hid_normed, 1)
            pe.wait_ge(exp_in, 1)
            for j in range(4):
                for c in range(2):
                    for t in range(NT):
                        last = nc.tensor.transpose(net.ps[:, 4 + j, (c * NT + t) * P:(c * NT + t + 1) * P],
                                                   hidn[:, t, (2 * j + c) * P:(2 * j + c + 1) * P], net.ident[:])
                last.then_inc(hid_turned, 1)
            for e in range(NE2):
                pe.wait_ge(hid_ready, 2 * (e + 1))
                for t in range(NT):
                    for c in range(2):
                        last = nc.tensor.matmul(net.ps[:, e, t * P:(t + 1) * P], hidT[:, 2 * e + c, t * P:(t + 1) * P],
                                                net.w2f["out"][:, 2 * e + c, :], start=c == 0, stop=c == 1)
                last.then_inc(out_ready, 1)

        @block.scalar
        def _(act):
            link = linker(act, act_link)
            act_rsqrt_seed(nc, act, link, net, NT, var_ready, 1, seed_ready)
            act.wait_ge(turned, 1)
            nc.scalar.copy(net.zT[:], net.ps[:, 6, 0:S]).then_inc(cols_ready, 1)
            act_rsqrt_seed(nc, act, link, net, NT, var_ready, 2, seed_ready)
            act.wait_ge(turned, 2)
            nc.scalar.activation(net.hnT[:], net.ps[:, 7, 0:S], ACT.Identity, scale=net.col("L2_rn_g", 0),
                                 bias=net.col("L2_rn_b", 0)).then_inc(cols_ready, 1)
            act_rsqrt_seed(nc, act, link, net, NT * NE2, var_ready, 3, seed_ready)
            act.wait_ge(exp_in, 1)
            e2 = net.small["e"][:, 0:NT, 0:NE2]
            nc.scalar.activation(e2, e2, ACT.Exp).then_inc(exp_out, 1)
            for j in range(4):
                act.wait_ge(hid_turned, j + 1)
                for c in range(2):
                    nc.scalar.activation(hidT[:, 2 * j + c, :], net.ps[:, 4 + j, c * S:(c + 1) * S], ACT.Relu,
                                         scale=net.col("L2_ln_g", 2 * j + c), bias=net.col("L2_ln_b", 2 * j + c)).then_inc(hid_ready, 1)
            act_rsqrt_seed(nc, act, link, net, NT, var_ready, 4, seed_ready)

        @block.vector
        def _(dve):
            link = linker(dve, dve_link)
            dve_norm_rows(nc, dve, link, net, rows_of(net.x), rows_of(net.z), NT, 1e-5, var_ready, seed_ready, 1).then_inc(rows_ready, 1)
            dve.wait_ge(rows_ready, 1)
            dve_norm_rows(nc, dve, link, net, rows_of(net.z), rows_of(net.hn), NT, 1e-5, var_ready, seed_ready, 2).then_inc(rows_ready, 1)
            dve.wait_ge(rows_ready, 2)
            dve.wait_ge(hid_in, 1)
            dve_stats(nc, link, net, hidden, NT * NE2, 1e-5, var_ready)
            dve_rsqrt(nc, dve, link, net, NT * NE2, seed_ready, 3, net.rstd[:, 0:NT * NE2])
            dve_normalise(nc, net, lambda i: hidn[:, i // NE2, (i % NE2) * H2:(i % NE2 + 1) * H2], hidden, NT * NE2).then_inc(hid_normed, 1)
            dve.wait_ge(logits_ready, 1)
            dve_top2(nc, dve, link, net, net.ps[:, 5, 0:NT * NE2].rearrange("p (t e) -> p t e", t=NT), NE2, net.small["p4"],
                     exp_in, exp_out, (1e-8, ALU.add), comb)
            for e in range(NE2):
                dve.wait_ge(out_ready, e + 1)
                for t in range(NT):
                    src = net.ps[:, e, t * P:(t + 1) * P]
                    if e == 0:
                        last = nc.vector.tensor_scalar(sums[:, t, :], src, comb[:, t, e:e + 1], None, ALU.mult)
                    else:
                        last = nc.vector.scalar_tensor_tensor(sums[:, t, :], src, comb[:, t, e:e + 1], sums[:, t, :], ALU.mult, ALU.add)
                link(last)
            link(dve_norm_rows(nc, dve, link, net, rows_of(sums), rows_of(net.hn), NT, 1e-5, var_ready, seed_ready, 4))
            both_rows = lambda name: net.row(name, 0).unsqueeze(1).to_broadcast([P, NT, D])
            link(nc.vector.tensor_tensor(net.hn[:], net.hn[:], both_rows("L2_on_g"), ALU.mult))
            link(nc.vector.tensor_tensor(net.hn[:], net.hn[:], both_rows("L2_on_b"), ALU.add))
            nc.vector.tensor_tensor(net.x[:], net.x[:], net.hn[:], ALU.add)
    net.end_phase()



def layer3_attention(net):
    nc = net.nc
    (dve_link, act_link, var_ready, seed_ready, rows_ready, turned, zT_ready, *att) = net.signals(14)
    groups = [(0, 4 + t, net.sums[:, t, 0:1], net.heads[:, t, 0:D].unsqueeze(1)) for t in range(NT)]
    attn = Attention(net, [(0, (0, 1), (4, 5), 0)], S, D,
                     lambda h, qt: net.zT[:, qt * P:(qt + 1) * P], lambda h: net.ctxT[:], lambda h, k: net.ctx[:, k, :],
                     net.ident_b[:], net.causal[:], D ** -0.5, None, lambda h, qt: net.sums[:, qt, 0:1], groups, att)

    with nc.Block() as block:
        @block.tensor
        def _(pe):
            pe.wait_ge(rows_ready, 1)
            for t in range(NT):
                last = nc.tensor.transpose(net.ps[:, 7, t * P:(t + 1) * P], net.z[:, t, :], net.ident[:])
            last.then_inc(turned, 1)
            pe.wait_ge(zT_ready, 1)
            attn.pe(nc, pe)

        @block.scalar
        def _(act):
            act_rsqrt_seed(nc, act, linker(act, act_link), net, NT, var_ready, 1, seed_ready)
            act.wait_ge(turned, 1)
            nc.scalar.copy(net.zT[:], net.ps[:, 7, 0:S]).then_inc(zT_ready, 1)
            attn.act(nc, act)

        @block.vector
        def _(dve):
            link = linker(dve, dve_link)
            dve_norm_rows(nc, dve, link, net, rows_of(net.x), rows_of(net.z), NT, 1e-5, var_ready, seed_ready, 1).then_inc(rows_ready, 1)
            attn.dve(nc, dve, link)
            dve.wait_ge(attn.group_done, NT)
            nc.vector.tensor_tensor(net.x[:], net.x[:], net.heads[:, :, 0:D], ALU.add).then_inc(rows_ready, 1)
            dve.wait_ge(rows_ready, 2)
            nc.vector.tensor_copy(net.x_all[:, bass.ds(net.batch * NT, NT), :], net.x[:])
    net.end_phase()



def layer3_experts(net, out):
    nc = net.nc
    (dve_link, act_link, pool_link, var_ready, seed_ready, rows_ready, turned, cols_ready, logits_ready, exp_in, exp_out,
     mask_ready, places_ready, slots_ready, diag_ready, spread_ready, spread_copied, hot_ready, take_ready, res_in, res_gelu,
     sent, sent_copied, inter_ready, inter_gelu, expert_ready, expert_copied, mixed, final, written,
     w_res, w_gate, w_experts) = net.signals(33)
    T = B * NT
    at, start = {}, 0
    for name, n in dict(hot=T * NE3 * CAP, take=NE3 * T * P, a=T * D, aT=T * P, z=T * D, res=4 * T * P, sent=NE3 * CAP,
                        eo=NE3 * D, inter=2 * 4 * CAP, slots=T * P, diag=T * P).items():
        at[name] = net.arena[:, start:start + n]
        start += n
    rows = lambda name: at[name].rearrange("p (t d) -> p t d", t=T)
    a_rows, z_rows, eo = rows("a"), rows("z"), rows("eo")
    hot = at["hot"].rearrange("p (t n) -> p t n", t=T)
    take = at["take"].rearrange("p (e s) -> p e s", e=NE3)
    res = at["res"].rearrange("p (c s) -> p c s", c=4)
    inter = at["inter"].rearrange("p (a c s) -> p a c s", a=2, c=4)
    diag = rows("diag")
    wi, wo = net.fc, net.proj
    iota, before, gate_w = net.w2f["in"], net.w2f["out"][:, 0, :], net.w2f["out"][:, 1, 0:NE3 + 2]
    r = net.small
    HALF = T * P // BANK

    with nc.Block() as block:
        @block.sync
        def _(sp):
            d = net.d
            sp.dma_start(before, d["before"]).then_inc(w_gate, 16)
            sp.dma_start(gate_w, d["gate"]).then_inc(w_gate, 16)
            sp.dma_start(iota[:], d["iota"]).then_inc(w_gate, 16)
            sp.dma_start(wi[:, NE3, :], d["res_in"]).then_inc(w_res, 16)
            sp.dma_start(wo[:, NE3, :, :], d["res_out"]).then_inc(w_res, 16)
            sp.dma_start(wi[:, 0:NE3, :], d["inter"]).then_inc(w_experts, 16)
            sp.dma_start(wo[:, 0:NE3, :, :], d["output"]).then_inc(w_experts, 16)
            for t in range(T):
                sp.wait_ge(final, t + 1)
                sp.dma_start(out[t // NT, (t % NT) * P:(t % NT + 1) * P, :], net.x_all[:, t, :]).then_inc(written, 16)
            sp.wait_ge(written, 16 * T)

        @block.tensor
        def _(pe):
            pe.wait_ge(rows_ready, 1)
            for j in range(HALF):
                for t in range(4):
                    last = nc.tensor.transpose(net.ps[:, j, t * P:(t + 1) * P], a_rows[:, 4 * j + t, :], net.ident[:])
                last.then_inc(turned, 1)
            pe.wait_ge(cols_ready, HALF)
            pe.wait_ge(w_gate, 48)
            for t in range(T):
                last = nc.tensor.matmul(net.ps[:, 2, t * 10:(t + 1) * 10], at["aT"][:, t * P:(t + 1) * P], gate_w, start=True, stop=True)
            last.then_inc(logits_ready, 1)
            pe.wait_ge(w_res, 32)
            for i in range(4 * HALF):
                c, j = divmod(i, HALF)
                if i >= 4:
                    pe.wait_ge(res_gelu, i - 3)
                nc.tensor.matmul(net.ps[:, 4 + i % 4, :], wi[:, NE3, c * P:(c + 1) * P], at["aT"][:, j * BANK:(j + 1) * BANK],
                                 start=True, stop=True).then_inc(res_in, 1)
            pe.wait_ge(mask_ready, 1)
            mask = r["mask"]
            flat = net.ps[:, 3, 0:T * NE3]
            nc.tensor.matmul(flat, before, mask[:].rearrange("p t e -> p (t e)"), start=True, stop=False)
            for t in range(T - 1):
                last = nc.tensor.matmul(net.ps[:, 3, (t + 1) * NE3:T * NE3].rearrange("p (t e) -> p t e", e=NE3), net.ones[:],
                                        mask[:, t, :].unsqueeze(1).to_broadcast([P, T - 1 - t, NE3]), start=False, stop=t == T - 2)
            last.then_inc(places_ready, 1)
            pe.wait_ge(diag_ready, 1)
            for j in range(HALF):
                nc.tensor.matmul(net.ps[:, j, :], net.ones[:], at["diag"][:, j * BANK:(j + 1) * BANK], start=True, stop=True).then_inc(spread_ready, 1)
            pe.wait_ge(res_gelu, 4 * HALF)
            for t in range(T):
                pe.wait_ge(hot_ready, t + 1)
                for j in range(2):
                    last = nc.tensor.matmul(net.ps[:, 4 + j, :], a_rows[:, t, :], hot[:, t, j * BANK:(j + 1) * BANK],
                                            start=t == 0, stop=t == T - 1)
            last.then_inc(sent, 1)
            pe.wait_ge(sent_copied, 2)
            pe.wait_ge(w_experts, 32)
            for e in range(NE3 + 1):
                if e < NE3:
                    if e >= 2:
                        pe.wait_ge(inter_gelu, 4 * (e - 1))
                    for c in range(4):
                        last = nc.tensor.matmul(net.ps[:, 6 + e % 2, c * CAP:(c + 1) * CAP], wi[:, e, c * P:(c + 1) * P],
                                                at["sent"][:, e * CAP:(e + 1) * CAP], start=True, stop=True)
                    last.then_inc(inter_ready, 1)
                if e >= 1:
                    v = e - 1
                    pe.wait_ge(inter_gelu, 4 * (v + 1))
                    if v >= 2:
                        pe.wait_ge(expert_copied, v - 1)
                    for c in range(4):
                        last = nc.tensor.matmul(net.ps[:, 4 + v % 2, 0:D], inter[:, v % 2, c, :], wo[:, v, c, :], start=c == 0, stop=c == 3)
                    last.then_inc(expert_ready, 1)
            pe.wait_ge(expert_copied, NE3)
            pe.wait_ge(take_ready, NE3)
            for t in range(T):
                if t >= 4:
                    pe.wait_ge(final, t - 3)
                bank = t % 4
                for e in range(NE3):
                    nc.tensor.matmul(net.ps[:, bank, 0:D], take[:, e, t * P:(t + 1) * P], eo[:, e, :], start=e == 0, stop=e == NE3 - 1)
                for c in range(4):
                    last = nc.tensor.matmul(net.ps[:, bank, D:2 * D], res[:, c, t * P:(t + 1) * P], wo[:, NE3, c, :],
                                            start=c == 0, stop=c == 3)
                last.then_inc(mixed, 1)

        @block.scalar
        def _(act):
            link = linker(act, act_link)
            act_rsqrt_seed(nc, act, link, net, T, var_ready, 1, seed_ready)
            act_rsqrt_seed(nc, act, link, net, T, var_ready, 2, seed_ready)
            for j in range(HALF):
                act.wait_ge(turned, j + 1)
                nc.scalar.copy(at["aT"][:, j * BANK:(j + 1) * BANK], net.ps[:, j, :]).then_inc(cols_ready, 1)
            act.wait_ge(exp_in, 1)
            nc.scalar.activation(r["e"][:], r["e"][:], ACT.Exp).then_inc(exp_out, 1)
            for i in range(4 * HALF):
                c, j = divmod(i, HALF)
                act.wait_ge(res_in, i + 1)
                nc.scalar.activation(res[:, c, j * BANK:(j + 1) * BANK], net.ps[:, 4 + i % 4, :], ACT.Gelu_apprx_tanh,
                                     bias=net.col("L3_rb", c)).then_inc(res_gelu, 1)
            for j in range(HALF):
                act.wait_ge(spread_ready, j + 1)
                nc.scalar.copy(at["slots"][:, j * BANK:(j + 1) * BANK], net.ps[:, j, :]).then_inc(spread_copied, 1)
            act.wait_ge(sent, 1)
            for j in range(2):
                nc.scalar.copy(at["sent"][:, j * BANK:(j + 1) * BANK], net.ps[:, 4 + j, :]).then_inc(sent_copied, 1)
            for e in range(NE3):
                act.wait_ge(inter_ready, e + 1)
                if e >= 2:
                    act.wait_ge(expert_ready, e - 1)
                for c in range(4):
                    nc.scalar.activation(inter[:, e % 2, c, :], net.ps[:, 6 + e % 2, c * CAP:(c + 1) * CAP], ACT.Gelu_apprx_tanh,
                                         bias=net.col("L3_b", 4 * e + c)).then_inc(inter_gelu, 1)

        @block.gpsimd
        def _(pool):
            pool.wait_ge(spread_copied, HALF)
            for e in range(NE3):
                nc.gpsimd.tensor_scalar(take[:, e, :], at["slots"], net.col("L3_slot", e), None, ALU.is_equal).then_inc(take_ready, 1)

        @block.vector
        def _(dve):
            link = linker(dve, dve_link)
            link(dve_norm_rows(nc, dve, link, net, rows_of(net.x_all), rows_of(z_rows), T, 1e-5, var_ready, seed_ready, 1))
            link(dve_norm_rows(nc, dve, link, net, rows_of(z_rows), rows_of(a_rows), T, 1e-12, var_ready, seed_ready, 2))
            every = lambda name: net.row(name, 0).unsqueeze(1).to_broadcast([P, T, D])
            link(nc.vector.tensor_tensor(a_rows, a_rows, every("L3_nw"), ALU.mult))
            nc.vector.tensor_tensor(a_rows, a_rows, every("L3_nb"), ALU.add).then_inc(rows_ready, 1)
            link(nc.vector.tensor_tensor(net.x_all[:], net.x_all[:], z_rows, ALU.add))
            dve.wait_ge(logits_ready, 1)
            logits = net.ps[:, 2, 0:T * 10].rearrange("p (t e) -> p t e", t=T)
            sm, mx, e10, top, idx, idxf = r["sm"], r["mx"], r["e"], r["top"], r["idx"], r["idxf"]
            parts = ((slice(0, NE3), slice(0, T)), (slice(NE3, NE3 + 2), slice(T, 2 * T)))
            for e, m in parts:
                last = nc.vector.reduce_max(mx[:, m], logits[:, :, e], AX.X)
            link(last)
            for e, m in parts:
                last = nc.vector.tensor_tensor(e10[:, :, e], logits[:, :, e], spread(mx[:, m], e.stop - e.start), ALU.subtract)
            last.then_inc(exp_in, 1)
            dve.wait_ge(exp_out, 1)
            for e, m in parts:
                last = nc.vector.reduce_sum(sm[:, m], e10[:, :, e], AX.X)
            link(last)
            link(nc.vector.reciprocal(sm[:], sm[:]))
            link(nc.vector.tensor_tensor(e10[:, :, 8:10], e10[:, :, 8:10], spread(sm[:, T:2 * T], 2), ALU.mult))
            link(nc.vector.tensor_tensor(r["p8"][:], e10[:, :, 0:NE3], spread(sm[:, 0:T], NE3), ALU.mult))
            for t in range(T):
                last = nc.vector.max(top[:, t, :], r["p8"][:, t, :])
            link(last)
            for t in range(T):
                last = nc.vector.max_index(idx[:, t, :], top[:, t, :], r["p8"][:, t, :])
            link(last)
            link(nc.vector.tensor_copy(idxf[:, :, 0:1], idx[:, :, 0:1]))
            nc.vector.tensor_tensor(r["mask"][:], net.iota[:, 0:NE3].unsqueeze(1).to_broadcast([P, T, NE3]), spread(idxf[:, :, 0], NE3),
                                    ALU.is_equal).then_inc(mask_ready, 1)
            dve.wait_ge(places_ready, 1)
            link(nc.vector.tensor_tensor(r["place"][:], net.ps[:, 3, 0:T * NE3].rearrange("p (t e) -> p t e", t=T), r["mask"][:], ALU.mult))
            loc, slot = mx[:, 0:T], mx[:, T:2 * T]
            link(nc.vector.reduce_sum(loc, r["place"][:], AX.X))
            link(nc.vector.scalar_tensor_tensor(slot, idxf[:, :, 0], float(CAP), loc, ALU.mult, ALU.add))
            link(nc.vector.tensor_scalar(loc, loc, float(CAP), None, ALU.is_lt))
            link(nc.vector.tensor_scalar(slot, slot, 1.0, None, ALU.add))
            link(nc.vector.tensor_tensor(slot, slot, loc, ALU.mult))
            link(nc.vector.tensor_scalar(slot, slot, -1.0, None, ALU.add))
            for t in range(T):
                last = nc.vector.tensor_scalar(diag[:, t, :], net.ident[:], slot[:, t:t + 1], None, ALU.mult)
            last.then_inc(diag_ready, 1)
            for t in range(T):
                nc.vector.tensor_scalar(hot[:, t, :], iota[:], slot[:, t:t + 1], None, ALU.is_equal).then_inc(hot_ready, 1)
            link(nc.vector.tensor_tensor(r["p8"][:, :, 0], top[:, :, 0], e10[:, :, 9], ALU.mult))
            for e in range(NE3):
                dve.wait_ge(expert_ready, e + 1)
                nc.vector.tensor_tensor(eo[:, e, :], net.ps[:, 4 + e % 2, 0:D], net.row("L3_ob", e), ALU.add).then_inc(expert_copied, 1)
            for t in range(T):
                dve.wait_ge(mixed, t + 1)
                tmp, bank = diag[:, t, :], net.ps[:, t % 4, :]
                link(nc.vector.tensor_tensor(tmp, bank[:, D:2 * D], net.row("L3_rob", 0), ALU.add))
                link(nc.vector.scalar_tensor_tensor(net.x_all[:, t, :], tmp, e10[:, t, 8:9], net.x_all[:, t, :], ALU.mult, ALU.add))
                nc.vector.scalar_tensor_tensor(net.x_all[:, t, :], bank[:, 0:D], r["p8"][:, t, 0:1], net.x_all[:, t, :],
                                               ALU.mult, ALU.add).then_inc(final, 1)
    net.end_phase()


def program(nc, d, out):
    es = ExitStack()
    with es:
        net = Net(nc, es)
        net.d = d
        sb, sem = net.sb, net.sem
        sizes = dict(w0q=1024, w0k=1024, w0v=1024, w0o=1024, wf_qkv0=1536, wf_o0=512, wf_10=2 * HID, wf_20=384, wf_qkv1=1536,
                     wf_o1=512, wf_11=2 * HID, wf_21=384, w1q=1024, w1kv=2048, w1o=1024, qT=8 * S, kT=16 * S, v=4096,
                     heads=2048, probs=2 * BANK, probsT=2 * BANK)
        arena = sb("arena", [P, sum(sizes.values())])
        at, start = {}, 0
        for name, size in sizes.items():
            at[name] = arena[:, start:start + size]
            start += size
        chunked = lambda name, c: at[name].rearrange("p (c n) -> p c n", c=c)
        net.arena = arena
        net.w0 = dict(q=at["w0q"], k=at["w0k"], v=at["w0v"], o=chunked("w0o", 8))
        net.wf = [dict(qkv=at[f"wf_qkv{l}"], o=chunked(f"wf_o{l}", 4), w1=at[f"wf_1{l}"], w2=chunked(f"wf_2{l}", 3)) for l in range(2)]
        net.w1 = dict(q=at["w1q"], kv=at["w1kv"], o=chunked("w1o", 8))
        net.fc, net.proj = sb("fc", [P, NE1 + 1, FF]), sb("proj", [P, NE1 + 1, 4, D])
        net.router1, net.router2 = sb("router1", [P, NE1]), sb("router2", [P, NE2])
        net.w2x = dict(q=sb("w2q", [P, 2, D]), k=sb("w2k", [P, 2, D]), v=sb("w2v", [P, 2 * D]), o=sb("w2o", [P, D]))
        net.w2f = dict([("in", sb("w2in", [P, NE2 * H2])), ("out", sb("w2out", [P, 2 * NE2, D]))])
        cols = sb("cols", [P, d["cols"].shape[1]])
        rows = sb("rows", [P, d["rows"].shape[1]])
        net.col = lambda name, i: cols[:, COLS[name] + i:COLS[name] + i + 1]
        net.row = lambda name, i, n=D: rows[:, ROWS[name] + i * n:ROWS[name] + (i + 1) * n]
        net.band, band_f = sb("band", [P, NT * S], BF16), at["qT"][:, NT * S:2 * NT * S]
        net.cos_t, net.sin_t = sb("cos_t", [P, 2, NT, 2, DH]), sb("sin_t", [P, 2, NT, 2, DH])
        net.causal, causal_f = sb("causal", [P, NT * S], BF16), at["qT"][:, 0:NT * S]
        net.ones, net.ones_b, net.iota = sb("ones", [P, P]), sb("ones_b", [P, P], BF16), sb("iota", [P, S])
        net.share = sb("share", [P, 2])
        net.ident = sb("ident", [P, P])
        net.ident_b = sb("ident_b", [P, P], BF16)
        net.mask0 = sb("mask0", [P, NT * S], BF16)
        mask0_w = sb("mask0_w", [P, NT * S // 4], I32)
        net.x, net.z, net.ctx = sb("x", [P, NT, D]), sb("z", [P, NT, D]), sb("ctx", [P, NT, D])
        net.zT, net.ctxT = sb("zT", [P, S]), sb("ctxT", [P, S])
        net.ptr_i, net.ids_i, net.kmask_u = sb("ptr_i", [P, NT], I32), sb("ids_i", [1, S], I32), sb("kmask_u", [1, S // 4], I32)
        net.stats, net.mv = sb("stats", [P, 8, 6]), sb("mv", [P, 8, 2])
        net.veps, net.lnv, net.seed = sb("veps", [P, 32]), sb("lnv", [P, 32]), sb("seed", [P, 32])
        net.nwt, net.rstd = sb("nwt", [P, 32]), sb("rstd", [P, 32])
        net.rowmax, net.negmax = sb("rowmax", [P, 4, 2]), sb("negmax", [P, 4, 2])
        net.sums, net.recip = sb("sums", [P, NT, H16]), sb("recip", [P, 4, H16])
        net.qT, net.kT, net.v, net.heads = chunked("qT", 8), chunked("kT", 8), chunked("v", 4), chunked("heads", NT)
        net.probs, net.probsT = chunked("probs", 2), chunked("probsT", 2)
        net.qk = net.kT[:].rearrange("p m s -> p (m s)")[:, 2048:4096].rearrange("p (t n) -> p t n", t=NT)
        net.qk_sin = net.v[:, 2:4, :]
        net.qk_rot = net.heads[:]
        net.squares = net.probs[:].rearrange("p s n -> p (s n)")
        net.ssq, net.rnorm = sb("ssq", [P, NT, 16]), sb("rnorm", [P, NT, 16])
        net.hT, net.hs, net.hn, net.hnT = sb("hT", [P, S]), sb("hs", [P, NT, D]), sb("hn", [P, NT, D]), sb("hnT", [P, S])
        net.kv_in, net.cn, net.kmask = sb("kv_in", [P, 2 * S]), sb("cn", [P, NT, D]), sb("kmask", [1, 2 * S], BF16)
        net.ids_f, net.s6, net.comb, net.hs2 = sb("ids_f", [1, S]), sb("s6", [P, 2, NT, 3]), sb("comb", [P, NT, 8]), sb("hs2", [P, NT, D])
        net.small = dict(mx=sb("r_mx", [P, 16]), sm=sb("r_sm", [P, 16]), top=sb("r_top", [P, 8, 8]), idx=sb("r_idx", [P, 8, 8], U32),
                         idxf=sb("r_idxf", [P, 8, 8]), e=sb("r_e", [P, 8, 10]), p8=sb("r_p8", [P, 8, 8]), p4=sb("r_p4", [P, NT, 8]),
                         w2=sb("r_w2", [P, NT, 2]), eq=sb("r_eq", [P, 2, NT, 8]), ptr=sb("r_ptr", [P, 4, NT]), rel=sb("r_rel", [P, NT]),
                         val=sb("r_val", [P, 6, NT]), new=sb("r_new", [P, NT]), any=sb("r_any", [P, NT]))
        net.small["mask"], net.small["place"] = sb("r_mask", [P, 8, 8]), sb("r_place", [P, 8, 8])
        net.small["is"] = sb("r_is", [P, 5, NT])
        net.small["w2"] = net.small["w2"][:]
        net.x_all = sb("x_all", [P, B * NT, D])
        net.gate = at["probsT"][:, 0:3 * S].rearrange("p (c s) -> p c s", c=3)
        net.hid = at["kT"][:, 0:3 * S].rearrange("p (c s) -> p c s", c=3)
        net.ps = es.enter_context(nc.psum_tensor("ps", [P, 8, BANK], F32))

        const_loaded, const_ready, const_link = sem("const_loaded"), sem("const_ready"), sem("const_link")
        net.w0_loaded, net.w0_count = sem("w0_loaded"), 16 * 4
        net.wf_loaded, net.wf_count = sem("wf_loaded"), 16 * 12
        net.w1_loaded, net.w1_count = sem("w1_loaded"), 16 * 3
        net.w1f_loaded, net.w1f_count = sem("w1f_loaded"), 16 * 3
        net.w2_loaded, net.w2_count = sem("w2_loaded"), 16 * 7

        with nc.Block() as block:
            @block.sync
            def _(sp):
                sp.dma_start(net.ident[:], d["ident"]).then_inc(const_loaded, 16)
                sp.dma_start(mask0_w[:].rearrange("p (t k) -> p t k", t=NT), d["mask0"].rearrange("(t p) k -> p t k", p=P)).then_inc(const_loaded, 16)
                sp.dma_start(band_f.rearrange("p (t k) -> p t k", t=NT), d["band"].rearrange("(t p) k -> p t k", p=P)).then_inc(const_loaded, 16)
                sp.dma_start(causal_f.rearrange("p (t k) -> p t k", t=NT), d["causal"].rearrange("(t p) k -> p t k", p=P)).then_inc(const_loaded, 16)
                sp.dma_start(net.iota[:], d["iota"][:, 0:S]).then_inc(const_loaded, 16)
                sp.dma_start(cols[:], d["cols"]).then_inc(const_loaded, 16)
                sp.dma_start(rows[:], d["rows"]).then_inc(const_loaded, 16)
                for table, name in ((net.cos_t, "cos"), (net.sin_t, "sin")):
                    for l in range(2):
                        sp.dma_start(table[:, l, :, :, :], d[name]).then_inc(const_loaded, 16)
                for name in "qkv":
                    sp.dma_start(net.w0[name][:], d["L0_xattn_w_" + name]).then_inc(net.w0_loaded, 16)
                sp.dma_start(net.w0["o"][:], d["L0_xattn_w_o"].rearrange("(c p) n -> p c n", p=P)).then_inc(net.w0_loaded, 16)
                for l in range(2):
                    sp.dma_start(net.wf[l]["qkv"][:], d["L0_ffn_wqkv"][l, :, :]).then_inc(net.wf_loaded, 16)
                    sp.dma_start(net.wf[l]["o"][:], d["L0_ffn_wo"][l, :, :].rearrange("(c p) n -> p c n", p=P)).then_inc(net.wf_loaded, 16)
                    sp.dma_start(net.wf[l]["w1"][:], d["L0_ffn_w1"][l, :, :]).then_inc(net.wf_loaded, 16)
                    for c, (c0, cn) in enumerate(HC):
                        sp.dma_start(net.wf[l]["w2"][0:cn, c, :], d["L0_ffn_w2"][l, c0:c0 + cn, :]).then_inc(net.wf_loaded, 16)
                sp.dma_start(at["w1q"], d["L1_xattn_Wq"]).then_inc(net.w1_loaded, 16)
                sp.dma_start(at["w1kv"], d["L1_xattn_Wkv"]).then_inc(net.w1_loaded, 16)
                sp.dma_start(net.w1["o"], d["L1_xattn_Wout"].rearrange("(c p) n -> p c n", p=P)).then_inc(net.w1_loaded, 16)
                sp.dma_start(net.fc[:], d["fc"]).then_inc(net.w1f_loaded, 16)
                sp.dma_start(net.proj[:], d["proj"]).then_inc(net.w1f_loaded, 16)
                sp.dma_start(net.router1[:], d["router1"]).then_inc(net.w1f_loaded, 16)
                for name, tile in (("w2q", net.w2x["q"]), ("w2k", net.w2x["k"]), ("w2v", net.w2x["v"]), ("w2o", net.w2x["o"]),
                                   ("router2", net.router2), ("w2in", net.w2f["in"]), ("w2out", net.w2f["out"])):
                    sp.dma_start(tile[:], d[name]).then_inc(net.w2_loaded, 16)

            @block.scalar
            def _(act):
                nc.scalar.preload_act_table_set("natural_log_exp_and_others")
                act.wait_ge(const_ready, 3)
                nc.scalar.activation(net.share[:], net.share[:], ACT.Exp).then_inc(const_ready, 1)

            @block.vector
            def _(dve):
                link = linker(dve, const_link)
                dve.wait_ge(const_loaded, 16 * 11)
                link(nc.vector.reduce_max(net.recip[:, 0, 0:1], net.row("council", 0, 2), AX.X))
                nc.vector.tensor_scalar(net.share[:], net.row("council", 0, 2), net.recip[:, 0, 0:1], None, ALU.subtract).then_inc(const_ready, 3)
                nc.vector.memset(net.ones[:], 1.0)
                nc.vector.memset(net.ones_b[:], 1.0)
                nc.vector.memset(net.small["p4"][:], -1.0)
                nc.vector.memset(net.kmask[:], 0.0)
                dve.wait_ge(const_ready, 4)
                link(nc.vector.reduce_sum(net.recip[:, 1, 0:1], net.share[:], AX.X))
                link(nc.vector.reciprocal(net.recip[:, 2, 0:1], net.recip[:, 1, 0:1]))
                nc.vector.tensor_scalar(net.share[:], net.share[:], net.recip[:, 2, 0:1], None, ALU.mult)
                nc.vector.tensor_scalar(net.causal[:], causal_f, MASKED, None, ALU.mult)
                nc.vector.tensor_copy(net.ident_b[:], net.ident[:])
                nc.vector.tensor_scalar(net.band[:], band_f, MASKED, None, ALU.mult)
                nc.vector.memset(net.hs[0:1, 0, D // 2:D], 0.0)
                for l in range(2):
                    for t in range(NT):
                        for a, name in enumerate(("q_scale", "k_scale")):
                            row = net.row(name, l, DH)
                            cos, sin = net.cos_t[:, l, t, a, :], net.sin_t[:, l, t, a, :]
                            nc.vector.tensor_tensor(cos, cos, row, ALU.mult)
                            nc.vector.tensor_tensor(sin[:, 0:32], sin[:, 0:32], row[:, 32:64], ALU.mult)
                            nc.vector.tensor_tensor(sin[:, 32:64], sin[:, 32:64], row[:, 0:32], ALU.mult)
                nc.vector.tensor_scalar(net.mask0[:], mask0_w[:].bitcast(U8), MASKED, None, ALU.mult)

        with nc.Fori(0, B) as batch:
            net.batch = batch
            layer0_attention(net)
            norm_x(net)
            for l in range(2):
                local_block(net, l)
            layer1_attention(net)
            layer1_experts(net)
            layer2_attention(net)
            layer2_experts(net)
            layer3_attention(net)
        layer3_experts(net, out)


def rotary_tables():
    half = np.arange(0, DH, 2, dtype=np.float32)
    t = np.arange(S, dtype=np.float32)
    angle = t[:, None] * (1.0 / 10000.0 ** (half / DH)).astype(np.float32)[None, :]
    base = (half + 0.4 * DH) / (1.4 * DH)
    scale = base[None, :] ** ((t - S // 2) / 32.0)[:, None]
    scale = np.concatenate([scale, scale], -1)
    cos = np.concatenate([np.cos(angle), np.cos(angle)], -1)
    sin = np.concatenate([-np.sin(angle), np.sin(angle)], -1)
    return [np.ascontiguousarray(np.stack([m * scale, m / scale], 1).reshape(NT, P, 2, DH).transpose(1, 0, 2, 3), dtype=np.float32)
            for m in (cos, sin)]


COLS = dict(L0_ln_g=0, L0_ln_b=2, L0_b1=4, L1_g_x=16, L1_b_x=17, L1_g_l=18, L1_b_l=19, L2_rn_g=20, L2_rn_b=21,
            L2_ln_g=22, L2_ln_b=30, L3_b=38, L3_rb=70, L3_slot=74, end=82)
ROWS = dict(q_scale=0, k_scale=128, L0_b2=256, L1_g_o=512, L1_b_o=640, L2_on_g=768, L2_on_b=896, council=1024, gain=1026,
            L3_nw=1028, L3_nb=1156, L3_ob=1284, L3_rob=1284 + 1024, end=1284 + 1152)


def packed_columns(a):
    cols = np.zeros((P, COLS["end"]), np.float32)
    for l in range(2):
        cols[:, COLS["L0_ln_g"] + l] = a["L0_ffn_ln_g"][l]
        cols[:, COLS["L0_ln_b"] + l] = a["L0_ffn_ln_b"][l]
        for part in range(2):
            for c, (c0, cn) in enumerate(HC):
                cols[0:cn, COLS["L0_b1"] + 6 * l + 3 * part + c] = a["L0_ffn_b1"][l, part * HID + c0:part * HID + c0 + cn]
    cols[:, COLS["L3_slot"]:COLS["end"]] = np.arange(P)[:, None] + CAP * np.arange(NE3)[None, :]
    for name, src in (("L1_g_x", "L1_xattn_g_x"), ("L1_b_x", "L1_xattn_b_x"), ("L1_g_l", "L1_xattn_g_l"), ("L1_b_l", "L1_xattn_b_l"),
                      ("L2_rn_g", "L2_ffn_rn_g"), ("L2_rn_b", "L2_ffn_rn_b"), ("L2_ln_g", "L2_ffn_ln_g"), ("L2_ln_b", "L2_ffn_ln_b"),
                      ("L3_b", "L3_ffn_inter_b"), ("L3_rb", "L3_ffn_res_inter_b")):
        n = a[src].size // P
        cols[:, COLS[name]:COLS[name] + n] = a[src].reshape(n, P).T
    return cols


def packed_rows(a):
    row = np.zeros(ROWS["end"], np.float32)
    for name, src in (("q_scale", "L0_ffn_q_scale"), ("k_scale", "L0_ffn_k_scale"), ("L0_b2", "L0_ffn_b2"), ("L1_g_o", "L1_xattn_g_o"),
                      ("L1_b_o", "L1_xattn_b_o"), ("L2_on_g", "L2_ffn_on_g"), ("L2_on_b", "L2_ffn_on_b"),
                      ("council", "L2_xattn_council_weights"), ("gain", "L2_xattn_gain"), ("L3_nw", "L3_ffn_attn_nw"),
                      ("L3_nb", "L3_ffn_attn_nb"), ("L3_ob", "L3_ffn_output_b"), ("L3_rob", "L3_ffn_res_output_b")):
        row[ROWS[name]:ROWS[name] + a[src].size] = a[src].reshape(-1)
    return np.ascontiguousarray(np.broadcast_to(row, (P, row.size)))


def laid_out(inputs):
    a = {k: np.asarray(v) for k, v in inputs.items()}
    c = np.ascontiguousarray
    cos, sin = rotary_tables()
    far = np.arange(S)[:, None] - np.arange(S)[None, :]
    return {
        "x": a["x"], "ctx": a["ctx_1024"], "ctxT": c(a["ctx_1024"].transpose(0, 2, 1)),
        "ids": a["itok_BxS_0_7"], "ptr": c(a["itok_BxS_0_4092"].reshape(B, NT, P).transpose(0, 2, 1)),
        "mask0": c(a["mask_1x1xSxS2_bk1"].reshape(S, S)).view(np.int32), "kmask": c(a["mask_BxS2_bf1"]).view(np.int32),
        **{k: a[k] for k in ("L0_xattn_w_q", "L0_xattn_w_k", "L0_xattn_w_v", "L0_xattn_w_o")},
        **{k: a[k] for k in ("L0_ffn_wqkv", "L0_ffn_wo", "L0_ffn_w1", "L0_ffn_w2")},
        "cols": packed_columns(a), "rows": packed_rows(a), "cos": cos, "sin": sin,
        "band": ((far < 0) | (far > 64)).astype(np.float32),
        "causal": (far < 0).astype(np.float32),
        "iota": np.ascontiguousarray(np.broadcast_to(np.arange(NE3 * CAP, dtype=np.float32), (P, NE3 * CAP))),
        **{k: a[k] for k in ("L1_xattn_Wq", "L1_xattn_Wkv", "L1_xattn_Wout")},
        "fc": c(np.concatenate([a["L1_ffn_w_fc"], a["L1_ffn_shared_fc"][None]]).transpose(2, 0, 1)),
        "proj": c(np.concatenate([a["L1_ffn_w_proj"], a["L1_ffn_shared_proj"][None]]).reshape(NE1 + 1, D, 4, P).transpose(3, 0, 2, 1)),
        "router1": c(a["L1_ffn_router_w"].T), "router2": c(a["L2_ffn_router_w"].T),
        "w2q": c(np.stack([a["L2_xattn_Wqj"].T, a["L2_xattn_Wqi"].T], 1)), "w2k": c(np.stack([a["L2_xattn_Wkj"].T, a["L2_xattn_Wki"].T], 1)),
        "w2v": c(np.concatenate([a["L2_xattn_Wvj"].T, a["L2_xattn_Wvi"].T], 1)), "w2o": c(a["L2_xattn_Wout"].T),
        "w2in": c(a["L2_ffn_w1"].transpose(1, 0, 2).reshape(D, NE2 * H2)),
        "w2out": c(a["L2_ffn_w2"].reshape(2 * NE2, P, D).transpose(1, 0, 2)),
        "before": c((far[0:P, 0:P] < 0).astype(np.float32)), "gate": c(np.concatenate([a["L3_ffn_wg"], a["L3_ffn_res_coef"]], 1)),
        "res_in": a["L3_ffn_res_inter_w"], "res_out": c(a["L3_ffn_res_output_w"].reshape(4, P, D).transpose(1, 0, 2)),
        "inter": c(a["L3_ffn_inter_w"].transpose(1, 0, 2)),
        "output": c(a["L3_ffn_output_w"].reshape(NE3, 4, P, D).transpose(2, 0, 1, 3)),
        "ident": np.eye(P, dtype=np.float32),
    }


def kernel(**inputs):
    import concourse.bacc as bacc
    from concourse.bass_utils import run_bass_kernel_spmd

    nc = bacc.Bacc("TRN2", target_bir_lowering=False, num_devices=1)
    arrays = {f"in_{k}": v for k, v in laid_out(inputs).items()}
    d = {k[3:]: nc.dram_tensor(k, v.shape, mybir.dt.from_np(v.dtype), kind="ExternalInput").ap() for k, v in arrays.items()}
    out = nc.dram_tensor("out", (B, S, D), F32, kind="ExternalOutput").ap()
    program(nc, d, out)
    return run_bass_kernel_spmd(nc, [arrays], core_ids=[0]).results[0]["out"]
```

```python
import numpy as np
import concourse.bass as bass
from concourse import mybir
from contextlib import ExitStack

F32 = mybir.dt.float32
BF16 = mybir.dt.bfloat16
I32 = mybir.dt.int32
U32 = mybir.dt.uint32
U8 = mybir.dt.uint8
ALU = mybir.AluOpType
ACT = mybir.ActivationFunctionType
AX = mybir.AxisListType

B, S, D = 4, 256, 128
P = 128
NT = S // P
T = B * NT
LB = 2
LT = LB * NT
DH = 64
H16, H8 = 16, 8
BANK = 512
HID = 341
HC = [(0, 128), (128, 128), (256, HID - 256)]
NE1, FF = 8, 512
NE2, H2 = 4, 256
NE3, CAP = 8, B * S // 8
MASKED = -1.0e30
LN_EXP = "natural_log_exp_and_others"


def linker(engine, sem):
    count = [0]

    def link(ins):
        count[0] += 1
        ins.then_inc(sem, 1)
        engine.wait_ge(sem, count[0])
    return link


class Net:

    def __init__(self, nc, es):
        self.nc, self.es = nc, es
        self.pool = [es.enter_context(nc.semaphore(f"phase_{i}")) for i in range(40)]

    def sb(self, name, shape, dt=F32):
        return self.es.enter_context(self.nc.sbuf_tensor(name, shape, dt))

    def sem(self, name):
        return self.es.enter_context(self.nc.semaphore(name))

    def signals(self, n):
        return self.pool[:n]

    def end_phase(self):
        self.nc.all_engine_barrier(sems_to_clear=range(self.pool[0].num, self.pool[-1].num + 1))



def dve_stats(nc, link, net, rows, n, eps, var_ready):
    for t in range(n):
        last = nc.vector.bn_stats(net.stats[:, t, :], rows(t))
    link(last)
    for t in range(n):
        last = nc.vector.bn_aggr(net.mv[:, t, :], net.stats[:, t, :])
    link(last)
    nc.vector.tensor_scalar(net.veps[:, 0:n], net.mv[:, 0:n, 1], eps, None, ALU.add).then_inc(var_ready, 1)


def act_rsqrt_seed(nc, act, link, net, n, var_ready, k, seed_ready):
    act.wait_ge(var_ready, k)
    link(nc.scalar.activation(net.lnv[:, 0:n], net.veps[:, 0:n], ACT.Ln))
    nc.scalar.activation(net.seed[:, 0:n], net.lnv[:, 0:n], ACT.Exp, scale=-0.5).then_inc(seed_ready, 1)


def dve_rsqrt(nc, dve, link, net, n, seed_ready, k, out, factor=1.0):
    dve.wait_ge(seed_ready, k)
    y, v, t = net.seed[:, 0:n], net.veps[:, 0:n], net.nwt[:, 0:n]
    link(nc.vector.scalar_tensor_tensor(t, y, -0.5 * factor, y, ALU.mult, ALU.mult))
    link(nc.vector.tensor_tensor(t, t, v, ALU.mult))
    link(nc.vector.scalar_tensor_tensor(out, t, 1.5 * factor, y, ALU.add, ALU.mult))


def dve_normalise(nc, net, out, rows, n):
    for t in range(n):
        last = nc.vector.tensor_scalar(out(t), rows(t), net.mv[:, t, 0:1], net.rstd[:, t:t + 1],
                                       ALU.subtract, ALU.mult)
    return last



def pe_projections(nc, pe, net, tiles, banks, tile_ready, emptied):
    for j, products in enumerate(tiles):
        if j >= banks:
            pe.wait_ge(emptied[j % 2], (j - banks) // 2 + 1)
        for a, b, stationary, moving in products:
            last = nc.tensor.matmul(net.ps[:, j % banks, a:b], stationary, moving, start=True, stop=True)
        last.then_inc(tile_ready, 1)


def empty_projections(nc, engine, copy, net, outs, banks, which, tile_ready, emptied):
    for j, out in enumerate(outs):
        if j % 2 == which:
            engine.wait_ge(tile_ready, j + 1)
            copy(out, net.ps[:, j % banks, :]).then_inc(emptied[which], 1)


def evac_counts(n):
    return ((n + 1) // 2, n // 2)



class Attention:
    LAG = 3

    def __init__(self, net, units, mask, qT, kT, v, scale, out, sems):
        self.net, self.units, self.mask, self.qT, self.kT, self.v, self.scale, self.out = net, units, mask, qT, kT, v, scale, out
        (self.scores_ready, self.masked, self.exped, self.inverted, self.normed, self.turned, self.act_copied,
         self.dve_copied, self.pv_done, self.out_copied) = sems
        segments = units[0][1]
        self.ns = len(segments)
        self.cols = [sum(nk for _, nk in segments[:i]) for i in range(self.ns)]
        self.blocks, self.products, at = [], [], 0
        for k in range(max(nk for _, nk in segments) // P):
            having = [i for i in range(self.ns) if segments[i][1] > k * P]
            self.products.append((k, at, len(having) * P, having[0] * P))
            for i in having:
                self.blocks.append((self.cols[i] + k * P, at))
                at += P
        self.width = at

    def out_count(self):
        return len(self.units) // 2

    def pe(self, nc, pe):
        net, ns, U = self.net, self.ns, len(self.units)
        for step in range(U + self.LAG + 3):
            if step < U:
                u = step
                h, segments = self.units[u]
                if u >= 2:
                    pe.wait_ge(self.masked, ns * (u - 1))
                for i, (qt, nk) in enumerate(segments):
                    last = nc.tensor.matmul(net.ps[:, u % 2, self.cols[i]:self.cols[i] + nk], self.qT(h, qt), self.kT(h, nk),
                                            start=True, stop=True)
                last.then_inc(self.scores_ready, 1)
            u = step - self.LAG
            if 0 <= u < U:
                pe.wait_ge(self.normed, ns * (u + 1))
                if u >= 2:
                    pe.wait_ge((self.act_copied, self.dve_copied)[u % 2], u // 2)
                for src, dst in self.blocks:
                    last = nc.tensor.transpose(net.ps[:, 2 + u % 2, dst:dst + P], net.probs[:, u % 4, src:src + P], net.ident[:])
                last.then_inc(self.turned, 1)
            u = step - self.LAG - 1
            if u >= 1 and u % 2 == 1 and u < U:
                p = u // 2
                pe.wait_ge(self.act_copied, p + 1)
                pe.wait_ge(self.dve_copied, p + 1)
                if p >= 4:
                    pe.wait_ge(self.out_copied, p - 3)
                for k, at, n, q in self.products:
                    for j in range(2):
                        last = nc.tensor.matmul(net.ps[DH * j:DH * (j + 1), 4 + p % 4, q:q + n],
                                                self.v(self.units[u - 1 + j][0], k), net.probsT[:, (u - 1 + j) % 4, at:at + n],
                                                start=k == 0, stop=k == len(self.products) - 1)
                last.then_inc(self.pv_done, 1)

    def copy_turned(self, nc, engine, copy, u):
        net = self.net
        if u < 0 or u >= len(self.units):
            return
        engine.wait_ge(self.turned, u + 1)
        if u >= 4:
            engine.wait_ge(self.pv_done, (u - 4) // 2 + 1)
        copy(net.probsT[:, u % 4, 0:self.width], net.ps[:, 2 + u % 2, 0:self.width]).then_inc((self.act_copied, self.dve_copied)[u % 2], 1)

    def act(self, nc, act):
        net, ns, U = self.net, self.ns, len(self.units)
        for step in range(U + self.LAG + 5):
            if step < U:
                u = step
                for i, (qt, nk) in enumerate(self.units[u][1]):
                    act.wait_ge(self.masked, ns * u + i + 1)
                    if u >= 4:
                        act.wait_ge(self.inverted, u - 3)
                    x = net.probs[:, u % 4, self.cols[i]:self.cols[i] + nk]
                    nc.scalar.activation(x, x, ACT.Exp, bias=net.negmax[:, u % 4, i:i + 1], scale=-1.0,
                                         accum_out=net.sums[:, u % 4, i:i + 1]).then_inc(self.exped, 1)
            if (step - self.LAG) % 2 == 0:
                self.copy_turned(nc, act, nc.scalar.copy, step - self.LAG)
            u = step - self.LAG - 2
            if u >= 1 and u % 2 == 1 and u < U:
                p = u // 2
                act.wait_ge(self.pv_done, p + 1)
                dst = self.out(self.units[u][0], self.units[u][1])
                nc.scalar.copy(dst, net.ps[:, 4 + p % 4, 0:dst.shape[-1]]).then_inc(self.out_copied, 1)

    def dve(self, nc, dve):
        net, ns, U = self.net, self.ns, len(self.units)
        for step in range(U + self.LAG + 2):
            if step < U:
                u = step
                h, segments = self.units[u]
                dve.wait_ge(self.scores_ready, u + 1)
                if u >= 4:
                    dve.wait_ge(self.turned, u - 3)
                for i, (qt, nk) in enumerate(segments):
                    c = slice(self.cols[i], self.cols[i] + nk)
                    nc.vector.tensor_tensor_reduce(out=net.probs[:, u % 4, c], in0=net.ps[:, u % 2, c], in1=self.mask[:, c],
                                                   scale=self.scale(h, qt), scalar=-MASKED, op0=ALU.add, op1=ALU.min,
                                                   accum_out=net.negmax[:, u % 4, i:i + 1]).then_inc(self.masked, 1)
            u = step - 1
            if 0 <= u < U:
                dve.wait_ge(self.exped, ns * (u + 1))
                if u >= 4:
                    dve.wait_ge(self.normed, ns * (u - 3))
                nc.vector.reciprocal(net.recip[:, u % 4, 0:ns], net.sums[:, u % 4, 0:ns]).then_inc(self.inverted, 1)
            if (step - self.LAG) % 2 == 1:
                self.copy_turned(nc, dve, nc.vector.tensor_copy, step - self.LAG)

    def pool(self, nc, pool):
        net = self.net
        for u, (h, segments) in enumerate(self.units):
            pool.wait_ge(self.inverted, u + 1)
            for i, (qt, nk) in enumerate(segments):
                x = net.probs[:, u % 4, self.cols[i]:self.cols[i] + nk]
                nc.gpsimd.tensor_scalar(x, x, net.recip[:, u % 4, i:i + 1], 1.0, ALU.mult, ALU.mult).then_inc(self.normed, 1)


def head_rows(h):
    return slice(DH * (h % 2), DH * (h % 2) + DH)


def pe_out_projection(nc, pe, net, attn, qT, chunks, w, result, tiles=NT):
    pe.wait_ge(attn.out_copied, attn.out_count())
    for t in range(tiles):
        for c in range(chunks):
            last = nc.tensor.matmul(net.ps[:, 0, t * P:(t + 1) * P], qT[:, c, t * P:(t + 1) * P], w[:, c, :],
                                    start=c == 0, stop=c == chunks - 1)
    last.then_inc(result, 1)


def batch_rows(net):
    return net.x_all[:, bass.ds(net.batch * NT, NT), :]


def batch_columns(net, ap):
    return ap[:, bass.ds(net.batch, 1), :].rearrange("p b s -> p (b s)")



def layer0_attention(net):
    nc = net.nc
    tile_ready, act_emptied, dve_emptied, ctxT_ready, zT_ready, o_ready, *att = net.signals(16)
    emptied = (act_emptied, dve_emptied)
    w = net.w0
    tiles, outs = [], []
    for m in range(0, 8, 2):
        tiles.append([(i * S, (i + 1) * S, w["k"][:, (m + i) * P:(m + i + 1) * P], net.ctxT[:]) for i in range(2)])
        outs.append(net.kT[:, m:m + 2, 0:S])
    for t in range(NT):
        for half in range(2):
            tiles.append([(0, BANK, net.ctxT[:, t * P:(t + 1) * P], w["v"][:, half * BANK:(half + 1) * BANK])])
            outs.append(net.v[:, t, half * BANK:(half + 1) * BANK])
    for m in range(0, 8, 2):
        tiles.append([(i * S, (i + 1) * S, w["q"][:, (m + i) * P:(m + i + 1) * P], net.zT[:]) for i in range(2)])
        outs.append(net.qT[:, m:m + 2, :])
    counts = evac_counts(len(tiles))
    attn = Attention(net, [(h, [(0, S), (1, S)]) for h in range(H16)], net.mask0,
                     lambda h, qt: net.qT[head_rows(h), h // 2, qt * P:(qt + 1) * P],
                     lambda h, nk: net.kT[head_rows(h), h // 2, 0:nk],
                     lambda h, k: net.v[:, k, h * DH:(h + 1) * DH],
                     lambda h, qt: -DH ** -0.5, lambda h, segments: net.qT[:, h // 2, :], att)

    with nc.Block() as block:
        @block.vector
        def _(dve):
            nc.vector.tensor_copy(net.ctxT[:], batch_columns(net, net.ctxT_all)).then_inc(ctxT_ready, 1)
            empty_projections(nc, dve, nc.vector.tensor_copy, net, outs, 8, 1, tile_ready, emptied)
            attn.dve(nc, dve)
            dve.wait_ge(o_ready, 1)
            x = batch_rows(net)
            nc.vector.tensor_tensor(x, x, net.ps[:, 0, 0:S].rearrange("p (t d) -> p t d", d=D), ALU.add)

        @block.scalar
        def _(act):
            nc.scalar.copy(net.zT[:], batch_columns(net, net.zT_all)).then_inc(zT_ready, 1)
            empty_projections(nc, act, nc.scalar.copy, net, outs, 8, 0, tile_ready, emptied)
            attn.act(nc, act)

        @block.tensor
        def _(pe):
            pe.wait_ge(ctxT_ready, 1)
            pe.wait_ge(zT_ready, 1)
            pe.wait_ge(net.w0_loaded, net.w0_count)
            pe_projections(nc, pe, net, tiles, 8, tile_ready, emptied)
            for which in range(2):
                pe.wait_ge(emptied[which], counts[which])
            attn.pe(nc, pe)
            pe_out_projection(nc, pe, net, attn, net.qT, 8, w["o"], o_ready)

        @block.gpsimd
        def _(pool):
            attn.pool(nc, pool)
    net.end_phase()



def local_block(net, l):
    nc = net.nc
    (dve_link, act_link, pool_link, zT_turned, zT_ready, qkv_ready, rows_copied, squares_ready, v_copied, cos_used,
     sin_ready, rotated, qk_turned, qk_act, qk_dve, sin_used, var_ready, seed_ready, o_ready,
     z_ready, shifted, rows_ready, hT_turned, hT_ready, gate_in, gated, hidden_ready, mlp_ready, *att) = net.signals(38)
    w, m = net.wf[l], net.local
    attn = Attention(net, [((b, h), [(0, P), (1, S)]) for b in range(LB) for h in range(H8)], net.band,
                     lambda bh, qt: m["qT"][head_rows(bh[1]), bh[1] // 2, bh[0] * S + qt * P:bh[0] * S + (qt + 1) * P],
                     lambda bh, nk: m["kT"][head_rows(bh[1]), bh[1] // 2, bh[0] * S:bh[0] * S + nk],
                     lambda bh, k: m["v"][:, bh[0] * NT + k, bh[1] * DH:(bh[1] + 1) * DH],
                     lambda bh, qt: net.rnorm[:, bh[0] * NT + qt, bh[1]:bh[1] + 1],
                     lambda bh, segments: m["qT"][:, bh[1] // 2, bh[0] * S:(bh[0] + 1) * S], att)
    half = slice(D // 2, D)

    def rot(x, a, b):
        return x[:, :, :, a:b]

    with nc.Block() as block:
        @block.tensor
        def _(pe):
            for t in range(LT):
                last = nc.tensor.transpose(net.ps[:, 7, t * P:(t + 1) * P], net.z[:, t, :], net.ident[:])
            last.then_inc(zT_turned, 1)
            pe.wait_ge(zT_ready, 3)
            if l == 0:
                pe.wait_ge(net.wf_loaded, net.wf_count)
            for t in range(LT):
                if t >= 2:
                    pe.wait_ge(squares_ready, t - 1)
                    pe.wait_ge(rows_copied, t - 1)
                    pe.wait_ge(v_copied, t - 1)
                for part in range(3):
                    last = nc.tensor.matmul(net.ps[:, 3 * (t % 2) + part, :], m["hT"][:, t * P:(t + 1) * P],
                                            w["qkv"][:, part * BANK:(part + 1) * BANK], start=True, stop=True)
                last.then_inc(qkv_ready, 1)
            for t in range(LT):
                pe.wait_ge(rotated, t + 1)
                if t >= 1:
                    pe.wait_ge(qk_act, t)
                    pe.wait_ge(qk_dve, t)
                for part in range(2):
                    for c in range(4):
                        last = nc.tensor.transpose(net.ps[:, 6 + part, c * P:(c + 1) * P],
                                                   m["rot"][:, t, part * BANK + c * P:part * BANK + (c + 1) * P],
                                                   net.ident[:])
                    last.then_inc(qk_turned, 1)
            pe.wait_ge(qk_act, LT)
            pe.wait_ge(qk_dve, LT)
            pe.wait_ge(v_copied, LT)
            attn.pe(nc, pe)
            pe_out_projection(nc, pe, net, attn, m["qT"], 4, w["o"], o_ready, LT)
            pe.wait_ge(rows_ready, 1)
            for t in range(LT):
                last = nc.tensor.transpose(net.ps[:, 0, t * P:(t + 1) * P], m["hn"][:, t, :], net.ident[:])
            last.then_inc(hT_turned, 1)
            pe.wait_ge(hT_ready, 1)
            for c, (c0, cn) in enumerate(HC):
                for part in range(2):
                    last = nc.tensor.matmul(net.ps[0:cn, 1 + 3 * part + c, :],
                                            w["w1"][:, part * HID + c0:part * HID + c0 + cn], m["hnT"][:],
                                            start=True, stop=True)
                last.then_inc(gate_in, 1)
            for t in range(LT):
                for c, (c0, cn) in enumerate(HC):
                    if t == 0:
                        pe.wait_ge(hidden_ready, c + 1)
                    last = nc.tensor.matmul(net.ps[:, 7, t * P:(t + 1) * P], m["hid"][0:cn, c, t * P:(t + 1) * P],
                                            w["w2"][0:cn, c, :], start=c == 0, stop=c == len(HC) - 1)
            last.then_inc(mlp_ready, 1)

        @block.scalar
        def _(act):
            link = linker(act, act_link)
            act.wait_ge(zT_turned, 1)
            nc.scalar.copy(m["hT"][0:D // 2, :], net.ps[0:D // 2, 7, :]).then_inc(zT_ready, 1)
            for t in range(LT):
                act.wait_ge(qkv_ready, t + 1)
                nc.scalar.copy(m["qk"][:, t, :], net.ps[:, 3 * (t % 2):3 * (t % 2) + 2, :].rearrange("p b n -> p (b n)")).then_inc(rows_copied, 1)
                if t >= 1:
                    act.wait_ge(cos_used, t)
                nc.scalar.activation(m["squares"][:], net.ps[:, 3 * (t % 2):3 * (t % 2) + 2, :].rearrange("p b n -> p (b n)"), ACT.Square).then_inc(squares_ready, 1)
                nc.scalar.copy(m["v"][:, t, 0:BANK], net.ps[:, 3 * (t % 2) + 2, :]).then_inc(v_copied, 1)
            act_rsqrt_seed(nc, act, link, net, LT * 16, var_ready, 1, seed_ready)
            for t in range(LT):
                act.wait_ge(qk_turned, 2 * t + 1)
                nc.scalar.copy(m["qT"][:, 0:4, t * P:(t + 1) * P],
                               net.ps[:, 6, :].rearrange("p (m s) -> p m s", m=4)).then_inc(qk_act, 1)
            attn.act(nc, act)
            act_rsqrt_seed(nc, act, link, net, LT, var_ready, 2, seed_ready)
            act.wait_ge(hT_turned, 1)
            nc.scalar.activation(m["hnT"][:], net.ps[:, 0, :], ACT.Identity, scale=net.col("L0_ln_g", l),
                                 bias=net.col("L0_ln_b", l)).then_inc(hT_ready, 1)
            for c, (c0, cn) in enumerate(HC):
                act.wait_ge(gate_in, c + 1)
                nc.scalar.activation(m["gate"][0:cn, c, :], net.ps[0:cn, 4 + c, :], ACT.Gelu,
                                     bias=net.col("L0_b1", 6 * l + 3 + c)[0:cn]).then_inc(gated, 1)
            nc.scalar.preload_act_table_set(LN_EXP)

        @block.gpsimd
        def _(pool):
            for t in range(LT):
                pool.wait_ge(rows_copied, t + 1)
                if t >= 2:
                    pool.wait_ge(sin_used, t - 1)
                x = m["qk"][:, t, :].rearrange("p (a h d) -> p a h d", a=2, d=DH)
                y = m["sin"][:, t % 2, :].rearrange("p (a h d) -> p a h d", a=2, d=DH)
                sin = net.sin_t[:, l, t % NT, :, :]
                for a, b in ((0, 32), (32, 0)):
                    last = nc.gpsimd.tensor_tensor(rot(y, a, a + 32), rot(x, b, b + 32),
                                                   sin[:, :, a:a + 32].unsqueeze(2).to_broadcast([P, 2, H8, 32]), ALU.mult)
                last.then_inc(sin_ready, 1)
            attn.pool(nc, pool)

        @block.sync
        def _(sp):
            sp.wait_ge(z_ready, 1)
            sp.dma_start(m["hs"][1:P, :, half], net.z[0:P - 1, :, half]).then_inc(shifted, 16)
            for b in range(LB):
                sp.dma_start(m["hs"][0:1, NT * b + 1, half], net.z[P - 1:P, NT * b, half]).then_inc(shifted, 16)
            sp.wait_ge(shifted, 16 * (1 + LB))

        @block.vector
        def _(dve):
            link = linker(dve, dve_link)
            dve.wait_ge(zT_turned, 1)
            by_batch = lambda ap: ap.rearrange("p (b s) -> p b s", b=LB)
            nc.vector.tensor_copy(by_batch(m["hT"][half, :])[:, :, 1:S], by_batch(net.ps[half, 7, :])[:, :, 0:S - 1]).then_inc(zT_ready, 1)
            nc.vector.memset(by_batch(m["hT"][half, :])[:, :, 0:1], 0.0).then_inc(zT_ready, 1)
            for t in range(LT):
                dve.wait_ge(rows_copied, t + 1)
                x = m["qk"][:, t, :].rearrange("p (a h d) -> p a h d", a=2, d=DH)
                y = m["rot"][:, t, :].rearrange("p (a h d) -> p a h d", a=2, d=DH)
                link(nc.vector.tensor_tensor(y, x, net.cos_t[:, l, t % NT, :, :].unsqueeze(2).to_broadcast([P, 2, H8, DH]), ALU.mult))
                dve.wait_ge(squares_ready, t + 1)
                nc.vector.reduce_sum(net.ssq[:, t, :], m["squares"][:].rearrange("p (h d) -> p h d", d=DH), AX.X).then_inc(cos_used, 1)
            dve.wait_ge(cos_used, LT)
            nc.vector.tensor_scalar(net.veps[:, 0:LT * 16], net.ssq[:].rearrange("p t h -> p (t h)"), 1e-24, 2.0 ** 30,
                                    ALU.max, ALU.mult).then_inc(var_ready, 1)
            dve_rsqrt(nc, dve, link, net, LT * 16, seed_ready, 1, net.rnorm[:].rearrange("p t h -> p (t h)"), 2.0 ** 15)
            for t in range(LT):
                dve.wait_ge(sin_ready, t + 1)
                nc.vector.tensor_tensor(m["rot"][:, t, :], m["rot"][:, t, :], m["sin"][:, t % 2, :], ALU.add).then_inc(sin_used, 1)
                dve.wait_ge(sin_used, t + 1)
                k = m["rot"][:, t, BANK:2 * BANK].rearrange("p (h d) -> p h d", d=DH)
                nc.vector.tensor_tensor(k, k, net.rnorm[:, t, H8:16].unsqueeze(2).to_broadcast([P, H8, DH]),
                                        ALU.mult).then_inc(rotated, 1)
            link(nc.vector.tensor_scalar(net.rnorm[:, :, 0:H8], net.rnorm[:, :, 0:H8], -8.0, None, ALU.mult))
            for t in range(LT):
                dve.wait_ge(qk_turned, 2 * t + 2)
                nc.vector.tensor_copy(m["kT"][:, 0:4, t * P:(t + 1) * P],
                                      net.ps[:, 7, :].rearrange("p (m s) -> p m s", m=4)).then_inc(qk_dve, 1)
            attn.dve(nc, dve)
            dve.wait_ge(o_ready, 1)
            nc.vector.tensor_tensor(net.z[:], net.z[:], net.ps[:, 0, :].rearrange("p (t d) -> p t d", d=D), ALU.add).then_inc(z_ready, 1)
            dve.wait_ge(z_ready, 1)
            for b in range(LB):
                nc.vector.memset(m["hs"][0:1, NT * b, half], 0.0)
            link(nc.vector.tensor_copy(m["hs"][:, :, 0:D // 2], net.z[:, :, 0:D // 2]))
            dve.wait_ge(shifted, 16 * (1 + LB))
            dve_stats(nc, link, net, lambda t: m["hs"][:, t, :], LT, 1e-5, var_ready)
            dve_rsqrt(nc, dve, link, net, LT, seed_ready, 2, net.rstd[:, 0:LT])
            dve_normalise(nc, net, lambda t: m["hn"][:, t, :], lambda t: m["hs"][:, t, :], LT).then_inc(rows_ready, 1)
            link(nc.vector.tensor_tensor(net.z[:], net.z[:], net.row("L0_b2", l).unsqueeze(1).to_broadcast([P, LT, D]), ALU.add))
            for c, (c0, cn) in enumerate(HC):
                dve.wait_ge(gated, c + 1)
                nc.vector.scalar_tensor_tensor(m["hid"][0:cn, c, :], net.ps[0:cn, 1 + c, :],
                                               net.col("L0_b1", 6 * l + c)[0:cn], m["gate"][0:cn, c, :],
                                               ALU.add, ALU.mult).then_inc(hidden_ready, 1)
            dve.wait_ge(mlp_ready, 1)
            link(nc.vector.tensor_tensor(net.z[:], net.z[:], net.ps[:, 7, :].rearrange("p (t d) -> p t d", d=D), ALU.add))
            if l == 1:
                x = turn_rows(net)
                nc.vector.tensor_tensor(x, x, net.z[:], ALU.add)
    net.end_phase()


def turn_rows(net):
    return net.x_all[:, bass.ds(net.turn * LT, LT), :]


def norm_turn(net):
    nc = net.nc
    dve_link, act_link, var_ready, seed_ready = net.signals(4)
    with nc.Block() as block:
        @block.vector
        def _(dve):
            link = linker(dve, dve_link)
            link(nc.vector.tensor_copy(net.z[:], turn_rows(net)))
            dve_stats(nc, link, net, rows_of(net.z), LT, 1e-5, var_ready)
            dve_rsqrt(nc, dve, link, net, LT, seed_ready, 1, net.rstd[:, 0:LT])
            dve_normalise(nc, net, rows_of(net.z), rows_of(net.z), LT)

        @block.scalar
        def _(act):
            act_rsqrt_seed(nc, act, linker(act, act_link), net, LT, var_ready, 1, seed_ready)
    net.end_phase()



def dve_norm_rows(nc, dve, link, net, src, out, n, eps, var_ready, seed_ready, k):
    dve_stats(nc, link, net, src, n, eps, var_ready)
    dve_rsqrt(nc, dve, link, net, n, seed_ready, k, net.rstd[:, 0:n])
    return dve_normalise(nc, net, out, src, n)


def spread(ap, n):
    return ap.unsqueeze(2).to_broadcast([P, ap.shape[1], n])


def dve_top2(nc, dve, link, net, logits, ne, probs, exp_in, exp_out, guard, comb):
    r = net.small
    mx, sm, top, idx, idxf = r["mx"][:, 0:T], r["sm"][:, 0:T], r["top"], r["idx"], r["idxf"]
    link(nc.vector.reduce_max(mx, logits, AX.X))
    nc.vector.tensor_tensor(r["e"][:, 0:T, 0:ne], logits, spread(mx, ne), ALU.subtract).then_inc(exp_in, 1)
    dve.wait_ge(exp_out, 1)
    link(nc.vector.reduce_sum(sm, r["e"][:, 0:T, 0:ne], AX.X))
    link(nc.vector.reciprocal(sm, sm))
    link(nc.vector.tensor_tensor(probs[:, 0:T, 0:ne], r["e"][:, 0:T, 0:ne], spread(sm, ne), ALU.mult))
    for t in range(T):
        last = nc.vector.max(top[:, t, :], probs[:, t, :])
    link(last)
    for t in range(T):
        last = nc.vector.max_index(idx[:, t, :], top[:, t, :], probs[:, t, :])
    link(last)
    link(nc.vector.tensor_copy(idxf[:, 0:T, :], idx[:, 0:T, :]))
    link(nc.vector.tensor_tensor(sm, top[:, 0:T, 0], top[:, 0:T, 1], ALU.add))
    link(nc.vector.tensor_scalar(sm, sm, guard[0], None, guard[1]))
    link(nc.vector.reciprocal(sm, sm))
    link(nc.vector.tensor_tensor(r["w2"], top[:, 0:T, 0:2], spread(sm, 2), ALU.mult))
    iota = net.iota[:, 0:ne].unsqueeze(1).to_broadcast([P, T, ne])
    for k in range(2):
        link(nc.vector.tensor_tensor(r["eq"][:, k, :, 0:ne], iota, spread(idxf[:, 0:T, k], ne), ALU.is_equal))
        link(nc.vector.tensor_tensor(r["eq"][:, k, :, 0:ne], r["eq"][:, k, :, 0:ne], spread(r["w2"][:, :, k], ne), ALU.mult))
    link(nc.vector.tensor_tensor(comb, r["eq"][:, 0, :, 0:ne], r["eq"][:, 1, :, 0:ne], ALU.add))


def rows_of(ap):
    return lambda t: ap[:, t, :]



def layer1_attention(net):
    nc = net.nc
    (dve_link, act_link, var_ready, seed_ready, cols_ready, mask_ready, mask_spread, mask_copied, tile_ready,
     act_emptied, dve_emptied, o_ready, *att) = net.signals(22)
    emptied = (act_emptied, dve_emptied)
    w = net.w1
    tiles, outs = [], []
    for m in range(8):
        tiles.append([(0, BANK, w["kv"][:, m * P:(m + 1) * P], net.kv_in[:])])
        outs.append(net.kT[:, m, :])
    for t in range(4):
        for half in range(2):
            tiles.append([(0, BANK, net.kv_in[:, t * P:(t + 1) * P], w["kv"][:, 1024 + half * BANK:1024 + (half + 1) * BANK])])
            outs.append(net.v[:, t, half * BANK:(half + 1) * BANK])
    for m in range(0, 8, 2):
        tiles.append([(i * S, (i + 1) * S, w["q"][:, (m + i) * P:(m + i + 1) * P], net.kv_in[:, S:2 * S]) for i in range(2)])
        outs.append(net.qT[:, m:m + 2, :])
    counts = evac_counts(len(tiles))
    attn = Attention(net, [(h, [(t, 2 * S)]) for t in range(NT) for h in range(H16)], net.kmask_all,
                     lambda h, qt: net.qT[head_rows(h), h // 2, qt * P:(qt + 1) * P],
                     lambda h, nk: net.kT[head_rows(h), h // 2, 0:nk],
                     lambda h, k: net.v[:, k, h * DH:(h + 1) * DH],
                     lambda h, qt: -DH ** -0.5,
                     lambda h, segments: net.qT[:, h // 2, segments[0][0] * P:(segments[0][0] + 1) * P], att)

    with nc.Block() as block:
        @block.tensor
        def _(pe):
            pe.wait_ge(cols_ready, 1)
            pe.wait_ge(net.w1_loaded, net.w1_count)
            pe_projections(nc, pe, net, tiles, 6, tile_ready, emptied)
            for which in range(2):
                pe.wait_ge(emptied[which], counts[which])
            pe.wait_ge(mask_ready, 1)
            nc.tensor.matmul(net.ps[:, 7, :], net.ones_b[0:1, :], net.kmask[:], start=True, stop=True).then_inc(mask_spread, 1)
            attn.pe(nc, pe)
            pe_out_projection(nc, pe, net, attn, net.qT, 8, w["o"], o_ready)

        @block.gpsimd
        def _(pool):
            attn.pool(nc, pool)

        @block.scalar
        def _(act):
            link = linker(act, act_link)
            nc.scalar.copy(net.kv_in[:], batch_columns(net, net.kv_all)).then_inc(cols_ready, 1)
            empty_projections(nc, act, nc.scalar.copy, net, outs, 6, 0, tile_ready, emptied)
            act.wait_ge(mask_spread, 1)
            nc.scalar.copy(net.kmask_all[:], net.ps[:, 7, :]).then_inc(mask_copied, 1)
            attn.act(nc, act)
            act_rsqrt_seed(nc, act, link, net, NT, var_ready, 1, seed_ready)

        @block.vector
        def _(dve):
            link = linker(dve, dve_link)
            nc.vector.tensor_copy(net.kmask[0:1, 0:S], batch_columns(net, net.kmask_f)).then_inc(mask_ready, 1)
            empty_projections(nc, dve, nc.vector.tensor_copy, net, outs, 6, 1, tile_ready, emptied)
            dve.wait_ge(mask_copied, 1)
            attn.dve(nc, dve)
            dve.wait_ge(o_ready, 1)
            out = net.ps[:, 0, 0:S].rearrange("p (t d) -> p t d", d=D)
            hn, x = net.o_rows, batch_rows(net)
            link(dve_norm_rows(nc, dve, link, net, rows_of(out), rows_of(hn), NT, 1e-5, var_ready, seed_ready, 1))
            both_rows = lambda name: net.row(name, 0).unsqueeze(1).to_broadcast([P, NT, D])
            link(nc.vector.tensor_tensor(hn[:], hn[:], both_rows("L1_g_o"), ALU.mult))
            link(nc.vector.tensor_tensor(hn[:], hn[:], both_rows("L1_b_o"), ALU.add))
            nc.vector.tensor_tensor(x, x, hn[:], ALU.add)
    net.end_phase()



def pe_turn_rows(nc, net, src, banks, turned):
    for j, bank in enumerate(banks):
        for t in range(BANK // P):
            last = nc.tensor.transpose(net.ps[:, bank, t * P:(t + 1) * P], src[:, j * (BANK // P) + t, :], net.ident[:])
        last.then_inc(turned, 1)


def prepare_layer1(net):
    nc = net.nc
    dve_link, act_link, loaded, var_ready, seed_ready, rows_ready, turned = net.signals(7)
    m = net.prep1
    zr, hn, cn = m["z"], m["hn"], m["cn"]

    with nc.Block() as block:
        @block.sync
        def _(sp):
            sp.dma_start(net.ctx_all[:], net.d["ctx"].rearrange("b (t p) d -> p (b t) d", p=P)).then_inc(loaded, 16)
            sp.dma_start(m["kmask"], net.d["kmask"].rearrange("b k -> (b k)").unsqueeze(0)).then_inc(loaded, 16)
            sp.wait_ge(loaded, 32)

        @block.tensor
        def _(pe):
            pe.wait_ge(rows_ready, 1)
            pe_turn_rows(nc, net, hn, (0, 1), turned)
            pe.wait_ge(rows_ready, 2)
            pe_turn_rows(nc, net, cn, (2, 3), turned)

        @block.scalar
        def _(act):
            link = linker(act, act_link)
            for k in range(3):
                act_rsqrt_seed(nc, act, link, net, T, var_ready, k + 1, seed_ready)
            for k, name in enumerate(("l", "x", )):
                for j in range(2):
                    act.wait_ge(turned, 2 * k + j + 1)
                    dst = net.kv_all[:, 2 * j:2 * j + 2, (1 - k) * S:(2 - k) * S]
                    nc.scalar.activation(dst, net.ps[:, 2 * k + j, :].rearrange("p (b s) -> p b s", b=2), ACT.Identity,
                                         scale=net.col("L1_g_" + name, 0), bias=net.col("L1_b_" + name, 0))

        @block.vector
        def _(dve):
            link = linker(dve, dve_link)
            link(dve_norm_rows(nc, dve, link, net, rows_of(net.x_all), rows_of(zr), T, 1e-5, var_ready, seed_ready, 1))
            dve_norm_rows(nc, dve, link, net, rows_of(zr), rows_of(hn), T, 1e-5, var_ready, seed_ready, 2).then_inc(rows_ready, 1)
            dve.wait_ge(rows_ready, 1)
            dve.wait_ge(loaded, 32)
            dve_norm_rows(nc, dve, link, net, rows_of(net.ctx_all), rows_of(cn), T, 1e-5, var_ready, seed_ready, 3).then_inc(rows_ready, 1)
            nc.vector.tensor_scalar(net.kmask_f[:].rearrange("p b s -> p (b s)"), m["kmask"].bitcast(U8), -MASKED, MASKED, ALU.mult, ALU.add)
    net.end_phase()



def layer1_experts(net):
    nc = net.nc
    (dve_link, act_link, var_ready, seed_ready, rows_ready, turned, zT_ready, logits_ready, exp_in, exp_out,
     fc_ready, relu_ready, hid_ready, proj_ready, added, loaded) = net.signals(16)
    m = net.late
    z, zT, relu, hid = m["z"], m["zT"], m["relu"], m["hid"]
    comb = net.comb[:, :, 0:NE1]
    halves = T * P // BANK
    groups = [(e, j) for e in [NE1] + list(range(NE1)) for j in range(halves)]
    G = len(groups)

    with nc.Block() as block:
        @block.sync
        def _(sp):
            sp.dma_start(m["ids_i"], net.d["ids"].rearrange("b s -> (b s)").unsqueeze(0)).then_inc(loaded, 16)
            sp.dma_start(net.ptr_i[:].rearrange("p (b t) -> p b t", b=B), net.d["ptr"].rearrange("b p t -> p b t")).then_inc(loaded, 16)

        @block.tensor
        def _(pe):
            pe.wait_ge(rows_ready, 1)
            pe_turn_rows(nc, net, z, (6, 7), turned)
            pe.wait_ge(zT_ready, halves)
            pe.wait_ge(net.w1f_loaded, net.w1f_count)
            for t in range(T):
                last = nc.tensor.matmul(net.ps[:, 6, t * NE1:(t + 1) * NE1], zT[:, t * P:(t + 1) * P], net.router1[:],
                                        start=True, stop=True)
            last.then_inc(logits_ready, 1)
            for g in range(G + 1):
                if g < G:
                    e, j = groups[g]
                    for c in range(4):
                        i = 4 * g + c
                        if i >= 4:
                            pe.wait_ge(hid_ready, i - 3)
                        nc.tensor.matmul(net.ps[:, c, :], net.fc[:, e, c * P:(c + 1) * P], zT[:, j * BANK:(j + 1) * BANK],
                                         start=True, stop=True).then_inc(fc_ready, 1)
                if g >= 1:
                    v = g - 1
                    e = groups[v][0]
                    pe.wait_ge(hid_ready, 4 * (v + 1))
                    if v >= 2:
                        pe.wait_ge(added, v - 1)
                    for t in range(4):
                        for c in range(4):
                            last = nc.tensor.matmul(net.ps[:, 4 + v % 2, t * P:(t + 1) * P], hid[:, v % 2, c, t * P:(t + 1) * P],
                                                    net.proj[:, e, c, :], start=c == 0, stop=c == 3)
                    last.then_inc(proj_ready, 1)

        @block.scalar
        def _(act):
            link = linker(act, act_link)
            act_rsqrt_seed(nc, act, link, net, T, var_ready, 1, seed_ready)
            for j in range(halves):
                act.wait_ge(turned, j + 1)
                nc.scalar.copy(zT[:, j * BANK:(j + 1) * BANK], net.ps[:, 6 + j, :]).then_inc(zT_ready, 1)
            for i in range(4 * G):
                if i == 8:
                    act.wait_ge(exp_in, 1)
                    e2 = net.small["e"][:, :, 0:NE1]
                    nc.scalar.activation(e2, e2, ACT.Exp).then_inc(exp_out, 1)
                act.wait_ge(fc_ready, i + 1)
                if i >= 4:
                    act.wait_ge(hid_ready, i - 3)
                nc.scalar.activation(relu[:, i % 4, :], net.ps[:, i % 4, :], ACT.Relu).then_inc(relu_ready, 1)

        @block.vector
        def _(dve):
            link = linker(dve, dve_link)
            dve_norm_rows(nc, dve, link, net, rows_of(net.x_all), rows_of(z), T, 1e-5, var_ready, seed_ready, 1).then_inc(rows_ready, 1)
            for g in range(G + 1):
                if g == 2:
                    dve.wait_ge(logits_ready, 1)
                    dve_top2(nc, dve, link, net, net.ps[:, 6, 0:T * NE1].rearrange("p (t e) -> p t e", t=T), NE1, net.small["p8"],
                             exp_in, exp_out, (1e-9, ALU.max), comb)
                if g < G:
                    if g >= 2:
                        dve.wait_ge(proj_ready, g - 1)
                    for c in range(4):
                        dve.wait_ge(relu_ready, 4 * g + c + 1)
                        nc.vector.scalar_tensor_tensor(hid[:, g % 2, c, :], net.ps[:, c, :], 0.0, relu[:, c, :],
                                                       ALU.max, ALU.mult).then_inc(hid_ready, 1)
                if g >= 1:
                    v = g - 1
                    e, j = groups[v]
                    dve.wait_ge(proj_ready, v + 1)
                    if v >= 2:
                        dve.wait_ge(added, v - 1)
                    out = net.ps[:, 4 + v % 2, :].rearrange("p (t d) -> p t d", d=D)
                    x = net.x_all[:, 4 * j:4 * j + 4, :]
                    if e < NE1:
                        for t in range(4):
                            last = nc.vector.scalar_tensor_tensor(x[:, t, :], out[:, t, :], comb[:, 4 * j + t, e:e + 1],
                                                                  x[:, t, :], ALU.mult, ALU.add)
                    else:
                        last = nc.vector.tensor_tensor(x, out, x, ALU.add)
                    last.then_inc(added, 1)
            dve.wait_ge(loaded, 32)
            nc.vector.tensor_copy(m["ids_f"], m["ids_i"])
    net.end_phase()



def layer2_attention(net):
    nc = net.nc
    (dve_link, act_link, var_ready, seed_ready, rows_ready, turned, zT_ready, proj_ready, act_emptied, dve_emptied, ids_bc,
     ptr_ready, hot_ready, scores_ready, scores_read, exp_in, exp_out, mixed, mix_turned, mix_copied, mean_ready, mean_copied,
     out_ready) = net.signals(23)
    w, m = net.w2x, net.late
    emptied = (act_emptied, dve_emptied)
    z, zT, q, k, v, hot, junk, mix, mixT, meanT = (m[n] for n in ("z", "zT", "q", "k", "v", "hot", "junk", "mix", "mixT", "meanT"))
    ctxT = net.ctxT_all[:].rearrange("p b s -> p (b s)")
    s6, r = net.s6, net.small
    JUNK = junk.shape[1]
    halves = T * P // BANK
    tiles, outs = [], []
    for a in range(2):
        for j in range(halves):
            tiles.append([(0, BANK, w["k"][:, a, :], ctxT[:, j * BANK:(j + 1) * BANK])])
            outs.append(k[:, a, j * BANK:(j + 1) * BANK])
    for t in range(0, T, 2):
        tiles.append([(i * S, (i + 1) * S, ctxT[:, (t + i) * P:(t + i + 1) * P], w["v"][:]) for i in range(2)])
        outs.append(v[:, t:t + 2, :].rearrange("p t n -> p (t n)"))
    n_ctx = len(tiles)
    for a in range(2):
        for j in range(halves):
            tiles.append([(0, BANK, w["q"][:, a, :], zT[:, j * BANK:(j + 1) * BANK])])
            outs.append(q[:, a, j * BANK:(j + 1) * BANK])
    counts = evac_counts(len(tiles))
    scores = [(b, a) for b in range(B) for a in range(2)]

    def pe_mean(pe, b):
        pe.wait_ge(mix_copied, 2 * b + 2)
        for a in range(2):
            for l in range(NT):
                last = nc.tensor.matmul(net.ps[:, 4 + b // 2, (b % 2) * S:(b % 2 + 1) * S], v[:, b * NT + l, a * P:(a + 1) * P],
                                        mixT[:, 2 * b + a, l * S:(l + 1) * S], start=a == 0 and l == 0, stop=a == 1 and l == NT - 1)
        last.then_inc(mean_ready, 1)

    def copy_mean(act, j):
        act.wait_ge(mean_ready, 2 * j + 2)
        nc.scalar.copy(meanT[:, j * BANK:(j + 1) * BANK], net.ps[:, 4 + j, :]).then_inc(mean_copied, 1)

    with nc.Block() as block:
        @block.sync
        def _(sp):
            d, wi, wo = net.d, net.fc, net.proj
            sp.dma_start(wi[:, NE3, :], d["res_in"]).then_inc(net.w3_res, 16)
            sp.dma_start(wo[:, NE3, :, :], d["res_out"]).then_inc(net.w3_res, 16)
            sp.dma_start(wi[:, 0:NE3, :], d["inter"]).then_inc(net.w3_experts, 16)
            sp.dma_start(wo[:, 0:NE3, :, :], d["output"]).then_inc(net.w3_experts, 16)

        @block.tensor
        def _(pe):
            pe.wait_ge(net.w2_loaded, net.w2_count)
            for j in range(halves):
                nc.tensor.matmul(net.ps[:, 6 + j, :], net.ones[0:1, :], m["ids_f"][:, j * BANK:(j + 1) * BANK],
                                 start=True, stop=True).then_inc(ids_bc, 1)
            for i, products in enumerate(tiles):
                if i == n_ctx:
                    pe.wait_ge(rows_ready, 1)
                    pe_turn_rows(nc, net, z, (4, 5), turned)
                    pe.wait_ge(zT_ready, halves)
                if i >= 4:
                    pe.wait_ge(emptied[i % 2], (i - 4) // 2 + 1)
                for a, b, stationary, moving in products:
                    last = nc.tensor.matmul(net.ps[:, i % 4, a:b], stationary, moving, start=True, stop=True)
                last.then_inc(proj_ready, 1)
            for which in range(2):
                pe.wait_ge(emptied[which], counts[which])
            for i, (b, a) in enumerate(scores):
                if i >= 4:
                    pe.wait_ge(scores_read, i - 3)
                for t in range(NT):
                    c = b * S + t * P
                    last = nc.tensor.matmul(net.ps[:, i % 4, t * S:(t + 1) * S], q[:, a, c:c + P],
                                            k[:, a, b * S:(b + 1) * S], start=True, stop=True)
                last.then_inc(scores_ready, 1)
            for i, (b, a) in enumerate(scores):
                pe.wait_ge(mixed, i + 1)
                if i >= 4:
                    pe.wait_ge(mix_copied, i - 3)
                for l in range(NT):
                    for t in range(NT):
                        last = nc.tensor.transpose(net.ps[:, i % 4, (l * NT + t) * P:(l * NT + t + 1) * P],
                                                   mix[:, i, t, l * P:(l + 1) * P], net.ident[:])
                last.then_inc(mix_turned, 1)
                if a == 1 and b >= 1:
                    pe_mean(pe, b - 1)
            pe_mean(pe, B - 1)
            for j in range(halves):
                pe.wait_ge(mean_copied, j + 1)
                for t in range(4 * j, 4 * j + 4):
                    last = nc.tensor.matmul(net.ps[:, 6 + j, (t % 4) * P:(t % 4 + 1) * P], meanT[:, t * P:(t + 1) * P], w["o"][:],
                                            start=True, stop=True)
                last.then_inc(out_ready, 1)

        @block.gpsimd
        def _(pool):
            pool.wait_ge(ptr_ready, 1)
            for t in range(T):
                for k_ in range(3):
                    last = nc.gpsimd.tensor_scalar(hot[:, k_, t, :], net.iota[:, 0:S], r["ptr"][:, k_, t:t + 1], None, ALU.is_equal)
                last.then_inc(hot_ready, 1)

        @block.scalar
        def _(act):
            link = linker(act, act_link)
            act_rsqrt_seed(nc, act, link, net, T, var_ready, 1, seed_ready)
            empty_projections(nc, act, nc.scalar.copy, net, outs[:n_ctx], 4, 0, proj_ready, emptied)
            for j in range(halves):
                act.wait_ge(turned, j + 1)
                nc.scalar.copy(zT[:, j * BANK:(j + 1) * BANK], net.ps[:, 4 + j, :]).then_inc(zT_ready, 1)
            for i in range(n_ctx, len(outs), 2):
                act.wait_ge(proj_ready, i + 1)
                nc.scalar.copy(outs[i], net.ps[:, i % 4, :]).then_inc(emptied[0], 1)
            act.wait_ge(exp_in, 1)
            nc.scalar.activation(s6[:], s6[:], ACT.Exp).then_inc(exp_out, 1)
            for i in range(len(scores)):
                act.wait_ge(mix_turned, i + 1)
                nc.scalar.copy(mixT[:, i, :], net.ps[:, i % 4, :]).then_inc(mix_copied, 1)
                if i % 4 == 3 and i >= 7:
                    copy_mean(act, i // 4 - 1)
            copy_mean(act, halves - 1)

        @block.vector
        def _(dve):
            link = linker(dve, dve_link)
            link(nc.vector.tensor_copy(r["ptr"][:, 3, :], net.ptr_i[:]))
            for w_ in range(3):
                last = nc.vector.tensor_scalar(r["ptr"][:, w_, :], r["ptr"][:, 3, :], float(w_), 0.0, ALU.add, ALU.max)
            link(last)
            nc.vector.tensor_scalar(r["ptr"][:, 0:3, :], r["ptr"][:, 0:3, :], float(S - 1), None, ALU.min).then_inc(ptr_ready, 1)
            dve_norm_rows(nc, dve, link, net, rows_of(net.x_all), rows_of(z), T, 1e-5, var_ready, seed_ready, 1).then_inc(rows_ready, 1)
            empty_projections(nc, dve, nc.vector.tensor_copy, net, outs, 4, 1, proj_ready, emptied)
            used = 0
            dve.wait_ge(ids_bc, halves)
            for t in range(T):
                dve.wait_ge(hot_ready, t + 1)
                last = nc.vector.scalar_tensor_tensor(junk[:, t, :], net.ps[:, 6 + t // 4, (t // NT % 2) * S:(t // NT % 2 + 1) * S], 1.0,
                                                      hot[:, 0, t, :], ALU.mult, ALU.mult, accum_out=r["rel"][:, t:t + 1])
            link(last)
            for i, (b, a) in enumerate(scores):
                dve.wait_ge(scores_ready, i + 1)
                if i >= 2:
                    dve.wait_ge(scores_read, i - 1)
                for t in range(NT):
                    for k_ in range(3):
                        last = nc.vector.scalar_tensor_tensor(junk[:, 6 * (i % 2) + 3 * t + k_, :], net.ps[:, i % 4, t * S:(t + 1) * S],
                                                              D ** -0.5, hot[:, k_, b * NT + t, :], ALU.mult, ALU.mult,
                                                              accum_out=s6[:, a, b * NT + t, k_:k_ + 1])
                last.then_inc(scores_read, 1)
            dve.wait_ge(scores_read, len(scores))
            v1, v2, val, eq = s6[:, 0, :, 1], s6[:, 0, :, 2], r["val"], r["is"]
            nc.vector.tensor_tensor(val[:, 0, :], v1, v2, ALU.add)
            nc.vector.tensor_tensor(val[:, 1, :], v1, v2, ALU.max)
            nc.vector.tensor_tensor(val[:, 4, :], v1, v2, ALU.subtract)
            for k_ in range(5):
                nc.vector.tensor_scalar(eq[:, k_, :], r["rel"][:], float(k_), None, ALU.is_equal)
            link(nc.vector.tensor_scalar(val[:, 2, :], v1, -1.0, None, ALU.mult))
            nc.vector.tensor_tensor(val[:, 3, :], val[:, 2, :], v2, ALU.max)
            link(nc.vector.tensor_scalar(val[:, 5, :], val[:, 4, :], -1.0, None, ALU.mult))
            link(nc.vector.tensor_tensor(val[:, 4, :], val[:, 4, :], val[:, 5, :], ALU.max))
            link(nc.vector.tensor_tensor(val[:, 0:5, :], val[:, 0:5, :], eq[:], ALU.mult))
            nc.vector.reduce_sum(r["new"][:], val[:, 0:5, :].rearrange("p k t -> p t k"), AX.X)
            link(nc.vector.reduce_sum(r["any"][:], eq[:].rearrange("p k t -> p t k"), AX.X))
            link(nc.vector.tensor_scalar(r["any"][:], r["any"][:], -1.0, 1.0, ALU.mult, ALU.add))
            link(nc.vector.tensor_tensor(r["any"][:], r["any"][:], s6[:, 0, :, 0], ALU.mult))
            link(nc.vector.tensor_tensor(s6[:, 0, :, 0], r["any"][:], r["new"][:], ALU.add))
            flat = s6[:].rearrange("p a t w -> p (a t) w")
            mx, sm = r["mx"][:, 0:2 * T], r["sm"][:, 0:2 * T]
            link(nc.vector.reduce_max(mx, flat, AX.X))
            nc.vector.tensor_tensor(flat, flat, spread(mx, 3), ALU.subtract).then_inc(exp_in, 1)
            dve.wait_ge(exp_out, 1)
            link(nc.vector.reduce_sum(sm, flat, AX.X))
            link(nc.vector.reciprocal(sm, sm))
            by_path = sm.rearrange("p (a t) -> p a t", a=2)
            link(nc.vector.tensor_tensor(by_path, by_path, spread(net.share[:], T), ALU.mult))
            link(nc.vector.tensor_tensor(flat, flat, spread(sm, 3), ALU.mult))
            for i, (b, a) in enumerate(scores):
                for t in range(NT):
                    bt = b * NT + t
                    last = nc.vector.tensor_scalar(mix[:, i, t, :], hot[:, 0, bt, :], s6[:, a, bt, 0:1], None, ALU.mult)
                link(last)
                for k_ in (1, 2):
                    for t in range(NT):
                        bt = b * NT + t
                        last = nc.vector.scalar_tensor_tensor(mix[:, i, t, :], hot[:, k_, bt, :], s6[:, a, bt, k_:k_ + 1],
                                                              mix[:, i, t, :], ALU.mult, ALU.add)
                    if k_ == 1:
                        link(last)
                last.then_inc(mixed, 1)
            for j in range(halves):
                dve.wait_ge(out_ready, j + 1)
                x = net.x_all[:, 4 * j:4 * j + 4, :]
                nc.vector.scalar_tensor_tensor(x, net.ps[:, 6 + j, :].rearrange("p (t d) -> p t d", d=D), net.row("gain", 0, 1),
                                               x, ALU.mult, ALU.add)
    net.end_phase()



def layer2_experts(net):
    nc = net.nc
    (dve_link, act_link, var_ready, seed_ready, rows_ready, turned, cols_ready, logits_ready, exp_in, exp_out,
     hid_in, act_hid_copied, dve_hid_copied, rstd_ready, dve_normed, pool_normed, hid_turned, hid_ready, out_ready, summed) = net.signals(20)
    m = net.late
    z, hn, zT, hnT, hid, hidT, sums = (m[n] for n in ("z", "hn", "zT", "hnT", "hid_rows", "hidT", "sums"))
    hid_copied = (act_hid_copied, dve_hid_copied)
    comb = net.comb[:, :, 0:NE2]
    halves = T * P // BANK
    cut = lambda t, e: hid[:, t, e * H2:(e + 1) * H2]
    jobs = [(j, c) for j in range(halves) for c in range(2 * NE2)]

    with nc.Block() as block:
        @block.tensor
        def _(pe):
            pe.wait_ge(rows_ready, 1)
            pe_turn_rows(nc, net, z, (6, 7), turned)
            pe.wait_ge(cols_ready, halves)
            for t in range(T):
                if t >= 3:
                    for which in range(2):
                        pe.wait_ge(hid_copied[which], t - 2)
                for half in range(2):
                    nc.tensor.matmul(net.ps[:, 2 * (t % 3) + half, :], zT[:, t * P:(t + 1) * P],
                                     net.w2f["in"][:, half * BANK:(half + 1) * BANK], start=True, stop=True).then_inc(hid_in, 1)
            pe.wait_ge(rows_ready, 2)
            pe_turn_rows(nc, net, hn, (6, 7), turned)
            pe.wait_ge(cols_ready, 2 * halves)
            for t in range(T):
                last = nc.tensor.matmul(net.ps[:, 6, t * NE2:(t + 1) * NE2], hnT[:, t * P:(t + 1) * P], net.router2[:],
                                        start=True, stop=True)
            last.then_inc(logits_ready, 1)
            for which in range(2):
                pe.wait_ge(hid_copied[which], T)
            for i in range(len(jobs) + 4):
                if i < len(jobs):
                    j, c = jobs[i]
                    if i >= 3:
                        pe.wait_ge(hid_ready, i - 2)
                    for t in range(4 * j, 4 * j + 4):
                        if t % 2 == 0:
                            pe.wait_ge((dve_normed, pool_normed)[c // 2 % 2], (t * NE2 // 2 + c // 4) + NE2 // 2 + 1)
                        last = nc.tensor.transpose(net.ps[:, i % 3, (t % 4) * P:(t % 4 + 1) * P], hid[:, t, c * P:(c + 1) * P], net.ident[:])
                    last.then_inc(hid_turned, 1)
                if i >= 4 and i % 2 == 1:
                    n = (i - 4) // 2
                    j, e = divmod(n, NE2)
                    pe.wait_ge(hid_ready, 2 * n + 2)
                    if n >= 3:
                        pe.wait_ge(summed, n - 2)
                    for t in range(4):
                        for c in range(2):
                            last = nc.tensor.matmul(net.ps[:, 3 + n % 3, t * P:(t + 1) * P],
                                                    hidT[:, 2 * e + c, (4 * j + t) * P:(4 * j + t + 1) * P],
                                                    net.w2f["out"][:, 2 * e + c, :], start=c == 0, stop=c == 1)
                    last.then_inc(out_ready, 1)

        @block.scalar
        def _(act):
            link = linker(act, act_link)
            act_rsqrt_seed(nc, act, link, net, T, var_ready, 1, seed_ready)
            for j in range(halves):
                act.wait_ge(turned, j + 1)
                nc.scalar.copy(zT[:, j * BANK:(j + 1) * BANK], net.ps[:, 6 + j, :]).then_inc(cols_ready, 1)
            act_rsqrt_seed(nc, act, link, net, T, var_ready, 2, seed_ready)
            for t in range(T):
                act.wait_ge(hid_in, 2 * t + 1)
                nc.scalar.copy(hid[:, t, 0:BANK], net.ps[:, 2 * (t % 3), :]).then_inc(hid_copied[0], 1)
            for j in range(halves):
                act.wait_ge(turned, halves + j + 1)
                nc.scalar.activation(hnT[:, j * BANK:(j + 1) * BANK], net.ps[:, 6 + j, :], ACT.Identity, scale=net.col("L2_rn_g", 0),
                                     bias=net.col("L2_rn_b", 0)).then_inc(cols_ready, 1)
            act_rsqrt_seed(nc, act, link, net, T * NE2, var_ready, 3, seed_ready)
            act.wait_ge(exp_in, 1)
            e2 = net.small["e"][:, :, 0:NE2]
            nc.scalar.activation(e2, e2, ACT.Exp).then_inc(exp_out, 1)
            for i, (j, c) in enumerate(jobs):
                act.wait_ge(hid_turned, i + 1)
                nc.scalar.activation(hidT[:, c, j * BANK:(j + 1) * BANK], net.ps[:, i % 3, :], ACT.Relu,
                                     scale=net.col("L2_ln_g", c), bias=net.col("L2_ln_b", c)).then_inc(hid_ready, 1)
            act_rsqrt_seed(nc, act, link, net, T, var_ready, 4, seed_ready)

        @block.gpsimd
        def _(pool):
            pool.wait_ge(rstd_ready, 1)
            for t in range(T):
                for e in (1, 3):
                    i = t * NE2 + e
                    nc.gpsimd.tensor_scalar(cut(t, e), cut(t, e), net.mv[:, i, 0:1], net.rstd[:, i:i + 1],
                                            ALU.subtract, ALU.mult).then_inc(pool_normed, 1)

        @block.vector
        def _(dve):
            link = linker(dve, dve_link)
            dve_norm_rows(nc, dve, link, net, rows_of(net.x_all), rows_of(z), T, 1e-5, var_ready, seed_ready, 1).then_inc(rows_ready, 1)
            dve.wait_ge(rows_ready, 1)
            dve_norm_rows(nc, dve, link, net, rows_of(z), rows_of(hn), T, 1e-5, var_ready, seed_ready, 2).then_inc(rows_ready, 1)
            dve.wait_ge(rows_ready, 2)
            for t in range(T):
                dve.wait_ge(hid_in, 2 * t + 2)
                link(nc.vector.tensor_copy(hid[:, t, BANK:2 * BANK], net.ps[:, 2 * (t % 3) + 1, :]))
                dve.sem_inc(hid_copied[1], 1)
                dve.wait_ge(hid_copied[0], t + 1)
                for e in range(NE2):
                    last = nc.vector.bn_stats(net.stats[:, t * NE2 + e, :], cut(t, e))
            link(last)
            for i in range(T * NE2):
                last = nc.vector.bn_aggr(net.mv[:, i, :], net.stats[:, i, :])
            link(last)
            nc.vector.tensor_scalar(net.veps[:, 0:T * NE2], net.mv[:, 0:T * NE2, 1], 1e-5, None, ALU.add).then_inc(var_ready, 1)
            dve_rsqrt(nc, dve, link, net, T * NE2, seed_ready, 3, net.rstd[:])
            dve.sem_inc(rstd_ready, 1)
            for t in range(T):
                for e in (0, 2):
                    i = t * NE2 + e
                    nc.vector.tensor_scalar(cut(t, e), cut(t, e), net.mv[:, i, 0:1], net.rstd[:, i:i + 1],
                                            ALU.subtract, ALU.mult).then_inc(dve_normed, 1)
            dve.wait_ge(logits_ready, 1)
            dve_top2(nc, dve, link, net, net.ps[:, 6, 0:T * NE2].rearrange("p (t e) -> p t e", t=T), NE2, net.small["p4"],
                     exp_in, exp_out, (1e-8, ALU.add), comb)
            for n in range(halves * NE2):
                j, e = divmod(n, NE2)
                dve.wait_ge(out_ready, n + 1)
                for t in range(4 * j, 4 * j + 4):
                    src = net.ps[:, 3 + n % 3, (t % 4) * P:(t % 4 + 1) * P]
                    if e == 0:
                        last = nc.vector.tensor_scalar(sums[:, t, :], src, comb[:, t, e:e + 1], None, ALU.mult)
                    else:
                        last = nc.vector.scalar_tensor_tensor(sums[:, t, :], src, comb[:, t, e:e + 1], sums[:, t, :], ALU.mult, ALU.add)
                last.then_inc(summed, 1)
                dve.wait_ge(summed, n + 1)
            link(dve_norm_rows(nc, dve, link, net, rows_of(sums), rows_of(hn), T, 1e-5, var_ready, seed_ready, 4))
            every = lambda name: net.row(name, 0).unsqueeze(1).to_broadcast([P, T, D])
            link(nc.vector.tensor_tensor(hn[:], hn[:], every("L2_on_g"), ALU.mult))
            link(nc.vector.tensor_tensor(hn[:], hn[:], every("L2_on_b"), ALU.add))
            nc.vector.tensor_tensor(net.x_all[:], net.x_all[:], hn[:], ALU.add)
    net.end_phase()



def layer3_attention(net):
    nc = net.nc
    (dve_link, act_link, var_ready, seed_ready, rows_ready, turned, zT_ready, scores_ready, masked, exped, normed, probs_turned,
     probs_copied, out_ready) = net.signals(14)
    keys = [P, S]
    cols = [0, P]
    blocks = [(0, 0), (1, 0), (1, 1)]
    m = net.late
    z, zT, probs, probsT = m["z"], m["zT"], m["probs3"], m["probsT3"]
    units = [(b, t) for b in range(B) for t in range(NT)]
    halves = T * P // BANK

    with nc.Block() as block:
        @block.sync
        def _(sp):
            d = net.d
            sp.dma_start(net.before, d["before"]).then_inc(net.w3_gate, 16)
            sp.dma_start(net.gate_w, d["gate"]).then_inc(net.w3_gate, 16)
            sp.dma_start(net.w2f["in"][:], d["iota"]).then_inc(net.w3_gate, 16)

        @block.tensor
        def _(pe):
            pe.wait_ge(rows_ready, 1)
            pe_turn_rows(nc, net, z, (6, 7), turned)
            for u, (b, t) in enumerate(units):
                if u % 4 == 0:
                    pe.wait_ge(zT_ready, u // 4 + 1)
                nc.tensor.matmul(net.ps[:, b, cols[t]:cols[t] + keys[t]], zT[:, u * P:(u + 1) * P], net.ctxT_all[:, b, 0:keys[t]],
                                 start=True, stop=True).then_inc(scores_ready, 1)
            for b in range(B):
                for j, (t, k) in enumerate(blocks):
                    pe.wait_ge(normed, b * NT + t + 1)
                    last = nc.tensor.transpose(net.ps[:, 4 + b, j * P:(j + 1) * P],
                                               probs[:, b, cols[t] + k * P:cols[t] + (k + 1) * P], net.ident[:])
                last.then_inc(probs_turned, 1)
            pe.wait_ge(masked, T)
            for b in range(B):
                pe.wait_ge(probs_copied, b + 1)
                for j, (t, k) in enumerate(blocks):
                    last = nc.tensor.matmul(net.ps[:, b // 2, ((b % 2) * NT + t) * P:((b % 2) * NT + t + 1) * P],
                                            probsT[:, b, j * P:(j + 1) * P], net.ctx_all[:, b * NT + k, :], start=k == 0, stop=k == t)
                if b % 2 == 1:
                    last.then_inc(out_ready, 1)

        @block.scalar
        def _(act):
            act_rsqrt_seed(nc, act, linker(act, act_link), net, T, var_ready, 1, seed_ready)
            for j in range(halves):
                act.wait_ge(turned, j + 1)
                nc.scalar.copy(zT[:, j * BANK:(j + 1) * BANK], net.ps[:, 6 + j, :]).then_inc(zT_ready, 1)
            for u, (b, t) in enumerate(units):
                act.wait_ge(masked, u + 1)
                x = probs[:, b, cols[t]:cols[t] + keys[t]]
                nc.scalar.activation(x, x, ACT.Exp, bias=net.negmax[:, b, t:t + 1], scale=-1.0,
                                     accum_out=net.sums[:, b, t:t + 1]).then_inc(exped, 1)
            for b in range(B):
                act.wait_ge(probs_turned, b + 1)
                nc.scalar.copy(probsT[:, b, :], net.ps[:, 4 + b, 0:3 * P]).then_inc(probs_copied, 1)

        @block.vector
        def _(dve):
            link = linker(dve, dve_link)
            dve_norm_rows(nc, dve, link, net, rows_of(net.x_all), rows_of(z), T, 1e-5, var_ready, seed_ready, 1).then_inc(rows_ready, 1)
            for step in range(T + 2):
                if step < T:
                    b, t = units[step]
                    dve.wait_ge(scores_ready, NT * (b + 1))
                    c = slice(cols[t], cols[t] + keys[t])
                    nc.vector.tensor_tensor_reduce(out=probs[:, b, c], in0=net.ps[:, b, c], in1=net.causal[:, c],
                                                   scale=-D ** -0.5, scalar=-MASKED, op0=ALU.add, op1=ALU.min,
                                                   accum_out=net.negmax[:, b, t:t + 1]).then_inc(masked, 1)
                if step >= 2:
                    b, t = units[step - 2]
                    dve.wait_ge(exped, step - 1)
                    x = probs[:, b, cols[t]:cols[t] + keys[t]]
                    link(nc.vector.reciprocal(net.recip[:, b, t:t + 1], net.sums[:, b, t:t + 1]))
                    nc.vector.tensor_scalar(x, x, net.recip[:, b, t:t + 1], None, ALU.mult).then_inc(normed, 1)
            for j in range(halves):
                dve.wait_ge(out_ready, j + 1)
                x = net.x_all[:, 4 * j:4 * j + 4, :]
                nc.vector.tensor_tensor(x, x, net.ps[:, j, :].rearrange("p (t d) -> p t d", d=D), ALU.add)
    net.end_phase()



def layer3_experts(net, out):
    nc = net.nc
    (dve_link, act_link, pool_link, var_ready, seed_ready, rows_ready, turned, cols_ready, logits_ready, exp_in, exp_out,
     mask_ready, places_ready, slots_ready, diag_ready, spread_ready, spread_copied, hot_ready, take_ready, res_in, res_gelu,
     sent, sent_copied, inter_ready, inter_gelu, expert_ready, expert_copied, mixed, final, written) = net.signals(30)
    w_res, w_gate, w_experts = net.w3_res, net.w3_gate, net.w3_experts
    at, start = {}, 0
    for name, n in dict(hot=T * NE3 * CAP, take=NE3 * T * P, a=T * D, aT=T * P, z=T * D, res=4 * T * P, sent=NE3 * CAP,
                        eo=NE3 * D, inter=2 * 4 * CAP, slots=T * P, diag=T * P).items():
        at[name] = net.arena[:, start:start + n]
        start += n
    rows = lambda name: at[name].rearrange("p (t d) -> p t d", t=T)
    a_rows, z_rows, eo = rows("a"), rows("z"), rows("eo")
    hot = at["hot"].rearrange("p (t n) -> p t n", t=T)
    take = at["take"].rearrange("p (e s) -> p e s", e=NE3)
    res = at["res"].rearrange("p (c s) -> p c s", c=4)
    inter = at["inter"].rearrange("p (a c s) -> p a c s", a=2, c=4)
    diag = rows("diag")
    wi, wo = net.fc, net.proj
    iota, before, gate_w = net.w2f["in"], net.before, net.gate_w
    r = net.small
    HALF = T * P // BANK

    with nc.Block() as block:
        @block.sync
        def _(sp):
            for t in range(T):
                sp.wait_ge(final, t + 1)
                sp.dma_start(out[t // NT, (t % NT) * P:(t % NT + 1) * P, :], net.x_all[:, t, :]).then_inc(written, 16)
            sp.wait_ge(written, 16 * T)

        @block.tensor
        def _(pe):
            pe.wait_ge(rows_ready, 1)
            for j in range(HALF):
                for t in range(4):
                    last = nc.tensor.transpose(net.ps[:, j, t * P:(t + 1) * P], a_rows[:, 4 * j + t, :], net.ident[:])
                last.then_inc(turned, 1)
            pe.wait_ge(cols_ready, HALF)
            pe.wait_ge(w_gate, 48)
            for t in range(T):
                last = nc.tensor.matmul(net.ps[:, 2, t * 10:(t + 1) * 10], at["aT"][:, t * P:(t + 1) * P], gate_w, start=True, stop=True)
            last.then_inc(logits_ready, 1)
            pe.wait_ge(w_res, 32)
            for i in range(4 * HALF):
                c, j = divmod(i, HALF)
                if i >= 4:
                    pe.wait_ge(res_gelu, i - 3)
                nc.tensor.matmul(net.ps[:, 4 + i % 4, :], wi[:, NE3, c * P:(c + 1) * P], at["aT"][:, j * BANK:(j + 1) * BANK],
                                 start=True, stop=True).then_inc(res_in, 1)
            pe.wait_ge(mask_ready, 1)
            mask = r["mask"]
            flat = net.ps[:, 3, 0:T * NE3]
            nc.tensor.matmul(flat, before, mask[:].rearrange("p t e -> p (t e)"), start=True, stop=False)
            for t in range(T - 1):
                last = nc.tensor.matmul(net.ps[:, 3, (t + 1) * NE3:T * NE3].rearrange("p (t e) -> p t e", e=NE3), net.ones[:],
                                        mask[:, t, :].unsqueeze(1).to_broadcast([P, T - 1 - t, NE3]), start=False, stop=t == T - 2)
            last.then_inc(places_ready, 1)
            pe.wait_ge(diag_ready, 1)
            for j in range(HALF):
                nc.tensor.matmul(net.ps[:, j, :], net.ones[:], at["diag"][:, j * BANK:(j + 1) * BANK], start=True, stop=True).then_inc(spread_ready, 1)
            pe.wait_ge(res_gelu, 4 * HALF)
            for t in range(T):
                pe.wait_ge(hot_ready, t + 1)
                for j in range(2):
                    last = nc.tensor.matmul(net.ps[:, 4 + j, :], a_rows[:, t, :], hot[:, t, j * BANK:(j + 1) * BANK],
                                            start=t == 0, stop=t == T - 1)
            last.then_inc(sent, 1)
            pe.wait_ge(sent_copied, 2)
            pe.wait_ge(w_experts, 32)
            for e in range(NE3 + 1):
                if e < NE3:
                    if e >= 2:
                        pe.wait_ge(inter_gelu, 4 * (e - 1))
                    for c in range(4):
                        last = nc.tensor.matmul(net.ps[:, 6 + e % 2, c * CAP:(c + 1) * CAP], wi[:, e, c * P:(c + 1) * P],
                                                at["sent"][:, e * CAP:(e + 1) * CAP], start=True, stop=True)
                    last.then_inc(inter_ready, 1)
                if e >= 1:
                    v = e - 1
                    pe.wait_ge(inter_gelu, 4 * (v + 1))
                    if v >= 2:
                        pe.wait_ge(expert_copied, v - 1)
                    for c in range(4):
                        last = nc.tensor.matmul(net.ps[:, 4 + v % 2, 0:D], inter[:, v % 2, c, :], wo[:, v, c, :], start=c == 0, stop=c == 3)
                    last.then_inc(expert_ready, 1)
            pe.wait_ge(expert_copied, NE3)
            pe.wait_ge(take_ready, NE3)
            for t in range(T):
                if t >= 4:
                    pe.wait_ge(final, t - 3)
                bank = t % 4
                for e in range(NE3):
                    nc.tensor.matmul(net.ps[:, bank, 0:D], take[:, e, t * P:(t + 1) * P], eo[:, e, :], start=e == 0, stop=e == NE3 - 1)
                for c in range(4):
                    last = nc.tensor.matmul(net.ps[:, bank, D:2 * D], res[:, c, t * P:(t + 1) * P], wo[:, NE3, c, :],
                                            start=c == 0, stop=c == 3)
                last.then_inc(mixed, 1)

        @block.scalar
        def _(act):
            link = linker(act, act_link)
            act_rsqrt_seed(nc, act, link, net, T, var_ready, 1, seed_ready)
            act_rsqrt_seed(nc, act, link, net, T, var_ready, 2, seed_ready)
            for j in range(HALF):
                act.wait_ge(turned, j + 1)
                nc.scalar.copy(at["aT"][:, j * BANK:(j + 1) * BANK], net.ps[:, j, :]).then_inc(cols_ready, 1)
            act.wait_ge(exp_in, 1)
            nc.scalar.activation(r["e"][:], r["e"][:], ACT.Exp).then_inc(exp_out, 1)
            for i in range(4 * HALF):
                c, j = divmod(i, HALF)
                act.wait_ge(res_in, i + 1)
                nc.scalar.activation(res[:, c, j * BANK:(j + 1) * BANK], net.ps[:, 4 + i % 4, :], ACT.Gelu_apprx_tanh,
                                     bias=net.col("L3_rb", c)).then_inc(res_gelu, 1)
            for j in range(HALF):
                act.wait_ge(spread_ready, j + 1)
                nc.scalar.copy(at["slots"][:, j * BANK:(j + 1) * BANK], net.ps[:, j, :]).then_inc(spread_copied, 1)
            act.wait_ge(sent, 1)
            for j in range(2):
                nc.scalar.copy(at["sent"][:, j * BANK:(j + 1) * BANK], net.ps[:, 4 + j, :]).then_inc(sent_copied, 1)
            for e in range(NE3):
                act.wait_ge(inter_ready, e + 1)
                if e >= 2:
                    act.wait_ge(expert_ready, e - 1)
                for c in range(4):
                    nc.scalar.activation(inter[:, e % 2, c, :], net.ps[:, 6 + e % 2, c * CAP:(c + 1) * CAP], ACT.Gelu_apprx_tanh,
                                         bias=net.col("L3_b", 4 * e + c)).then_inc(inter_gelu, 1)

        @block.gpsimd
        def _(pool):
            pool.wait_ge(spread_copied, HALF)
            for e in range(NE3):
                nc.gpsimd.tensor_scalar(take[:, e, :], at["slots"], net.col("L3_slot", e), None, ALU.is_equal).then_inc(take_ready, 1)

        @block.vector
        def _(dve):
            link = linker(dve, dve_link)
            dve.wait_ge(w_gate, 48)
            link(dve_norm_rows(nc, dve, link, net, rows_of(net.x_all), rows_of(z_rows), T, 1e-5, var_ready, seed_ready, 1))
            link(dve_norm_rows(nc, dve, link, net, rows_of(z_rows), rows_of(a_rows), T, 1e-12, var_ready, seed_ready, 2))
            every = lambda name: net.row(name, 0).unsqueeze(1).to_broadcast([P, T, D])
            link(nc.vector.tensor_tensor(a_rows, a_rows, every("L3_nw"), ALU.mult))
            nc.vector.tensor_tensor(a_rows, a_rows, every("L3_nb"), ALU.add).then_inc(rows_ready, 1)
            link(nc.vector.tensor_tensor(net.x_all[:], net.x_all[:], z_rows, ALU.add))
            dve.wait_ge(logits_ready, 1)
            logits = net.ps[:, 2, 0:T * 10].rearrange("p (t e) -> p t e", t=T)
            sm, mx, e10, top, idx, idxf = r["sm"], r["mx"], r["e"], r["top"], r["idx"], r["idxf"]
            parts = ((slice(0, NE3), slice(0, T)), (slice(NE3, NE3 + 2), slice(T, 2 * T)))
            for e, m in parts:
                last = nc.vector.reduce_max(mx[:, m], logits[:, :, e], AX.X)
            link(last)
            for e, m in parts:
                last = nc.vector.tensor_tensor(e10[:, :, e], logits[:, :, e], spread(mx[:, m], e.stop - e.start), ALU.subtract)
            last.then_inc(exp_in, 1)
            dve.wait_ge(exp_out, 1)
            for e, m in parts:
                last = nc.vector.reduce_sum(sm[:, m], e10[:, :, e], AX.X)
            link(last)
            link(nc.vector.reciprocal(sm[:], sm[:]))
            link(nc.vector.tensor_tensor(e10[:, :, 8:10], e10[:, :, 8:10], spread(sm[:, T:2 * T], 2), ALU.mult))
            link(nc.vector.tensor_tensor(r["p8"][:], e10[:, :, 0:NE3], spread(sm[:, 0:T], NE3), ALU.mult))
            for t in range(T):
                last = nc.vector.max(top[:, t, :], r["p8"][:, t, :])
            link(last)
            for t in range(T):
                last = nc.vector.max_index(idx[:, t, :], top[:, t, :], r["p8"][:, t, :])
            link(last)
            link(nc.vector.tensor_copy(idxf[:, :, 0:1], idx[:, :, 0:1]))
            nc.vector.tensor_tensor(r["mask"][:], net.iota[:, 0:NE3].unsqueeze(1).to_broadcast([P, T, NE3]), spread(idxf[:, :, 0], NE3),
                                    ALU.is_equal).then_inc(mask_ready, 1)
            dve.wait_ge(places_ready, 1)
            link(nc.vector.tensor_tensor(r["place"][:], net.ps[:, 3, 0:T * NE3].rearrange("p (t e) -> p t e", t=T), r["mask"][:], ALU.mult))
            loc, slot = mx[:, 0:T], mx[:, T:2 * T]
            link(nc.vector.reduce_sum(loc, r["place"][:], AX.X))
            link(nc.vector.scalar_tensor_tensor(slot, idxf[:, :, 0], float(CAP), loc, ALU.mult, ALU.add))
            link(nc.vector.tensor_scalar(loc, loc, float(CAP), None, ALU.is_lt))
            link(nc.vector.tensor_scalar(slot, slot, 1.0, None, ALU.add))
            link(nc.vector.tensor_tensor(slot, slot, loc, ALU.mult))
            link(nc.vector.tensor_scalar(slot, slot, -1.0, None, ALU.add))
            for t in range(T):
                last = nc.vector.tensor_scalar(diag[:, t, :], net.ident[:], slot[:, t:t + 1], None, ALU.mult)
            last.then_inc(diag_ready, 1)
            for t in range(T):
                nc.vector.tensor_scalar(hot[:, t, :], iota[:], slot[:, t:t + 1], None, ALU.is_equal).then_inc(hot_ready, 1)
            link(nc.vector.tensor_tensor(r["p8"][:, :, 0], top[:, :, 0], e10[:, :, 9], ALU.mult))
            for e in range(NE3):
                dve.wait_ge(expert_ready, e + 1)
                nc.vector.tensor_tensor(eo[:, e, :], net.ps[:, 4 + e % 2, 0:D], net.row("L3_ob", e), ALU.add).then_inc(expert_copied, 1)
            for t in range(T):
                dve.wait_ge(mixed, t + 1)
                tmp, bank = diag[:, t, :], net.ps[:, t % 4, :]
                link(nc.vector.tensor_tensor(tmp, bank[:, D:2 * D], net.row("L3_rob", 0), ALU.add))
                link(nc.vector.scalar_tensor_tensor(net.x_all[:, t, :], tmp, e10[:, t, 8:9], net.x_all[:, t, :], ALU.mult, ALU.add))
                nc.vector.scalar_tensor_tensor(net.x_all[:, t, :], bank[:, 0:D], r["p8"][:, t, 0:1], net.x_all[:, t, :],
                                               ALU.mult, ALU.add).then_inc(final, 1)
    net.end_phase()


def start(net):
    nc, d, m = net.nc, net.d, net.first
    dve_link, act_link, loaded, var_ready, seed_ready, rows_ready, turned = net.signals(7)
    halves = T * P // BANK
    with nc.Block() as block:
        @block.sync
        def _(sp):
            sp.dma_start(net.x_all[:], d["x"].rearrange("b (t p) d -> p (b t) d", p=P)).then_inc(loaded, 16)
            sp.dma_start(net.ident[:], d["ident"]).then_inc(loaded, 16)
            sp.dma_start(m["mask0_w"].rearrange("p (t k) -> p t k", t=NT), d["mask0"].rearrange("(t p) k -> p t k", p=P)).then_inc(loaded, 16)
            sp.dma_start(net.ctxT_all[:], d["ctxT"].rearrange("b d s -> d b s")).then_inc(loaded, 16)
            for name in "kvq":
                sp.dma_start(net.w0[name][:], d["L0_xattn_w_" + name]).then_inc(net.w0_loaded, 16)
            sp.dma_start(net.w0["o"][:], d["L0_xattn_w_o"].rearrange("(c p) n -> p c n", p=P)).then_inc(net.w0_loaded, 16)
            for dst, name in ((m["band"], "band"), (m["causal"], "causal")):
                sp.dma_start(dst.rearrange("p (t k) -> p t k", t=NT), d[name].rearrange("(t p) k -> p t k", p=P)).then_inc(net.tables_loaded, 16)
            sp.dma_start(net.iota[:], d["iota"][:, 0:S]).then_inc(net.tables_loaded, 16)
            sp.dma_start(net.cols[:], d["cols"]).then_inc(net.tables_loaded, 16)
            sp.dma_start(net.rows[:], d["rows"]).then_inc(net.tables_loaded, 16)
            for table, name in ((net.cos_t, "cos"), (net.sin_t, "sin")):
                for l in range(2):
                    sp.dma_start(table[:, l, :, :, :], d[name]).then_inc(net.tables_loaded, 16)
            for l in range(2):
                sp.dma_start(net.wf[l]["qkv"][:], d["L0_ffn_wqkv"][l, :, :]).then_inc(net.wf_loaded, 16)
                sp.dma_start(net.wf[l]["o"][:], d["L0_ffn_wo"][l, :, :].rearrange("(c p) n -> p c n", p=P)).then_inc(net.wf_loaded, 16)
                sp.dma_start(net.wf[l]["w1"][:], d["L0_ffn_w1"][l, :, :]).then_inc(net.wf_loaded, 16)
                for c, (c0, cn) in enumerate(HC):
                    sp.dma_start(net.wf[l]["w2"][0:cn, c, :], d["L0_ffn_w2"][l, c0:c0 + cn, :]).then_inc(net.wf_loaded, 16)
            sp.dma_start(net.w1["q"], d["L1_xattn_Wq"]).then_inc(net.w1_loaded, 16)
            sp.dma_start(net.w1["kv"], d["L1_xattn_Wkv"]).then_inc(net.w1_loaded, 16)
            sp.dma_start(net.w1["o"], d["L1_xattn_Wout"].rearrange("(c p) n -> p c n", p=P)).then_inc(net.w1_loaded, 16)
            sp.dma_start(net.fc[:], d["fc"]).then_inc(net.w1f_loaded, 16)
            sp.dma_start(net.proj[:], d["proj"]).then_inc(net.w1f_loaded, 16)
            sp.dma_start(net.router1[:], d["router1"]).then_inc(net.w1f_loaded, 16)
            for name, tile in (("w2q", net.w2x["q"]), ("w2k", net.w2x["k"]), ("w2v", net.w2x["v"]), ("w2o", net.w2x["o"]),
                               ("router2", net.router2), ("w2in", net.w2f["in"]), ("w2out", net.w2f["out"])):
                sp.dma_start(tile[:], d[name]).then_inc(net.w2_loaded, 16)

        @block.tensor
        def _(pe):
            pe.wait_ge(rows_ready, 1)
            pe_turn_rows(nc, net, m["z"], (0, 1), turned)

        @block.scalar
        def _(act):
            nc.scalar.preload_act_table_set(LN_EXP)
            act_rsqrt_seed(nc, act, linker(act, act_link), net, T, var_ready, 1, seed_ready)
            for j in range(halves):
                act.wait_ge(turned, j + 1)
                nc.scalar.copy(net.zT_all[:, 2 * j:2 * j + 2, :].rearrange("p b s -> p (b s)"), net.ps[:, j, :])

        @block.vector
        def _(dve):
            link = linker(dve, dve_link)
            nc.vector.memset(net.ones[:], 1.0)
            nc.vector.memset(net.ones_b[:], 1.0)
            nc.vector.memset(net.small["p4"][:], -1.0)
            nc.vector.memset(net.kmask[:], 0.0)
            dve.wait_ge(loaded, 64)
            dve_norm_rows(nc, dve, link, net, rows_of(net.x_all), rows_of(m["z"]), T, 1e-5, var_ready, seed_ready, 1).then_inc(rows_ready, 1)
            nc.vector.tensor_scalar(net.mask0[:], m["mask0_w"].bitcast(U8), MASKED, None, ALU.mult)
    net.end_phase()


def prepare_tables(net):
    nc, m = net.nc, net.first
    table_link, shares_in, shares_out = net.signals(3)
    with nc.Block() as block:
        @block.scalar
        def _(act):
            act.wait_ge(shares_in, 1)
            nc.scalar.activation(net.share[:], net.share[:], ACT.Exp).then_inc(shares_out, 1)

        @block.vector
        def _(dve):
            link = linker(dve, table_link)
            dve.wait_ge(net.tables_loaded, net.tables_count)
            link(nc.vector.reduce_max(net.recip[:, 0, 0:1], net.row("council", 0, 2), AX.X))
            nc.vector.tensor_scalar(net.share[:], net.row("council", 0, 2), net.recip[:, 0, 0:1], None, ALU.subtract).then_inc(shares_in, 1)
            for mask, src in ((net.causal, m["causal"]), (net.band, m["band"])):
                nc.vector.tensor_scalar(mask[:, 0:P], src[:, 0:P], MASKED, None, ALU.mult)
                nc.vector.tensor_scalar(mask[:, P:P + S], src[:, S:2 * S], MASKED, None, ALU.mult)
            for l in range(2):
                for a, name in enumerate(("q_scale", "k_scale")):
                    row = net.row(name, l, DH).unsqueeze(1).to_broadcast([P, NT, DH])
                    cos, sin = net.cos_t[:, l, :, a, :], net.sin_t[:, l, :, a, :]
                    nc.vector.tensor_tensor(cos, cos, row, ALU.mult)
                    nc.vector.tensor_tensor(sin[:, :, 0:32], sin[:, :, 0:32], row[:, :, 32:64], ALU.mult)
                    nc.vector.tensor_tensor(sin[:, :, 32:64], sin[:, :, 32:64], row[:, :, 0:32], ALU.mult)
            dve.wait_ge(shares_out, 1)
            link(nc.vector.reduce_sum(net.recip[:, 1, 0:1], net.share[:], AX.X))
            link(nc.vector.reciprocal(net.recip[:, 2, 0:1], net.recip[:, 1, 0:1]))
            nc.vector.tensor_scalar(net.share[:], net.share[:], net.recip[:, 2, 0:1], None, ALU.mult)
    net.end_phase()


def carve(region, sizes):
    at, start = {}, 0
    for name, size in sizes.items():
        assert start + size <= region.shape[1], (name, start + size, region.shape[1])
        at[name] = region[:, start:start + size]
        start += size
    return at


def program(nc, d, out):
    es = ExitStack()
    with es:
        net = Net(nc, es)
        net.d = d
        sb, sem = net.sb, net.sem
        weights = dict(wf_qkv0=1536, wf_o0=512, wf_10=2 * HID, wf_20=384, wf_qkv1=1536, wf_o1=512, wf_11=2 * HID, wf_21=384,
                       w1q=1024, w1kv=2048, w1o=1024)
        W0, WORK = 4096, 8 * S + 16 * S + 4096 + 8 * BANK
        n_weights = sum(weights.values())
        arena = sb("arena", [P, n_weights + W0 + WORK])
        net.arena = arena
        at = carve(arena[:, 0:n_weights], weights)
        cut = lambda ap, c: ap.rearrange("p (c n) -> p c n", c=c)
        net.wf = [dict(qkv=at[f"wf_qkv{l}"], o=cut(at[f"wf_o{l}"], 4), w1=at[f"wf_1{l}"], w2=cut(at[f"wf_2{l}"], 3)) for l in range(2)]
        net.w1 = dict(q=at["w1q"], kv=at["w1kv"], o=cut(at["w1o"], 8))
        w0_region, work = arena[:, n_weights:n_weights + W0], arena[:, n_weights + W0:n_weights + W0 + WORK]
        w0 = carve(w0_region, dict(q=1024, k=1024, v=1024, o=1024))
        net.w0 = dict(q=w0["q"], k=w0["k"], v=w0["v"], o=cut(w0["o"], 8))
        att = carve(work, dict(probs=4 * BANK, probsT=4 * BANK, qT=8 * S, kT=16 * S, v=4096))
        net.qT, net.kT, net.v = cut(att["qT"], 8), cut(att["kT"], 8), cut(att["v"], 4)
        net.probs, net.probsT = cut(att["probs"], 4), cut(att["probsT"], 4)
        first = carve(att["v"][:, 2048:4096], dict(zT=T * P, band=NT * S, causal=NT * S))
        net.zT_all = cut(first["zT"], B)
        net.first = dict(z=cut(att["probs"][:, 0:T * D], T), band=first["band"], causal=first["causal"],
                         mask0_w=att["probsT"][:, 0:NT * S // 4].bitcast(I32))
        behind = carve(w0_region, dict(ctx=T * D, kv=B * 2 * S, kmask=B * S))
        net.ctx_all, net.kv_all, net.kmask_f = cut(behind["ctx"], T), cut(behind["kv"], B), cut(behind["kmask"], B)[0:1]
        norms = carve(att["kT"], dict(z=T * D, hn=T * D, cn=T * D))
        net.prep1 = dict(kmask=att["qT"][0:1, 0:B * S // 4].bitcast(I32), **{n: cut(ap, T) for n, ap in norms.items()})
        net.o_rows = cut(att["probs"][:, 0:NT * D], NT)
        local = carve(w0_region, dict(kT=4 * LB * S, v=LT * BANK))
        mlp = carve(att["kT"], dict(hs=LT * D, hn=LT * D, hnT=LT * P))
        net.local = dict(qT=cut(att["qT"], 4), kT=cut(local["kT"], 4), v=cut(local["v"], LT), qk=cut(att["kT"], LT), rot=cut(att["v"], LT),
                         sin=cut(att["probs"], 2), squares=att["probsT"][:, 0:2 * BANK], hT=att["probsT"][:, 2 * BANK:3 * BANK],
                         hs=cut(mlp["hs"], LT), hn=cut(mlp["hn"], LT), hnT=mlp["hnT"],
                         gate=cut(att["probsT"][:, 0:3 * LT * P], 3), hid=cut(att["probs"][:, 0:3 * LT * P], 3))
        front, back = arena[:, 0:n_weights], arena[:, n_weights + T * D:n_weights + W0 + WORK]
        l1 = carve(back, dict(z=T * D, zT=T * P, relu=4 * BANK, hid=8 * BANK))
        l2_front = carve(front, dict(ids_i=B * S, ids_f=B * S, mix=8 * BANK, mixT=8 * BANK))
        l2_back = carve(back, dict(z=T * D, zT=T * P, q=2 * T * P, k=2 * T * P, v=T * 2 * D, hot=3 * T * S, junk=12 * S))
        f2 = carve(back, dict(z=T * D, zT=T * P, hn=T * D, hnT=T * P, sums=T * D, hidT=8 * T * P))
        l3 = carve(front, dict(probs=B * 3 * P, probsT=B * 3 * P))
        net.late = dict(z=cut(l1["z"], T), zT=l1["zT"], relu=cut(l1["relu"], 4), hid=l1["hid"].rearrange("p (a m s) -> p a m s", a=2, m=4),
                        ids_i=l2_front["ids_i"][0:1].bitcast(I32), ids_f=l2_front["ids_f"][0:1],
                        mix=l2_front["mix"].rearrange("p (a t l) -> p a t l", a=8, t=NT), mixT=cut(l2_front["mixT"], 8),
                        q=cut(l2_back["q"], 2), k=cut(l2_back["k"], 2), v=cut(l2_back["v"], T), junk=cut(l2_back["junk"], 12),
                        hot=l2_back["hot"].rearrange("p (w t l) -> p w t l", w=3, t=T), meanT=l2_back["z"],
                        hn=cut(f2["hn"], T), hnT=f2["hnT"], sums=cut(f2["sums"], T), hidT=cut(f2["hidT"], 8),
                        hid_rows=cut(front[:, 0:T * NE2 * H2], T), probs3=cut(l3["probs"], B), probsT3=cut(l3["probsT"], B))
        net.fc, net.proj = sb("fc", [P, NE1 + 1, FF]), sb("proj", [P, NE1 + 1, 4, D])
        net.router1, net.router2 = sb("router1", [P, NE1]), sb("router2", [P, NE2])
        net.w2x = dict(q=sb("w2q", [P, 2, D]), k=sb("w2k", [P, 2, D]), v=sb("w2v", [P, 2 * D]), o=sb("w2o", [P, D]))
        net.w2f = dict([("in", sb("w2in", [P, NE2 * H2])), ("out", sb("w2out", [P, 2 * NE2, D]))])
        net.before, net.gate_w = net.w2f["out"][:, 0, :], net.w2f["out"][:, 1, 0:NE3 + 2]
        net.cols, net.rows = sb("cols", [P, d["cols"].shape[1]]), sb("rows", [P, d["rows"].shape[1]])
        net.col = lambda name, i: net.cols[:, COLS[name] + i:COLS[name] + i + 1]
        net.row = lambda name, i, n=D: net.rows[:, ROWS[name] + i * n:ROWS[name] + (i + 1) * n]
        net.band, net.causal, net.mask0 = (sb(n, [P, NT * S], BF16) for n in ("band", "causal", "mask0"))
        net.cos_t, net.sin_t = sb("cos_t", [P, 2, NT, 2, DH]), sb("sin_t", [P, 2, NT, 2, DH])
        net.ones, net.ones_b, net.iota = sb("ones", [P, P]), sb("ones_b", [P, P], BF16), sb("iota", [P, S])
        net.share, net.ident = sb("share", [P, 2]), sb("ident", [P, P])
        net.x_all, net.ctxT_all, net.z = sb("x_all", [P, T, D]), sb("ctxT_all", [P, B, S]), sb("z", [P, LT, D])
        net.kv_in, net.ptr_i = sb("kv_in", [P, 2 * S]), sb("ptr_i", [P, T], I32)
        net.ctxT, net.zT = net.kv_in[:, 0:S], net.kv_in[:, S:2 * S]
        net.kmask, net.kmask_all = sb("kmask", [1, 2 * S], BF16), sb("kmask_all", [P, 2 * S], BF16)
        net.stats, net.mv = sb("stats", [P, 32, 6]), sb("mv", [P, 32, 2])
        net.veps, net.lnv, net.seed, net.nwt = (sb(n, [P, LT * 16]) for n in ("veps", "lnv", "seed", "nwt"))
        net.rstd = sb("rstd", [P, 32])
        net.negmax, net.sums, net.recip = (sb(n, [P, 4, 2]) for n in ("negmax", "sums", "recip"))
        net.ssq, net.rnorm = sb("ssq", [P, LT, 16]), sb("rnorm", [P, LT, 16])
        net.s6, net.comb = sb("s6", [P, 2, T, 3]), sb("comb", [P, T, 8])
        net.small = dict(mx=sb("r_mx", [P, 16]), sm=sb("r_sm", [P, 16]), top=sb("r_top", [P, 8, 8]), idx=sb("r_idx", [P, 8, 8], U32),
                         idxf=sb("r_idxf", [P, 8, 8]), e=sb("r_e", [P, 8, 10]), p8=sb("r_p8", [P, 8, 8]), p4=sb("r_p4", [P, T, 8]),
                         w2=sb("r_w2", [P, T, 2])[:], eq=sb("r_eq", [P, 2, T, 8]), ptr=sb("r_ptr", [P, 4, T]), rel=sb("r_rel", [P, T]),
                         val=sb("r_val", [P, 6, T]), new=sb("r_new", [P, T]), any=sb("r_any", [P, T]), mask=sb("r_mask", [P, 8, 8]),
                         place=sb("r_place", [P, 8, 8]), **{"is": sb("r_is", [P, 5, T])})
        net.ps = es.enter_context(nc.psum_tensor("ps", [P, 8, BANK], F32))

        net.w0_loaded, net.w0_count = sem("w0_loaded"), 16 * 4
        net.tables_loaded, net.tables_count = sem("tables_loaded"), 16 * 9
        net.wf_loaded, net.wf_count = sem("wf_loaded"), 16 * 12
        net.w1_loaded, net.w1_count = sem("w1_loaded"), 16 * 3
        net.w1f_loaded, net.w1f_count = sem("w1f_loaded"), 16 * 3
        net.w2_loaded, net.w2_count = sem("w2_loaded"), 16 * 7
        net.w3_res, net.w3_gate, net.w3_experts = sem("w3_res"), sem("w3_gate"), sem("w3_experts")

        start(net)
        with nc.Fori(0, B) as batch:
            net.batch = batch
            layer0_attention(net)
        prepare_tables(net)
        with nc.Fori(0, B // LB) as turn:
            net.turn = turn
            norm_turn(net)
            for l in range(2):
                local_block(net, l)
        prepare_layer1(net)
        with nc.Fori(0, B) as batch:
            net.batch = batch
            layer1_attention(net)
        layer1_experts(net)
        layer2_attention(net)
        layer2_experts(net)
        layer3_attention(net)
        layer3_experts(net, out)


def rotary_tables():
    half = np.arange(0, DH, 2, dtype=np.float32)
    t = np.arange(S, dtype=np.float32)
    angle = t[:, None] * (1.0 / 10000.0 ** (half / DH)).astype(np.float32)[None, :]
    base = (half + 0.4 * DH) / (1.4 * DH)
    scale = base[None, :] ** ((t - S // 2) / 32.0)[:, None]
    scale = np.concatenate([scale, scale], -1)
    cos = np.concatenate([np.cos(angle), np.cos(angle)], -1)
    sin = np.concatenate([-np.sin(angle), np.sin(angle)], -1)
    return [np.ascontiguousarray(np.stack([m * scale, m / scale], 1).reshape(NT, P, 2, DH).transpose(1, 0, 2, 3), dtype=np.float32)
            for m in (cos, sin)]


COLS = dict(L0_ln_g=0, L0_ln_b=2, L0_b1=4, L1_g_x=16, L1_b_x=17, L1_g_l=18, L1_b_l=19, L2_rn_g=20, L2_rn_b=21,
            L2_ln_g=22, L2_ln_b=30, L3_b=38, L3_rb=70, L3_slot=74, end=82)
ROWS = dict(q_scale=0, k_scale=128, L0_b2=256, L1_g_o=512, L1_b_o=640, L2_on_g=768, L2_on_b=896, council=1024, gain=1026,
            L3_nw=1028, L3_nb=1156, L3_ob=1284, L3_rob=1284 + 1024, end=1284 + 1152)


def packed_columns(a):
    cols = np.zeros((P, COLS["end"]), np.float32)
    for l in range(2):
        cols[:, COLS["L0_ln_g"] + l] = a["L0_ffn_ln_g"][l]
        cols[:, COLS["L0_ln_b"] + l] = a["L0_ffn_ln_b"][l]
        for part in range(2):
            for c, (c0, cn) in enumerate(HC):
                cols[0:cn, COLS["L0_b1"] + 6 * l + 3 * part + c] = a["L0_ffn_b1"][l, part * HID + c0:part * HID + c0 + cn]
    cols[:, COLS["L3_slot"]:COLS["end"]] = np.arange(P)[:, None] + CAP * np.arange(NE3)[None, :]
    for name, src in (("L1_g_x", "L1_xattn_g_x"), ("L1_b_x", "L1_xattn_b_x"), ("L1_g_l", "L1_xattn_g_l"), ("L1_b_l", "L1_xattn_b_l"),
                      ("L2_rn_g", "L2_ffn_rn_g"), ("L2_rn_b", "L2_ffn_rn_b"), ("L2_ln_g", "L2_ffn_ln_g"), ("L2_ln_b", "L2_ffn_ln_b"),
                      ("L3_b", "L3_ffn_inter_b"), ("L3_rb", "L3_ffn_res_inter_b")):
        n = a[src].size // P
        cols[:, COLS[name]:COLS[name] + n] = a[src].reshape(n, P).T
    return cols


def packed_rows(a):
    row = np.zeros(ROWS["end"], np.float32)
    for name, src in (("q_scale", "L0_ffn_q_scale"), ("k_scale", "L0_ffn_k_scale"), ("L0_b2", "L0_ffn_b2"), ("L1_g_o", "L1_xattn_g_o"),
                      ("L1_b_o", "L1_xattn_b_o"), ("L2_on_g", "L2_ffn_on_g"), ("L2_on_b", "L2_ffn_on_b"),
                      ("council", "L2_xattn_council_weights"), ("gain", "L2_xattn_gain"), ("L3_nw", "L3_ffn_attn_nw"),
                      ("L3_nb", "L3_ffn_attn_nb"), ("L3_ob", "L3_ffn_output_b"), ("L3_rob", "L3_ffn_res_output_b")):
        row[ROWS[name]:ROWS[name] + a[src].size] = a[src].reshape(-1)
    return np.ascontiguousarray(np.broadcast_to(row, (P, row.size)))


def laid_out(inputs):
    a = {k: np.asarray(v) for k, v in inputs.items()}
    c = np.ascontiguousarray
    cos, sin = rotary_tables()
    far = np.arange(S)[:, None] - np.arange(S)[None, :]
    return {
        "x": a["x"], "ctx": a["ctx_1024"], "ctxT": c(a["ctx_1024"].transpose(0, 2, 1)),
        "ids": a["itok_BxS_0_7"], "ptr": c(a["itok_BxS_0_4092"].reshape(B, NT, P).transpose(0, 2, 1)),
        "mask0": c(a["mask_1x1xSxS2_bk1"].reshape(S, S)).view(np.int32), "kmask": c(a["mask_BxS2_bf1"]).view(np.int32),
        **{k: a[k] for k in ("L0_xattn_w_q", "L0_xattn_w_k", "L0_xattn_w_v", "L0_xattn_w_o")},
        **{k: a[k] for k in ("L0_ffn_wqkv", "L0_ffn_wo", "L0_ffn_w1", "L0_ffn_w2")},
        "cols": packed_columns(a), "rows": packed_rows(a), "cos": cos, "sin": sin,
        "band": ((far < 0) | (far > 64)).astype(np.float32),
        "causal": (far < 0).astype(np.float32),
        "iota": np.ascontiguousarray(np.broadcast_to(np.arange(NE3 * CAP, dtype=np.float32), (P, NE3 * CAP))),
        **{k: a[k] for k in ("L1_xattn_Wq", "L1_xattn_Wkv", "L1_xattn_Wout")},
        "fc": c(np.concatenate([a["L1_ffn_w_fc"], a["L1_ffn_shared_fc"][None]]).transpose(2, 0, 1)),
        "proj": c(np.concatenate([a["L1_ffn_w_proj"], a["L1_ffn_shared_proj"][None]]).reshape(NE1 + 1, D, 4, P).transpose(3, 0, 2, 1)),
        "router1": c(a["L1_ffn_router_w"].T), "router2": c(a["L2_ffn_router_w"].T),
        "w2q": c(np.stack([a["L2_xattn_Wqj"].T, a["L2_xattn_Wqi"].T], 1)), "w2k": c(np.stack([a["L2_xattn_Wkj"].T, a["L2_xattn_Wki"].T], 1)),
        "w2v": c(np.concatenate([a["L2_xattn_Wvj"].T, a["L2_xattn_Wvi"].T], 1)), "w2o": c(a["L2_xattn_Wout"].T),
        "w2in": c(a["L2_ffn_w1"].transpose(1, 0, 2).reshape(D, NE2 * H2)),
        "w2out": c(a["L2_ffn_w2"].reshape(2 * NE2, P, D).transpose(1, 0, 2)),
        "before": c((far[0:P, 0:P] < 0).astype(np.float32)), "gate": c(np.concatenate([a["L3_ffn_wg"], a["L3_ffn_res_coef"]], 1)),
        "res_in": a["L3_ffn_res_inter_w"], "res_out": c(a["L3_ffn_res_output_w"].reshape(4, P, D).transpose(1, 0, 2)),
        "inter": c(a["L3_ffn_inter_w"].transpose(1, 0, 2)),
        "output": c(a["L3_ffn_output_w"].reshape(NE3, 4, P, D).transpose(2, 0, 1, 3)),
        "ident": np.eye(P, dtype=np.float32),
    }


def kernel(**inputs):
    import concourse.bacc as bacc
    from concourse.bass_utils import run_bass_kernel_spmd

    nc = bacc.Bacc("TRN2", target_bir_lowering=False, num_devices=1)
    arrays = {f"in_{k}": v for k, v in laid_out(inputs).items()}
    d = {k[3:]: nc.dram_tensor(k, v.shape, mybir.dt.from_np(v.dtype), kind="ExternalInput").ap() for k, v in arrays.items()}
    out = nc.dram_tensor("out", (B, S, D), F32, kind="ExternalOutput").ap()
    program(nc, d, out)
    return run_bass_kernel_spmd(nc, [arrays], core_ids=[0]).results[0]["out"]
```

```python
import numpy as np
import concourse.bass as bass
from concourse import mybir
from contextlib import ExitStack

F32 = mybir.dt.float32
BF16 = mybir.dt.bfloat16
I32 = mybir.dt.int32
U32 = mybir.dt.uint32
U8 = mybir.dt.uint8
ALU = mybir.AluOpType
ACT = mybir.ActivationFunctionType
AX = mybir.AxisListType

B, S, D = 4, 256, 128
P = 128
NT = S // P
T = B * NT
LB = 2
LT = LB * NT
DH = 64
H16, H8 = 16, 8
BANK = 512
HID = 341
HC = [(0, 128), (128, 128), (256, HID - 256)]
NE1, FF = 8, 512
NE2, H2 = 4, 256
NE3, CAP = 8, B * S // 8
MASKED = -1.0e30
LN_EXP = "natural_log_exp_and_others"


def linker(engine, sem):
    count = [0]

    def link(ins):
        count[0] += 1
        ins.then_inc(sem, 1)
        engine.wait_ge(sem, count[0])
    return link


class Net:

    def __init__(self, nc, es):
        self.nc, self.es = nc, es
        self.pool = [es.enter_context(nc.semaphore(f"phase_{i}")) for i in range(44)]

    def sb(self, name, shape, dt=F32):
        return self.es.enter_context(self.nc.sbuf_tensor(name, shape, dt))

    def sem(self, name):
        return self.es.enter_context(self.nc.semaphore(name))

    def signals(self, n):
        return self.pool[:n]

    def end_phase(self):
        self.nc.all_engine_barrier(sems_to_clear=range(self.pool[0].num, self.pool[-1].num + 1))



def dve_stats(nc, link, net, rows, n, eps, var_ready):
    for t in range(n):
        last = nc.vector.bn_stats(net.stats[:, t, :], rows(t))
    link(last)
    for t in range(n):
        last = nc.vector.bn_aggr(net.mv[:, t, :], net.stats[:, t, :])
    link(last)
    nc.vector.tensor_scalar(net.veps[:, 0:n], net.mv[:, 0:n, 1], eps, None, ALU.add).then_inc(var_ready, 1)


def act_rsqrt_seed(nc, act, link, net, n, var_ready, k, seed_ready):
    act.wait_ge(var_ready, k)
    link(nc.scalar.activation(net.lnv[:, 0:n], net.veps[:, 0:n], ACT.Ln))
    nc.scalar.activation(net.seed[:, 0:n], net.lnv[:, 0:n], ACT.Exp, scale=-0.5).then_inc(seed_ready, 1)


def dve_rsqrt(nc, dve, link, net, n, seed_ready, k, out, factor=1.0):
    dve.wait_ge(seed_ready, k)
    y, v, t = net.seed[:, 0:n], net.veps[:, 0:n], net.nwt[:, 0:n]
    link(nc.vector.scalar_tensor_tensor(t, y, -0.5 * factor, y, ALU.mult, ALU.mult))
    link(nc.vector.tensor_tensor(t, t, v, ALU.mult))
    link(nc.vector.scalar_tensor_tensor(out, t, 1.5 * factor, y, ALU.add, ALU.mult))


def dve_normalise(nc, net, out, rows, n):
    for t in range(n):
        last = nc.vector.tensor_scalar(out(t), rows(t), net.mv[:, t, 0:1], net.rstd[:, t:t + 1],
                                       ALU.subtract, ALU.mult)
    return last



def pe_projections(nc, pe, net, tiles, banks, tile_ready, emptied, first=0):
    for j, products in enumerate(tiles):
        if j >= banks:
            pe.wait_ge(emptied[j % 2], (j - banks) // 2 + 1)
        for a, b, stationary, moving in products:
            last = nc.tensor.matmul(net.ps[:, (j + first) % banks, a:b], stationary, moving, start=True, stop=True)
        last.then_inc(tile_ready, 1)


def empty_projections(nc, engine, copy, net, outs, banks, which, tile_ready, emptied, first=0):
    for j, out in enumerate(outs):
        if j % 2 == which:
            engine.wait_ge(tile_ready, j + 1)
            copy(out, net.ps[:, (j + first) % banks, :]).then_inc(emptied[which], 1)


def evac_counts(n):
    return ((n + 1) // 2, n // 2)



class Attention:
    LAG = 3

    def __init__(self, net, units, mask, qT, kT, v, scale, out, sems, out_banks=4, act_copies=0):
        self.out_banks = out_banks
        self.act_copies = act_copies
        self.net, self.units, self.mask, self.qT, self.kT, self.v, self.scale, self.out = net, units, mask, qT, kT, v, scale, out
        (self.scores_ready, self.masked, self.exped, self.inverted, self.normed, self.turned, self.act_copied,
         self.dve_copied, self.pv_done, self.out_copied) = sems
        segments = units[0][1]
        self.ns = len(segments)
        self.cols = [sum(nk for _, nk in segments[:i]) for i in range(self.ns)]
        self.blocks, self.products, at = [], [], 0
        for k in range(max(nk for _, nk in segments) // P):
            having = [i for i in range(self.ns) if segments[i][1] > k * P]
            self.products.append((k, at, len(having) * P, having[0] * P))
            for i in having:
                self.blocks.append((self.cols[i] + k * P, at))
                at += P
        self.width = at

    def out_count(self):
        return len(self.units) // 2

    def pe(self, nc, pe, step_done=lambda step: None):
        net, ns, U = self.net, self.ns, len(self.units)
        for step in range(U + self.LAG + 3):
            if step < U:
                u = step
                h, segments = self.units[u]
                if u >= 2:
                    pe.wait_ge(self.masked, ns * (u - 1))
                for i, (qt, nk) in enumerate(segments):
                    last = nc.tensor.matmul(net.ps[:, u % 2, self.cols[i]:self.cols[i] + nk], self.qT(h, qt), self.kT(h, nk),
                                            start=True, stop=True)
                last.then_inc(self.scores_ready, 1)
            u = step - self.LAG
            if 0 <= u < U:
                pe.wait_ge(self.normed, ns * (u + 1))
                if u >= 2:
                    pe.wait_ge(self.copied_by(u - 2), self.copies(u - 2, self.copied_by(u - 2)))
                for src, dst in self.blocks:
                    last = nc.tensor.transpose(net.ps[:, 2 + u % 2, dst:dst + P], net.probs[:, u % 4, src:src + P], net.ident[:])
                last.then_inc(self.turned, 1)
            u = step - self.LAG - 1
            if u >= 1 and u % 2 == 1 and u < U:
                p = u // 2
                for copied in (self.act_copied, self.dve_copied):
                    if self.copies(u, copied) > 0:
                        pe.wait_ge(copied, self.copies(u, copied))
                if p >= self.out_banks:
                    pe.wait_ge(self.out_copied, p - self.out_banks + 1)
                for k, at, n, q in self.products:
                    for j in range(2):
                        last = nc.tensor.matmul(net.ps[DH * j:DH * (j + 1), 4 + p % self.out_banks, q:q + n],
                                                self.v(self.units[u - 1 + j][0], k), net.probsT[:, (u - 1 + j) % 4, at:at + n],
                                                start=k == 0, stop=k == len(self.products) - 1)
                last.then_inc(self.pv_done, 1)
            step_done(step)

    def copied_by(self, u):
        return self.act_copied if u < self.act_copies or u % 2 == 0 else self.dve_copied

    def copies(self, u, copied):
        return sum(self.copied_by(v) is copied for v in range(u + 1))

    def copy_turned(self, nc, engine, copy, copied, u):
        net = self.net
        if u < 0 or u >= len(self.units) or self.copied_by(u) is not copied:
            return
        engine.wait_ge(self.turned, u + 1)
        if u >= 4:
            engine.wait_ge(self.pv_done, (u - 4) // 2 + 1)
        copy(net.probsT[:, u % 4, 0:self.width], net.ps[:, 2 + u % 2, 0:self.width]).then_inc(copied, 1)

    def act(self, nc, act, step_done=lambda step: None):
        net, ns, U = self.net, self.ns, len(self.units)
        for step in range(U + self.LAG + 5):
            if step < U:
                u = step
                for i, (qt, nk) in enumerate(self.units[u][1]):
                    act.wait_ge(self.masked, ns * u + i + 1)
                    if u >= 4:
                        act.wait_ge(self.inverted, u - 3)
                    x = net.probs[:, u % 4, self.cols[i]:self.cols[i] + nk]
                    nc.scalar.activation(x, x, ACT.Exp, bias=net.negmax[:, u % 4, i:i + 1], scale=-1.0,
                                         accum_out=net.sums[:, u % 4, i:i + 1]).then_inc(self.exped, 1)
            self.copy_turned(nc, act, nc.scalar.copy, self.act_copied, step - self.LAG)
            u = step - self.LAG - 2
            if u >= 1 and u % 2 == 1 and u < U:
                p = u // 2
                act.wait_ge(self.pv_done, p + 1)
                dst = self.out(self.units[u][0], self.units[u][1])
                nc.scalar.copy(dst, net.ps[:, 4 + p % self.out_banks, 0:dst.shape[-1]]).then_inc(self.out_copied, 1)
            step_done(step)

    def dve(self, nc, dve, step_done=lambda step: None):
        net, ns, U = self.net, self.ns, len(self.units)
        for step in range(U + self.LAG + 2):
            if step < U:
                u = step
                h, segments = self.units[u]
                dve.wait_ge(self.scores_ready, u + 1)
                if u >= 4:
                    dve.wait_ge(self.turned, u - 3)
                for i, (qt, nk) in enumerate(segments):
                    c = slice(self.cols[i], self.cols[i] + nk)
                    nc.vector.tensor_tensor_reduce(out=net.probs[:, u % 4, c], in0=net.ps[:, u % 2, c], in1=self.mask[:, c],
                                                   scale=self.scale(h, qt), scalar=-MASKED, op0=ALU.add, op1=ALU.min,
                                                   accum_out=net.negmax[:, u % 4, i:i + 1]).then_inc(self.masked, 1)
            u = step - 1
            if 0 <= u < U:
                dve.wait_ge(self.exped, ns * (u + 1))
                if u >= 4:
                    dve.wait_ge(self.normed, ns * (u - 3))
                nc.vector.reciprocal(net.recip[:, u % 4, 0:ns], net.sums[:, u % 4, 0:ns]).then_inc(self.inverted, 1)
            self.copy_turned(nc, dve, nc.vector.tensor_copy, self.dve_copied, step - self.LAG)
            step_done(step)

    def pool(self, nc, pool):
        net = self.net
        for u, (h, segments) in enumerate(self.units):
            pool.wait_ge(self.inverted, u + 1)
            for i, (qt, nk) in enumerate(segments):
                x = net.probs[:, u % 4, self.cols[i]:self.cols[i] + nk]
                nc.gpsimd.tensor_scalar(x, x, net.recip[:, u % 4, i:i + 1], 1.0, ALU.mult, ALU.mult).then_inc(self.normed, 1)


def head_rows(h):
    return slice(DH * (h % 2), DH * (h % 2) + DH)


class OutProjection:

    def __init__(self, net, attn, qT, w, bank, result, of_pair, tile0=0):
        self.tile0 = tile0
        self.net, self.attn, self.qT, self.w, self.bank, self.result = net, attn, qT, w, bank, result
        pairs = attn.out_count()
        self.jobs = [(p, of_pair(p)[0], t) for p in range(pairs) for t in of_pair(p)[1]]
        self.emitted, self.early = 0, sum(p < pairs - 2 for p, c, t in self.jobs)

    def products(self, nc, pe, a, b):
        for i, (p, c, t) in enumerate(self.jobs[a:b], a):
            if i == a or p != self.jobs[i - 1][0]:
                pe.wait_ge(self.attn.out_copied, p + 1)
            last = nc.tensor.matmul(self.net.ps[:, self.bank, (t - self.tile0) * P:(t - self.tile0 + 1) * P], self.qT[:, c, t * P:(t + 1) * P], self.w[:, c, :],
                                    start=i == 0, stop=i == len(self.jobs) - 1)
        return last

    def step_done(self, nc, pe, step):
        part = step - len(self.attn.units)
        if 0 <= part < 3:
            self.products(nc, pe, self.emitted, self.early * (part + 1) // 3)
            self.emitted = self.early * (part + 1) // 3

    def finish(self, nc, pe):
        self.products(nc, pe, self.emitted, len(self.jobs)).then_inc(self.result, 1)


def batch_rows(net):
    return net.x_all[:, bass.ds(net.batch * NT, NT), :]


def last_batch_rows(net, ap):
    return ap[:, bass.ds(net.batch * NT, NT), :]


def batch_columns(net, ap):
    return ap[:, bass.ds(net.batch, 1), :].rearrange("p b s -> p (b s)")



def layer0_attention(net):
    nc = net.nc
    (tile_ready, act_emptied, dve_emptied, ctxT_ready, zT_ready, o_ready, dve_link, act_link, var_ready, seed_ready,
     *att) = net.signals(20)
    NORM_IN, NORM_OUT, LAST_IN, LAST_OUT = 5, 7, 9, 11
    emptied = (act_emptied, dve_emptied)
    w = net.w0
    tiles, outs = [], []
    for m in range(0, 8, 2):
        tiles.append([(i * S, (i + 1) * S, w["q"][:, (m + i) * P:(m + i + 1) * P], net.zT[:]) for i in range(2)])
        outs.append(net.qT[:, m:m + 2, :])
    for m in range(0, 8, 2):
        tiles.append([(i * S, (i + 1) * S, w["k"][:, (m + i) * P:(m + i + 1) * P], net.ctxT[:]) for i in range(2)])
        outs.append(net.kT[:, m:m + 2, 0:S])
    n_qk = len(tiles)
    for t in range(NT):
        for half in range(2):
            tiles.append([(0, BANK, net.ctxT[:, t * P:(t + 1) * P], w["v"][:, half * BANK:(half + 1) * BANK])])
            outs.append(net.v[:, t, half * BANK:(half + 1) * BANK])
    qk_counts, counts = evac_counts(n_qk), evac_counts(len(tiles))
    attn = Attention(net, [(h, [(0, S), (1, S)]) for h in range(H16)], net.mask0,
                     lambda h, qt: net.qT[head_rows(h), h // 2, qt * P:(qt + 1) * P],
                     lambda h, nk: net.kT[head_rows(h), h // 2, 0:nk],
                     lambda h, k: net.v[:, k, h * DH:(h + 1) * DH],
                     lambda h, qt: -DH ** -0.5, lambda h, segments: net.qT[:, h // 2, :], att, out_banks=3)
    project = OutProjection(net, attn, net.qT, w["o"], 7, o_ready, lambda p: (p, range(NT)))

    with nc.Block() as block:
        @block.vector
        def _(dve):
            nc.vector.tensor_copy(net.ctxT[:], batch_columns(net, net.ctxT_all)).then_inc(ctxT_ready, 1)
            empty_projections(nc, dve, nc.vector.tensor_copy, net, outs, 8, 1, tile_ready, emptied, 2)
            link = linker(dve, dve_link)
            tile = lambda ap: lambda t: ap[:, bass.ds(net.batch * NT + t, 1), :].rearrange("p t d -> p (t d)")
            last_x, last_z = tile(net.x_padded), tile(net.z_padded)
            ctx = [net.cn_all[:, bass.ds(net.batch * NT + t, 1), :].rearrange("p t d -> p (t d)") for t in range(NT)]

            def step_done(step):
                if step == NORM_IN:
                    dve_stats(nc, link, net, lambda t: ctx[t], NT, 1e-5, var_ready)
                if step == NORM_OUT:
                    dve_rsqrt(nc, dve, link, net, NT, seed_ready, 1, net.rstd[:, 0:NT])
                    dve_normalise(nc, net, lambda t: ctx[t], lambda t: ctx[t], NT)
                if step == LAST_IN:
                    dve_stats(nc, link, net, last_x, NT, 1e-5, var_ready)
                if step == LAST_OUT:
                    dve_rsqrt(nc, dve, link, net, NT, seed_ready, 2, net.rstd[:, 0:NT])
                    dve_normalise(nc, net, last_z, last_x, NT)
            attn.dve(nc, dve, step_done)
            dve.wait_ge(o_ready, 1)
            x = batch_rows(net)
            nc.vector.tensor_tensor(x, x, net.ps[:, 7, 0:S].rearrange("p (t d) -> p t d", d=D), ALU.add)

        @block.scalar
        def _(act):
            nc.scalar.copy(net.zT[:], batch_columns(net, net.zT_all)).then_inc(zT_ready, 1)
            empty_projections(nc, act, nc.scalar.copy, net, outs, 8, 0, tile_ready, emptied, 2)
            link = linker(act, act_link)

            def step_done(step):
                if step == NORM_IN:
                    act_rsqrt_seed(nc, act, link, net, NT, var_ready, 1, seed_ready)
                if step == LAST_IN:
                    act_rsqrt_seed(nc, act, link, net, NT, var_ready, 2, seed_ready)
            attn.act(nc, act, step_done)

        @block.tensor
        def _(pe):
            pe.wait_ge(ctxT_ready, 1)
            pe.wait_ge(zT_ready, 1)
            pe.wait_ge(net.w0_loaded, net.w0_count)
            pe_projections(nc, pe, net, tiles, 8, tile_ready, emptied, 2)
            for which in range(2):
                pe.wait_ge(emptied[which], qk_counts[which])

            def step_done(step):
                if step == 1:
                    for which in range(2):
                        pe.wait_ge(emptied[which], counts[which])
                project.step_done(nc, pe, step)
            attn.pe(nc, pe, step_done)
            project.finish(nc, pe)

        @block.gpsimd
        def _(pool):
            attn.pool(nc, pool)
    net.end_phase()



def local_block(net, l):
    nc = net.nc
    (dve_link, act_link, pool_link, zT_turned, zT_ready, qkv_ready, rows_copied, squares_ready, v_copied, cos_done,
     sin_ready, rotated, qk_turned, qk_act, qk_dve, summed, sin_added, pool_cos, pool_added, z_copied, var_ready, seed_ready, o_ready,
     z_ready, shifted, rows_ready, hT_turned, hT_ready, gate_in, gated, hidden_ready, mlp_ready, *att) = net.signals(42)
    w, m = net.wf[l], net.local
    attn = Attention(net, [((b, h), [(0, P), (1, S)]) for b in range(LB) for h in range(H8)], net.band,
                     lambda bh, qt: m["qT"][head_rows(bh[1]), bh[1] // 2, bh[0] * S + qt * P:bh[0] * S + (qt + 1) * P],
                     lambda bh, nk: m["kT"][head_rows(bh[1]), bh[1] // 2, bh[0] * S:bh[0] * S + nk],
                     lambda bh, k: m["v"][:, bh[0] * NT + k, bh[1] * DH:(bh[1] + 1) * DH],
                     lambda bh, qt: net.rnorm[:, bh[0] * NT + qt, bh[1]:bh[1] + 1],
                     lambda bh, segments: m["qT"][:, bh[1] // 2, bh[0] * S:(bh[0] + 1) * S], att, out_banks=2, act_copies=H8)
    project = [OutProjection(net, attn, m["qT"], w["o"], 7 - b, o_ready,
                             lambda p, b=b: (p % 4, range(b * NT, b * NT + NT) if p // 4 == b else ()), b * NT) for b in range(LB)]
    SQUARES, SEED, ROTATE, TURN, COPY = {0: 2, 1: 3}, 1, {2: 2, 3: 3}, {4: 2, 5: 3}, {5: 2, 6: 3}

    PROJECT, ADD, STATS, NORMED, TURN_H = H8 + 5, H8 + 6, H8 + 7, H8 + 8, H8 + 9

    def tiles_of(b):
        return range(b * NT, b * NT + NT)

    def add_output(dve, b):
        dve.wait_ge(o_ready, b + 1)
        zb = net.z[:, b * NT:b * NT + NT, :]
        nc.vector.tensor_tensor(zb, zb, net.ps[:, 7 - b, 0:S].rearrange("p (t d) -> p t d", d=D), ALU.add).then_inc(z_ready, 1)

    def shift_rows(pe, b):
        pe.wait_ge(z_ready, b + 1)
        z2 = net.z[:, b * NT:b * NT + NT, half]
        nc.tensor.matmul(net.ps[:, 7 - b, S:S + NT * (D // 2)], net.next_row[:], z2, start=True, stop=False)
        nc.tensor.matmul(net.ps[:, 7 - b, S + D // 2:S + D], net.next_tile[:], z2[:, 0, :], start=False, stop=True).then_inc(shifted, 1)

    def shifted_row(t):
        c = S + (t % NT) * (D // 2)
        return net.ps[:, 7 - t // NT, c:c + D // 2]

    def norm_in(dve, link, b):
        dve.wait_ge(z_ready, b + 1)
        for t in tiles_of(b):
            nc.vector.bn_stats(net.stats[:, 2 * t, :], net.z[:, t, 0:D // 2])
        dve.wait_ge(shifted, b + 1)
        for t in tiles_of(b):
            last = nc.vector.bn_stats(net.stats[:, 2 * t + 1, :], shifted_row(t))
        link(last)
        for t in tiles_of(b):
            last = nc.vector.bn_aggr(net.mv[:, t, :], net.stats[:, 2 * t:2 * t + 2, :])
        link(last)
        nc.vector.tensor_scalar(net.veps[:, 0:NT], net.mv[:, b * NT:b * NT + NT, 1], 1e-5, None, ALU.add).then_inc(var_ready, 1)

    def norm_out(dve, link, b):
        dve_rsqrt(nc, dve, link, net, NT, seed_ready, 3 + b, net.rstd[:, b * NT:b * NT + NT])
        for t in tiles_of(b):
            for out, rows in ((m["hn"][:, t, 0:D // 2], net.z[:, t, 0:D // 2]), (m["hn"][:, t, half], shifted_row(t))):
                last = nc.vector.tensor_scalar(out, rows, net.mv[:, t, 0:1], net.rstd[:, t:t + 1], ALU.subtract, ALU.mult)
        last.then_inc(rows_ready, 1)

    def turn_h(pe, b):
        pe.wait_ge(rows_ready, b + 1)
        for t in tiles_of(b):
            last = nc.tensor.transpose(net.ps[:, 7 - b, (t % NT) * P:(t % NT + 1) * P], m["hn"][:, t, :], net.ident[:])
        last.then_inc(hT_turned, 1)

    def copy_h(act, b):
        act.wait_ge(hT_turned, b + 1)
        nc.scalar.activation(m["hnT"][:, b * S:(b + 1) * S], net.ps[:, 7 - b, 0:S], ACT.Identity, scale=net.col("L0_ln_g", l),
                             bias=net.col("L0_ln_b", l)).then_inc(hT_ready, 1)

    def hidden_in(pe, b, c):
        pe.wait_ge(hT_ready, b + 1)
        c0, cn = HC[c]
        for part in range(2):
            last = nc.tensor.matmul(net.ps[0:cn, 3 * b + c, part * S:(part + 1) * S], w["w1"][:, part * HID + c0:part * HID + c0 + cn],
                                    m["hnT"][:, b * S:(b + 1) * S], start=True, stop=True)
        last.then_inc(gate_in, 1)

    chunks = [(b, c) for b in range(LB) for c in range(len(HC))]

    def turn_bank(t):
        return 4 if t == 1 else 6

    def turn_qk(pe, t):
        pe.wait_ge(rotated, t + 1)
        if t >= 2:
            pe.wait_ge(qk_act, t)
            pe.wait_ge(qk_dve, t)
        for part in range(2):
            for c in range(4):
                last = nc.tensor.transpose(net.ps[:, turn_bank(t) + part, c * P:(c + 1) * P],
                                           m["rot"][:, t, part * BANK + c * P:part * BANK + (c + 1) * P], net.ident[:])
            last.then_inc(qk_turned, 1)

    def copy_q(act, t):
        act.wait_ge(qk_turned, 2 * t + 1)
        nc.scalar.copy(m["qT"][:, 0:4, t * P:(t + 1) * P], net.ps[:, turn_bank(t), :].rearrange("p (m s) -> p m s", m=4)).then_inc(qk_act, 1)

    def copy_k(dve, t):
        dve.wait_ge(qk_turned, 2 * t + 2)
        nc.vector.tensor_copy(m["kT"][:, 0:4, t * P:(t + 1) * P], net.ps[:, turn_bank(t) + 1, :].rearrange("p (m s) -> p m s", m=4)).then_inc(qk_dve, 1)

    def times_cos(engine, multiply, t, done):
        engine.wait_ge(rows_copied, t + 1)
        x = m["qk"][:, t, :].rearrange("p (a h d) -> p a h d", a=2, d=DH)
        y = m["rot"][:, t, :].rearrange("p (a h d) -> p a h d", a=2, d=DH)
        multiply(y, x, net.cos_t[:, l, t % NT, :, :].unsqueeze(2).to_broadcast([P, 2, H8, DH]), ALU.mult).then_inc(done, 1)

    def sum_squares(dve, t):
        dve.wait_ge(squares_ready, t + 1)
        nc.vector.reduce_sum(net.ssq[:, t, :], m["squares"][:, t, :].rearrange("p (h d) -> p h d", d=DH), AX.X).then_inc(summed, 1)

    def norms_in(dve, b):
        dve.wait_ge(summed, NT * (b + 1))
        nc.vector.tensor_scalar(net.veps[:, 0:NT * 16], net.ssq[:, NT * b:NT * (b + 1), :].rearrange("p t h -> p (t h)"), 1e-24, 2.0 ** 30,
                                ALU.max, ALU.mult).then_inc(var_ready, 1)

    def norms_out(dve, link, b):
        mine = net.rnorm[:, NT * b:NT * (b + 1), :]
        dve_rsqrt(nc, dve, link, net, NT * 16, seed_ready, b + 1, mine.rearrange("p t h -> p (t h)"), 2.0 ** 15)
        link(nc.vector.tensor_scalar(mine[:, :, 0:H8], mine[:, :, 0:H8], -8.0, None, ALU.mult))

    def add_sin(dve, t):
        if t < NT:
            dve.wait_ge(cos_done, t + 1)
            dve.wait_ge(sin_ready, t + 1)
            nc.vector.tensor_tensor(m["rot"][:, t, :], m["rot"][:, t, :], m["sin"][:, t, :], ALU.add).then_inc(sin_added, 1)
            dve.wait_ge(sin_added, t + 1)
        else:
            dve.wait_ge(pool_added, t - NT + 1)
        k = m["rot"][:, t, BANK:2 * BANK].rearrange("p (h d) -> p h d", d=DH)
        nc.vector.tensor_tensor(k, k, net.rnorm[:, t, H8:16].unsqueeze(2).to_broadcast([P, H8, DH]), ALU.mult).then_inc(rotated, 1)
    half = slice(D // 2, D)

    def rot(x, a, b):
        return x[:, :, :, a:b]

    with nc.Block() as block:
        @block.tensor
        def _(pe):
            if l == 0:
                pe.wait_ge(z_copied, 1)
            for t in range(LT):
                last = nc.tensor.transpose(net.ps[:, 7, t * P:(t + 1) * P], net.z[:, t, :], net.ident[:])
            last.then_inc(zT_turned, 1)
            pe.wait_ge(zT_ready, 3)
            pe.wait_ge(net.wf_loaded, net.wf_count * (l + 1))
            for t in range(LT):
                if t >= 2:
                    pe.wait_ge(squares_ready, t - 1)
                    pe.wait_ge(rows_copied, t - 1)
                    pe.wait_ge(v_copied, t - 1)
                for part in range(3):
                    last = nc.tensor.matmul(net.ps[:, 3 * (t % 2) + part, :], m["hT"][:, t * P:(t + 1) * P],
                                            w["qkv"][:, part * BANK:(part + 1) * BANK], start=True, stop=True)
                    if part >= 1:
                        last.then_inc(qkv_ready, 1)
            pe.wait_ge(v_copied, LT)
            pe.wait_ge(squares_ready, LT)
            pe.wait_ge(rows_copied, LT)
            for t in range(NT):
                turn_qk(pe, t)
            pe.wait_ge(qk_act, NT)
            pe.wait_ge(qk_dve, NT)

            def step_done(step):
                if step == PROJECT:
                    project[0].finish(nc, pe)
                if step == ADD:
                    shift_rows(pe, 0)
                if step == TURN_H:
                    turn_h(pe, 0)
                project[1].step_done(nc, pe, step)
                if step in TURN:
                    turn_qk(pe, TURN[step])
                if step == H8 - 1:
                    pe.wait_ge(qk_act, LT)
                    pe.wait_ge(qk_dve, LT)
            attn.pe(nc, pe, step_done)
            project[1].finish(nc, pe)
            hidden_in(pe, 0, 0)
            shift_rows(pe, 1)
            hidden_in(pe, 0, 1)
            hidden_in(pe, 0, 2)
            turn_h(pe, 1)
            for c in range(len(HC)):
                hidden_in(pe, 1, c)
            for t in range(LT):
                for c, (c0, cn) in enumerate(HC):
                    if t % NT == 0:
                        pe.wait_ge(hidden_ready, chunks.index((t // NT, c)) + 1)
                    last = nc.tensor.matmul(net.ps[:, 7, t * P:(t + 1) * P], m["hid"][0:cn, c, t * P:(t + 1) * P],
                                            w["w2"][0:cn, c, :], start=c == 0, stop=c == len(HC) - 1)
            last.then_inc(mlp_ready, 1)

        @block.scalar
        def _(act):
            link = linker(act, act_link)
            act.wait_ge(zT_turned, 1)
            nc.scalar.copy(m["hT"][0:D // 2, :], net.ps[0:D // 2, 7, :]).then_inc(zT_ready, 1)
            for t in range(LT):
                act.wait_ge(qkv_ready, 2 * t + 1)
                nc.scalar.copy(m["qk"][:, t, :], net.ps[:, 3 * (t % 2):3 * (t % 2) + 2, :].rearrange("p b n -> p (b n)")).then_inc(rows_copied, 1)
                nc.scalar.activation(m["squares"][:, t, :], net.ps[:, 3 * (t % 2):3 * (t % 2) + 2, :].rearrange("p b n -> p (b n)"), ACT.Square).then_inc(squares_ready, 1)
                act.wait_ge(qkv_ready, 2 * t + 2)
                nc.scalar.copy(m["v"][:, t, 0:BANK], net.ps[:, 3 * (t % 2) + 2, :]).then_inc(v_copied, 1)
                if t == NT:
                    act_rsqrt_seed(nc, act, link, net, NT * 16, var_ready, 1, seed_ready)
            for t in range(NT):
                copy_q(act, t)

            def step_done(step):
                if step == SEED:
                    act_rsqrt_seed(nc, act, link, net, NT * 16, var_ready, 2, seed_ready)
                if step in COPY:
                    copy_q(act, COPY[step])
                if step == STATS:
                    act_rsqrt_seed(nc, act, link, net, NT, var_ready, 3, seed_ready)
                if step == TURN_H:
                    copy_h(act, 0)
            attn.act(nc, act, step_done)
            act_rsqrt_seed(nc, act, link, net, NT, var_ready, 4, seed_ready)
            nc.scalar.preload_act_table(ACT.Gelu)
            copy_h(act, 1)
            for i, (b, c) in enumerate(chunks):
                cn = HC[c][1]
                act.wait_ge(gate_in, i + 1)
                nc.scalar.activation(m["gate"][0:cn, c, b * S:(b + 1) * S], net.ps[0:cn, 3 * b + c, S:2 * S], ACT.Gelu,
                                     bias=net.col("L0_b1", 6 * l + 3 + c)[0:cn]).then_inc(gated, 1)
            nc.scalar.preload_act_table_set(LN_EXP)

        @block.gpsimd
        def _(pool):
            for t in range(LT):
                pool.wait_ge(rows_copied, t + 1)
                x = m["qk"][:, t, :].rearrange("p (a h d) -> p a h d", a=2, d=DH)
                y = m["sin"][:, t, :].rearrange("p (a h d) -> p a h d", a=2, d=DH)
                sin = net.sin_t[:, l, t % NT, :, :]
                for a, b in ((0, 32), (32, 0)):
                    last = nc.gpsimd.tensor_tensor(rot(y, a, a + 32), rot(x, b, b + 32),
                                                   sin[:, :, a:a + 32].unsqueeze(2).to_broadcast([P, 2, H8, 32]), ALU.mult)
                last.then_inc(sin_ready, 1)
            times_cos(pool, nc.gpsimd.tensor_tensor, 3, pool_cos)
            for t in range(NT, LT):
                pool.wait_ge(sin_ready, t + 1)
                if t == 2:
                    pool.wait_ge(cos_done, 3)
                else:
                    pool.wait_ge(pool_cos, 1)
                nc.gpsimd.tensor_tensor(m["rot"][:, t, :], m["rot"][:, t, :], m["sin"][:, t, :], ALU.add).then_inc(pool_added, 1)
            attn.pool(nc, pool)

        @block.vector
        def _(dve):
            link = linker(dve, dve_link)
            if l == 0:
                turn = net.z_padded[:, bass.ds(net.turn * LT + NT, LT), :]
                nc.vector.tensor_copy(net.z[:], turn).then_inc(z_copied, 1)
            dve.wait_ge(zT_turned, 1)
            by_batch = lambda ap: ap.rearrange("p (b s) -> p b s", b=LB)
            nc.vector.tensor_copy(by_batch(m["hT"][half, :])[:, :, 1:S], by_batch(net.ps[half, 7, :])[:, :, 0:S - 1]).then_inc(zT_ready, 1)
            nc.vector.memset(by_batch(m["hT"][half, :])[:, :, 0:1], 0.0).then_inc(zT_ready, 1)
            for t in range(NT):
                times_cos(dve, nc.vector.tensor_tensor, t, cos_done)
                sum_squares(dve, t)
            norms_in(dve, 0)
            times_cos(dve, nc.vector.tensor_tensor, 2, cos_done)
            norms_out(dve, link, 0)
            for t in range(NT):
                add_sin(dve, t)
            copy_k(dve, 0)
            copy_k(dve, 1)

            def step_done(step):
                if step in SQUARES:
                    sum_squares(dve, SQUARES[step])
                if step == SEED:
                    norms_in(dve, 1)
                if step in ROTATE:
                    if step == SEED + 1:
                        norms_out(dve, link, 1)
                    add_sin(dve, ROTATE[step])
                if step in COPY:
                    copy_k(dve, COPY[step])
                if step == ADD:
                    add_output(dve, 0)
                if step == STATS:
                    norm_in(dve, link, 0)
                if step == NORMED:
                    norm_out(dve, link, 0)
            attn.dve(nc, dve, step_done)
            add_output(dve, 1)
            norm_in(dve, link, 1)
            norm_out(dve, link, 1)
            dve.wait_ge(rows_ready, 2)
            link(nc.vector.tensor_tensor(net.z[:], net.z[:], net.row("L0_b2", l).unsqueeze(1).to_broadcast([P, LT, D]), ALU.add))
            for i, (b, c) in enumerate(chunks):
                cn = HC[c][1]
                dve.wait_ge(gated, i + 1)
                nc.vector.scalar_tensor_tensor(m["hid"][0:cn, c, b * S:(b + 1) * S], net.ps[0:cn, 3 * b + c, 0:S],
                                               net.col("L0_b1", 6 * l + c)[0:cn], m["gate"][0:cn, c, b * S:(b + 1) * S],
                                               ALU.add, ALU.mult).then_inc(hidden_ready, 1)
            dve.wait_ge(mlp_ready, 1)
            link(nc.vector.tensor_tensor(net.z[:], net.z[:], net.ps[:, 7, :].rearrange("p (t d) -> p t d", d=D), ALU.add))
            if l == 1:
                x = turn_rows(net)
                nc.vector.tensor_tensor(x, x, net.z[:], ALU.add)
    net.end_phase()


def turn_rows(net):
    return net.x_all[:, bass.ds(net.turn * LT, LT), :]



def dve_norm_rows(nc, dve, link, net, src, out, n, eps, var_ready, seed_ready, k):
    dve_stats(nc, link, net, src, n, eps, var_ready)
    dve_rsqrt(nc, dve, link, net, n, seed_ready, k, net.rstd[:, 0:n])
    return dve_normalise(nc, net, out, src, n)


def spread(ap, n):
    return ap.unsqueeze(2).to_broadcast([P, ap.shape[1], n])


def dve_top2(nc, dve, link, net, logits, ne, probs, exp_in, exp_out, k, guard, comb, t0=0, n=T):
    r, ts = net.small, slice(t0, t0 + n)
    mx, sm, top, idx, idxf = r["mx"][:, ts], r["sm"][:, ts], r["top"][:, ts, :], r["idx"][:, ts, :], r["idxf"][:, ts, :]
    e, eq, w2, probs = r["e"][:, ts, 0:ne], r["eq"][:, :, ts, 0:ne], r["w2"][:, ts, :], probs[:, ts, :]
    link(nc.vector.reduce_max(mx, logits, AX.X))
    nc.vector.tensor_tensor(e, logits, spread(mx, ne), ALU.subtract).then_inc(exp_in, 1)
    dve.wait_ge(exp_out, k)
    link(nc.vector.reduce_sum(sm, e, AX.X))
    link(nc.vector.reciprocal(sm, sm))
    link(nc.vector.tensor_tensor(probs[:, :, 0:ne], e, spread(sm, ne), ALU.mult))
    for t in range(n):
        last = nc.vector.max(top[:, t, :], probs[:, t, :])
    link(last)
    for t in range(n):
        last = nc.vector.max_index(idx[:, t, :], top[:, t, :], probs[:, t, :])
    link(last)
    nc.vector.tensor_copy(idxf, idx)
    link(nc.vector.tensor_tensor(sm, top[:, :, 0], top[:, :, 1], ALU.add))
    link(nc.vector.tensor_scalar(sm, sm, guard[0], None, guard[1]))
    link(nc.vector.reciprocal(sm, sm))
    iota = net.iota[:, 0:ne].unsqueeze(1).to_broadcast([P, n, ne])
    for c in range(2):
        nc.vector.tensor_tensor(eq[:, c], iota, spread(idxf[:, :, c], ne), ALU.is_equal)
    link(nc.vector.tensor_tensor(w2, top[:, :, 0:2], spread(sm, 2), ALU.mult))
    for c in range(2):
        last = nc.vector.tensor_tensor(eq[:, c], eq[:, c], spread(w2[:, :, c], ne), ALU.mult)
    link(last)
    link(nc.vector.tensor_tensor(comb, eq[:, 0], eq[:, 1], ALU.add))


def rows_of(ap):
    return lambda t: ap[:, t, :]



def layer1_attention(net):
    nc = net.nc
    (cols_ready, mask_ready, mask_spread, mask_copied, tile_ready,
     act_emptied, dve_emptied, o_ready, dve_link, act_link, var_ready, seed_ready, *att) = net.signals(22)
    NORM_IN, NORM_OUT = 6, 9
    emptied = (act_emptied, dve_emptied)
    w = net.w1
    tiles, outs = [], []
    for m in range(0, 8, 2):
        tiles.append([(i * S, (i + 1) * S, w["q"][:, (m + i) * P:(m + i + 1) * P], net.kv_in[:, S:2 * S]) for i in range(2)])
        outs.append(net.qT[:, m:m + 2, :])
    for m in range(8):
        tiles.append([(0, BANK, w["kv"][:, m * P:(m + 1) * P], net.kv_in[:])])
        outs.append(net.kT[:, m, :])
    for t in range(4):
        for half in range(2):
            tiles.append([(0, BANK, net.kv_in[:, t * P:(t + 1) * P], w["kv"][:, 1024 + half * BANK:1024 + (half + 1) * BANK])])
            outs.append(net.v[:, t, half * BANK:(half + 1) * BANK])
    late_counts, counts = evac_counts(len(tiles) - 4), evac_counts(len(tiles))
    attn = Attention(net, [(h, [(t, 2 * S)]) for t in range(NT) for h in range(H16)], net.kmask_all,
                     lambda h, qt: net.qT[head_rows(h), h // 2, qt * P:(qt + 1) * P],
                     lambda h, nk: net.kT[head_rows(h), h // 2, 0:nk],
                     lambda h, k: net.v[:, k, h * DH:(h + 1) * DH],
                     lambda h, qt: -DH ** -0.5,
                     lambda h, segments: net.qT[:, h // 2, segments[0][0] * P:(segments[0][0] + 1) * P], att, out_banks=3)
    project = OutProjection(net, attn, net.qT, w["o"], 7, o_ready, lambda p: (p % 8, [p // 8]))

    with nc.Block() as block:
        @block.tensor
        def _(pe):
            pe.wait_ge(mask_ready, 1)
            nc.tensor.matmul(net.ps[:, 7, :], net.ones_b[0:1, :], net.kmask[:], start=True, stop=True).then_inc(mask_spread, 1)
            pe.wait_ge(cols_ready, 1)
            pe.wait_ge(net.w1_loaded, net.w1_count)
            pe_projections(nc, pe, net, tiles, 6, tile_ready, emptied, 4)
            for which in range(2):
                pe.wait_ge(emptied[which], late_counts[which])
            pe.wait_ge(mask_copied, 1)

            def step_done(step):
                if step == 1:
                    for which in range(2):
                        pe.wait_ge(emptied[which], counts[which])
                project.step_done(nc, pe, step)
            attn.pe(nc, pe, step_done)
            project.finish(nc, pe)

        @block.gpsimd
        def _(pool):
            attn.pool(nc, pool)

        @block.scalar
        def _(act):
            nc.scalar.copy(net.kv_in[:], batch_columns(net, net.kv_all)).then_inc(cols_ready, 1)
            act.wait_ge(mask_spread, 1)
            nc.scalar.copy(net.kmask_all[:], net.ps[:, 7, :]).then_inc(mask_copied, 1)
            empty_projections(nc, act, nc.scalar.copy, net, outs, 6, 0, tile_ready, emptied, 4)
            link = linker(act, act_link)

            def step_done(step):
                if step == NORM_IN:
                    act_rsqrt_seed(nc, act, link, net, NT, var_ready, 1, seed_ready)
            attn.act(nc, act, step_done)

        @block.vector
        def _(dve):
            nc.vector.tensor_copy(net.kmask[0:1, 0:S], batch_columns(net, net.kmask_f)).then_inc(mask_ready, 1)
            empty_projections(nc, dve, nc.vector.tensor_copy, net, outs, 6, 1, tile_ready, emptied, 4)
            dve.wait_ge(mask_copied, 1)
            link = linker(dve, dve_link)
            last_o = lambda t: net.z_padded[:, bass.ds(net.batch * NT + t, 1), :].rearrange("p t d -> p (t d)")
            last_rows = last_batch_rows(net, net.z_padded)

            def step_done(step):
                if step == NORM_IN:
                    dve_stats(nc, link, net, last_o, NT, 1e-5, var_ready)
                if step == NORM_OUT:
                    dve_rsqrt(nc, dve, link, net, NT, seed_ready, 1, net.rstd[:, 0:NT])
                    link(dve_normalise(nc, net, last_o, last_o, NT))
                    nc.vector.tensor_tensor(last_rows, last_rows, net.row("L1_g_o", 0).unsqueeze(1).to_broadcast([P, NT, D]), ALU.mult)
            attn.dve(nc, dve, step_done)
            dve.wait_ge(o_ready, 1)
            out = net.z_padded[:, bass.ds(net.batch * NT + NT, NT), :]
            nc.vector.tensor_copy(out, net.ps[:, 7, 0:S].rearrange("p (t d) -> p t d", d=D))
    net.end_phase()



HT = BANK // P


def half_tiles(j):
    return slice(HT * j, HT * j + HT)


def dve_norm_half(nc, dve, link, net, src, out, j, eps, var_ready, seed_ready, k):
    return dve_norm_rows(nc, dve, link, net, rows_of(src[:, half_tiles(j), :]), rows_of(out[:, half_tiles(j), :]), HT, eps,
                         var_ready, seed_ready, k)


def pe_turn_rows(nc, net, src, banks, turned, halves=range(T * P // BANK)):
    for j, bank in zip(halves, banks):
        for t in range(HT):
            last = nc.tensor.transpose(net.ps[:, bank, t * P:(t + 1) * P], src[:, HT * j + t, :], net.ident[:])
        last.then_inc(turned, 1)


def prepare_layer1(net):
    nc = net.nc
    dve_link, act_link, loaded, var_ready, seed_ready, rows_ready, turned = net.signals(7)
    m = net.prep1
    zr, hn = m["z"], m["hn"]

    with nc.Block() as block:
        @block.sync
        def _(sp):
            sp.dma_start(net.ctx_all[:], net.d["ctx"].rearrange("b (t p) d -> p (b t) d", p=P)).then_inc(loaded, 16)
            sp.dma_start(m["kmask"], net.d["kmask"].rearrange("b k -> (b k)").unsqueeze(0)).then_inc(loaded, 16)
            sp.wait_ge(turned, 2)
            d = net.d
            sp.dma_start(net.fc[:], d["fc"]).then_inc(net.w1f_loaded, 16)
            sp.dma_start(net.proj[:], d["proj"]).then_inc(net.w1f_loaded, 16)
            sp.dma_start(net.router1[:], d["router1"]).then_inc(net.w1f_loaded, 16)
            for name, tile in (("w2q", net.w2x["q"]), ("w2k", net.w2x["k"]), ("w2v", net.w2x["v"]), ("w2o", net.w2x["o"]),
                               ("router2", net.router2), ("w2in", net.w2f["in"]), ("w2out", net.w2f["out"])):
                sp.dma_start(tile[:], d[name]).then_inc(net.w2_loaded, 16)
            sp.wait_ge(loaded, 32)

        @block.tensor
        def _(pe):
            pe_turn_rows(nc, net, net.cn_all, (0, 1), turned)
            pe.wait_ge(rows_ready, 1)
            pe_turn_rows(nc, net, hn, (2, 3), turned)

        @block.scalar
        def _(act):
            link = linker(act, act_link)
            for k, name in enumerate(("x", "l")):
                for j in range(2):
                    act.wait_ge(turned, 2 * k + j + 1)
                    dst = net.kv_all[:, 2 * j:2 * j + 2, k * S:(k + 1) * S]
                    nc.scalar.activation(dst, net.ps[:, 2 * k + j, :].rearrange("p (b s) -> p b s", b=2), ACT.Identity,
                                         scale=net.col("L1_g_" + name, 0), bias=net.col("L1_b_" + name, 0))
                if k == 0:
                    for n in range(2):
                        act_rsqrt_seed(nc, act, link, net, T, var_ready, n + 1, seed_ready)

        @block.vector
        def _(dve):
            link = linker(dve, dve_link)
            link(dve_norm_rows(nc, dve, link, net, rows_of(net.x_all), rows_of(zr), T, 1e-5, var_ready, seed_ready, 1))
            dve_norm_rows(nc, dve, link, net, rows_of(zr), rows_of(hn), T, 1e-5, var_ready, seed_ready, 2).then_inc(rows_ready, 1)
            dve.wait_ge(loaded, 32)
            nc.vector.tensor_scalar(net.kmask_f[:].rearrange("p b s -> p (b s)"), m["kmask"].bitcast(U8), -MASKED, MASKED, ALU.mult, ALU.add)
    net.end_phase()



def layer1_experts(net):
    nc = net.nc
    (dve_link, act_link, var_ready, seed_ready, rows_ready, turned, zT_ready, logits_ready, exp_in, exp_out,
     fc_ready, relu_ready, hid_ready, proj_ready, added, loaded, biased) = net.signals(17)
    m = net.late
    z, zT, relu, hid = m["z"], m["zT"], m["relu"], m["hid"]
    comb = net.comb[:, :, 0:NE1]
    halves = T * P // BANK
    n = NE1 + 1
    groups = [(e, j) for j in range(halves) for e in [NE1] + list(range(NE1))]
    G = len(groups)
    TURN = n - 2

    def pe_turn_half(pe, j):
        pe.wait_ge(rows_ready, j + 1)
        for t in range(HT):
            last = nc.tensor.transpose(net.ps[:, 7, t * P:(t + 1) * P], z[:, HT * j + t, :], net.ident[:])
        last.then_inc(turned, 1)

    def pe_logits(pe, j):
        pe.wait_ge(zT_ready, j + 1)
        if j >= 1:
            pe.wait_ge(exp_in, j)
        for t in range(HT * j, HT * j + HT):
            last = nc.tensor.matmul(net.ps[:, 6, t * NE1:(t + 1) * NE1], zT[:, t * P:(t + 1) * P], net.router1[:],
                                    start=True, stop=True)
        last.then_inc(logits_ready, 1)

    def copy_columns(act, j):
        act.wait_ge(turned, j + 1)
        nc.scalar.copy(zT[:, j * BANK:(j + 1) * BANK], net.ps[:, 7, :]).then_inc(zT_ready, 1)

    def rows_step(dve, link, j, step):
        ts = slice(HT * j, HT * j + HT)
        x, zj = net.x_all[:, ts, :], z[:, ts, :]
        o = net.z_padded[:, NT + HT * j:NT + HT * (j + 1), :]
        unnormed = net.z_padded[:, B * NT:(B + 1) * NT, :]
        if step == 0:
            dve_stats(nc, link, net, rows_of(unnormed), NT, 1e-5, var_ready)
        elif step == 1:
            dve_rsqrt(nc, dve, link, net, NT, seed_ready, 2, net.rstd[:, 0:NT])
            link(dve_normalise(nc, net, rows_of(unnormed), rows_of(unnormed), NT))
            link(nc.vector.tensor_tensor(unnormed, unnormed, net.row("L1_g_o", 0).unsqueeze(1).to_broadcast([P, NT, D]), ALU.mult))
        elif step == 2:
            dve.wait_ge(biased, 1)
            link(nc.vector.tensor_tensor(x, x, o, ALU.add))
        elif step == 3:
            dve_stats(nc, link, net, rows_of(x), HT, 1e-5, var_ready)
        else:
            dve_rsqrt(nc, dve, link, net, HT, seed_ready, 2 * j + 1, net.rstd[:, 0:HT])
            dve_normalise(nc, net, rows_of(zj), rows_of(x), HT).then_inc(rows_ready, 1)

    with nc.Block() as block:
        @block.sync
        def _(sp):
            sp.dma_start(m["ids_i"], net.d["ids"].rearrange("b s -> (b s)").unsqueeze(0)).then_inc(loaded, 16)
            sp.dma_start(net.ptr_i[:].rearrange("p (b t) -> p b t", b=B), net.d["ptr"].rearrange("b p t -> p b t")).then_inc(loaded, 16)

        @block.tensor
        def _(pe):
            pe.wait_ge(net.w1f_loaded, net.w1f_count)
            pe_turn_half(pe, 0)
            for g in range(G + 1):
                if g == TURN:
                    pe_turn_half(pe, 1)
                if g % n == 0 and g < G:
                    pe_logits(pe, g // n)
                if g < G:
                    e, j = groups[g]
                    for c in range(4):
                        i = 4 * g + c
                        if i >= 4:
                            pe.wait_ge(hid_ready, i - 3)
                        nc.tensor.matmul(net.ps[:, c, :], net.fc[:, e, c * P:(c + 1) * P], zT[:, j * BANK:(j + 1) * BANK],
                                         start=True, stop=True).then_inc(fc_ready, 1)
                if g >= 1:
                    v = g - 1
                    e = groups[v][0]
                    pe.wait_ge(hid_ready, 4 * (v + 1))
                    if v >= 2:
                        pe.wait_ge(added, v - 1)
                    for t in range(4):
                        for c in range(4):
                            last = nc.tensor.matmul(net.ps[:, 4 + v % 2, t * P:(t + 1) * P], hid[:, v % 2, c, t * P:(t + 1) * P],
                                                    net.proj[:, e, c, :], start=c == 0, stop=c == 3)
                    last.then_inc(proj_ready, 1)

        @block.scalar
        def _(act):
            link = linker(act, act_link)
            act_rsqrt_seed(nc, act, link, net, HT, var_ready, 1, seed_ready)
            copy_columns(act, 0)
            for i in range(4 * G):
                if i == 8:
                    act_rsqrt_seed(nc, act, link, net, NT, var_ready, 2, seed_ready)
                if i == 20:
                    act_rsqrt_seed(nc, act, link, net, HT, var_ready, 3, seed_ready)
                if i == 4 * (TURN + 1):
                    copy_columns(act, 1)
                if i % (4 * n) == 8:
                    j = i // (4 * n)
                    act.wait_ge(exp_in, j + 1)
                    e2 = net.small["e"][:, HT * j:HT * j + HT, 0:NE1]
                    nc.scalar.activation(e2, e2, ACT.Exp).then_inc(exp_out, 1)
                act.wait_ge(fc_ready, i + 1)
                if i >= 4:
                    act.wait_ge(hid_ready, i - 3)
                nc.scalar.activation(relu[:, i % 4, :], net.ps[:, i % 4, :], ACT.Relu).then_inc(relu_ready, 1)

        @block.gpsimd
        def _(pool):
            nc.gpsimd.tensor_tensor(net.x_all, net.x_all, net.row("L1_b_o", 0).unsqueeze(1).to_broadcast([P, T, D]),
                                    ALU.add).then_inc(biased, 1)

        @block.vector
        def _(dve):
            link = linker(dve, dve_link)
            for step in (2, 3, 4):
                rows_step(dve, link, 0, step)
            for g in range(G + 1):
                if g % n == 2:
                    t0 = HT * (g // n)
                    dve.wait_ge(logits_ready, g // n + 1)
                    dve_top2(nc, dve, link, net, net.ps[:, 6, t0 * NE1:(t0 + HT) * NE1].rearrange("p (t e) -> p t e", t=HT), NE1,
                             net.small["p8"], exp_in, exp_out, g // n + 1, (1e-9, ALU.max), comb[:, t0:t0 + HT, :], t0, HT)
                if g < G:
                    if g >= 2:
                        dve.wait_ge(proj_ready, g - 1)
                    for c in range(4):
                        dve.wait_ge(relu_ready, 4 * g + c + 1)
                        nc.vector.scalar_tensor_tensor(hid[:, g % 2, c, :], net.ps[:, c, :], 0.0, relu[:, c, :],
                                                       ALU.max, ALU.mult).then_inc(hid_ready, 1)
                if 1 <= g <= 5:
                    rows_step(dve, link, 1, g - 1)
                if g >= 1:
                    v = g - 1
                    e, j = groups[v]
                    dve.wait_ge(proj_ready, v + 1)
                    if v >= 1:
                        dve.wait_ge(added, v)
                    out = net.ps[:, 4 + v % 2, :].rearrange("p (t d) -> p t d", d=D)
                    x = net.x_all[:, 4 * j:4 * j + 4, :]
                    if e < NE1:
                        for t in range(4):
                            last = nc.vector.scalar_tensor_tensor(x[:, t, :], out[:, t, :], comb[:, 4 * j + t, e:e + 1],
                                                                  x[:, t, :], ALU.mult, ALU.add)
                    else:
                        last = nc.vector.tensor_tensor(x, out, x, ALU.add)
                    last.then_inc(added, 1)
            dve.wait_ge(loaded, 32)
            nc.vector.tensor_copy(m["ids_f"], m["ids_i"])
    net.end_phase()



def layer2_attention(net):
    nc = net.nc
    (dve_link, act_link, var_ready, seed_ready, rows_ready, turned, zT_ready, proj_ready, act_emptied, dve_emptied, ids_bc,
     ptr_ready, hot_ready, scores_ready, scores_read, exp_in, exp_out, mixed, mix_turned, mix_copied, mean_ready, mean_copied,
     out_ready, weights_ready, first_mixed, picked) = net.signals(26)
    w, m = net.w2x, net.late
    emptied = (act_emptied, dve_emptied)
    z, zT, q, k, v, hot, junk, mix, mixT, meanT = (m[n] for n in ("z", "zT", "q", "k", "v", "hot", "junk", "mix", "mixT", "meanT"))
    ctxT = net.ctxT_all[:].rearrange("p b s -> p (b s)")
    s6, r = net.s6, net.small
    JUNK = junk.shape[1]
    halves = T * P // BANK
    tiles, outs = [], []
    for a in range(2):
        for j in range(halves):
            tiles.append([(0, BANK, w["k"][:, a, :], ctxT[:, j * BANK:(j + 1) * BANK])])
            outs.append(k[:, a, j * BANK:(j + 1) * BANK])
    for t in range(0, T, 2):
        tiles.append([(i * S, (i + 1) * S, ctxT[:, (t + i) * P:(t + i + 1) * P], w["v"][:]) for i in range(2)])
        outs.append(v[:, t:t + 2, :].rearrange("p t n -> p (t n)"))
    n_ctx = len(tiles)
    for a in range(2):
        for j in range(halves):
            tiles.append([(0, BANK, w["q"][:, a, :], zT[:, j * BANK:(j + 1) * BANK])])
            outs.append(q[:, a, j * BANK:(j + 1) * BANK])
    counts = evac_counts(len(tiles))
    scores = [(b, a) for b in range(B) for a in range(2)]

    def pe_mean(pe, b):
        pe.wait_ge(mix_copied, 2 * b + 2)
        for a in range(2):
            for l in range(NT):
                last = nc.tensor.matmul(net.ps[:, 4 + b // 2, (b % 2) * S:(b % 2 + 1) * S], v[:, b * NT + l, a * P:(a + 1) * P],
                                        mixT[:, 2 * b + a, l * S:(l + 1) * S], start=a == 0 and l == 0, stop=a == 1 and l == NT - 1)
        last.then_inc(mean_ready, 1)

    def copy_mean(act, j):
        act.wait_ge(mean_ready, 2 * j + 2)
        nc.scalar.copy(meanT[:, j * BANK:(j + 1) * BANK], net.ps[:, 4 + j, :]).then_inc(mean_copied, 1)

    with nc.Block() as block:
        @block.sync
        def _(sp):
            d, wi, wo = net.d, net.fc, net.proj
            sp.dma_start(wi[:, NE3, :], d["res_in"]).then_inc(net.w3_res, 16)
            sp.dma_start(wo[:, NE3, :, :], d["res_out"]).then_inc(net.w3_res, 16)
            sp.dma_start(wi[:, 0:NE3, :], d["inter"]).then_inc(net.w3_experts, 16)
            sp.dma_start(wo[:, 0:NE3, :, :], d["output"]).then_inc(net.w3_experts, 16)

        @block.tensor
        def _(pe):
            pe.wait_ge(net.w2_loaded, net.w2_count)
            for j in range(halves):
                nc.tensor.matmul(net.ps[:, 6 + j, :], net.ones[0:1, :], m["ids_f"][:, j * BANK:(j + 1) * BANK],
                                 start=True, stop=True).then_inc(ids_bc, 1)
            for i, products in enumerate(tiles):
                if i == n_ctx:
                    pe.wait_ge(rows_ready, 1)
                    pe_turn_rows(nc, net, z, (4, 5), turned)
                    pe.wait_ge(zT_ready, halves)
                if i >= 4:
                    pe.wait_ge(emptied[i % 2], (i - 4) // 2 + 1)
                for a, b, stationary, moving in products:
                    last = nc.tensor.matmul(net.ps[:, i % 4, a:b], stationary, moving, start=True, stop=True)
                last.then_inc(proj_ready, 1)
            for which in range(2):
                pe.wait_ge(emptied[which], counts[which])
            for i, (b, a) in enumerate(scores):
                if i >= 4:
                    pe.wait_ge(scores_read, i - 3)
                for t in range(NT):
                    c = b * S + t * P
                    last = nc.tensor.matmul(net.ps[:, i % 4, t * S:(t + 1) * S], q[:, a, c:c + P],
                                            k[:, a, b * S:(b + 1) * S], start=True, stop=True)
                last.then_inc(scores_ready, 1)
            for i, (b, a) in enumerate(scores):
                pe.wait_ge(mixed, i + 1)
                if i >= 4:
                    pe.wait_ge(mix_copied, i - 3)
                for l in range(NT):
                    for t in range(NT):
                        last = nc.tensor.transpose(net.ps[:, i % 4, (l * NT + t) * P:(l * NT + t + 1) * P],
                                                   mix[:, i, t, l * P:(l + 1) * P], net.ident[:])
                last.then_inc(mix_turned, 1)
                if a == 1 and b >= 1:
                    pe_mean(pe, b - 1)
            pe_mean(pe, B - 1)
            for j in range(halves):
                pe.wait_ge(mean_copied, j + 1)
                for t in range(4 * j, 4 * j + 4):
                    last = nc.tensor.matmul(net.ps[:, 6 + j, (t % 4) * P:(t % 4 + 1) * P], meanT[:, t * P:(t + 1) * P], w["o"][:],
                                            start=True, stop=True)
                last.then_inc(out_ready, 1)

        @block.gpsimd
        def _(pool):
            pool.wait_ge(ptr_ready, 1)
            for t in range(T):
                nc.gpsimd.tensor_scalar(hot[:, 2, t, :], net.iota[:, 0:S], r["ptr"][:, 2, t:t + 1], None, ALU.is_equal).then_inc(hot_ready, 1)

        @block.scalar
        def _(act):
            link = linker(act, act_link)
            act_rsqrt_seed(nc, act, link, net, T, var_ready, 1, seed_ready)
            empty_projections(nc, act, nc.scalar.copy, net, outs[:n_ctx], 4, 0, proj_ready, emptied)
            for j in range(halves):
                act.wait_ge(turned, j + 1)
                nc.scalar.copy(zT[:, j * BANK:(j + 1) * BANK], net.ps[:, 4 + j, :]).then_inc(zT_ready, 1)
            for i in range(n_ctx, len(outs), 2):
                act.wait_ge(proj_ready, i + 1)
                nc.scalar.copy(outs[i], net.ps[:, i % 4, :]).then_inc(emptied[0], 1)
            act.wait_ge(exp_in, 1)
            nc.scalar.activation(s6[:], s6[:], ACT.Exp).then_inc(exp_out, 1)
            act.wait_ge(weights_ready, 1)
            for i, (b, a) in enumerate(scores):
                for t in range(NT):
                    bt = b * NT + t
                    last = nc.scalar.activation(mix[:, i, t, :], hot[:, 0, bt, :], ACT.Copy, scale=s6[:, a, bt, 0:1])
                last.then_inc(first_mixed, 1)
            for i in range(len(scores)):
                act.wait_ge(mix_turned, i + 1)
                nc.scalar.copy(mixT[:, i, :], net.ps[:, i % 4, :]).then_inc(mix_copied, 1)
                if i % 4 == 3 and i >= 7:
                    copy_mean(act, i // 4 - 1)
            copy_mean(act, halves - 1)

        @block.vector
        def _(dve):
            link = linker(dve, dve_link)
            link(nc.vector.tensor_copy(r["ptr"][:, 3, :], net.ptr_i[:]))
            for w_ in range(3):
                last = nc.vector.tensor_scalar(r["ptr"][:, w_, :], r["ptr"][:, 3, :], float(w_), 0.0, ALU.add, ALU.max)
            link(last)
            nc.vector.tensor_scalar(r["ptr"][:, 0:3, :], r["ptr"][:, 0:3, :], float(S - 1), None, ALU.min).then_inc(ptr_ready, 1)
            dve_norm_rows(nc, dve, link, net, rows_of(net.x_all), rows_of(z), T, 1e-5, var_ready, seed_ready, 1).then_inc(rows_ready, 1)
            ones = [(k_, t) for t in range(T) for k_ in range(2)]

            def pick_ids(ts):
                for t in ts:
                    nc.vector.scalar_tensor_tensor(junk[:, t, :], net.ps[:, 6 + t // 4, (t // NT % 2) * S:(t // NT % 2 + 1) * S], 1.0,
                                                   hot[:, 0, t, :], ALU.mult, ALU.mult, accum_out=r["rel"][:, t:t + 1]).then_inc(picked, 1)
            for i in range(1, len(outs), 2):
                dve.wait_ge(proj_ready, i + 1)
                nc.vector.tensor_copy(outs[i], net.ps[:, i % 4, :]).then_inc(emptied[1], 1)
                for k_, t in ones[3 * (i // 2):3 * (i // 2) + 3]:
                    last = nc.vector.tensor_scalar(hot[:, k_, t, :], net.iota[:, 0:S], r["ptr"][:, k_, t:t + 1], None, ALU.is_equal)
                if i == 7:
                    link(last)
                    dve.wait_ge(ids_bc, halves)
                    pick_ids(range(0, 6))
            link(last)
            pick_ids(range(6, T))
            dve.wait_ge(picked, T)
            dve.wait_ge(hot_ready, T)
            for i, (b, a) in enumerate(scores):
                dve.wait_ge(scores_ready, i + 1)
                if i >= 2:
                    dve.wait_ge(scores_read, i - 1)
                for t in range(NT):
                    for k_ in range(3):
                        last = nc.vector.scalar_tensor_tensor(junk[:, 6 * (i % 2) + 3 * t + k_, :], net.ps[:, i % 4, t * S:(t + 1) * S],
                                                              D ** -0.5, hot[:, k_, b * NT + t, :], ALU.mult, ALU.mult,
                                                              accum_out=s6[:, a, b * NT + t, k_:k_ + 1])
                last.then_inc(scores_read, 1)
            dve.wait_ge(scores_read, len(scores))
            v1, v2, val, eq = s6[:, 0, :, 1], s6[:, 0, :, 2], r["val"], r["is"]
            nc.vector.tensor_tensor(val[:, 0, :], v1, v2, ALU.add)
            nc.vector.tensor_tensor(val[:, 1, :], v1, v2, ALU.max)
            nc.vector.tensor_tensor(val[:, 4, :], v1, v2, ALU.subtract)
            for k_ in range(5):
                nc.vector.tensor_scalar(eq[:, k_, :], r["rel"][:], float(k_), None, ALU.is_equal)
            link(nc.vector.tensor_scalar(val[:, 2, :], v1, -1.0, None, ALU.mult))
            nc.vector.tensor_tensor(val[:, 3, :], val[:, 2, :], v2, ALU.max)
            link(nc.vector.tensor_scalar(val[:, 5, :], val[:, 4, :], -1.0, None, ALU.mult))
            link(nc.vector.tensor_tensor(val[:, 4, :], val[:, 4, :], val[:, 5, :], ALU.max))
            link(nc.vector.tensor_tensor(val[:, 0:5, :], val[:, 0:5, :], eq[:], ALU.mult))
            nc.vector.reduce_sum(r["new"][:], val[:, 0:5, :].rearrange("p k t -> p t k"), AX.X)
            link(nc.vector.reduce_sum(r["any"][:], eq[:].rearrange("p k t -> p t k"), AX.X))
            link(nc.vector.tensor_scalar(r["any"][:], r["any"][:], -1.0, 1.0, ALU.mult, ALU.add))
            link(nc.vector.tensor_tensor(r["any"][:], r["any"][:], s6[:, 0, :, 0], ALU.mult))
            link(nc.vector.tensor_tensor(s6[:, 0, :, 0], r["any"][:], r["new"][:], ALU.add))
            flat = s6[:].rearrange("p a t w -> p (a t) w")
            mx, sm = r["mx"][:, 0:2 * T], r["sm"][:, 0:2 * T]
            link(nc.vector.reduce_max(mx, flat, AX.X))
            nc.vector.tensor_tensor(flat, flat, spread(mx, 3), ALU.subtract).then_inc(exp_in, 1)
            dve.wait_ge(exp_out, 1)
            link(nc.vector.reduce_sum(sm, flat, AX.X))
            link(nc.vector.reciprocal(sm, sm))
            by_path = sm.rearrange("p (a t) -> p a t", a=2)
            link(nc.vector.tensor_tensor(by_path, by_path, spread(net.share[:], T), ALU.mult))
            nc.vector.tensor_tensor(flat, flat, spread(sm, 3), ALU.mult).then_inc(weights_ready, 1)
            dve.wait_ge(weights_ready, 1)
            for i, (b, a) in enumerate(scores):
                dve.wait_ge(first_mixed, i + 1)
                for k_ in (1, 2):
                    for t in range(NT):
                        bt = b * NT + t
                        last = nc.vector.scalar_tensor_tensor(mix[:, i, t, :], hot[:, k_, bt, :], s6[:, a, bt, k_:k_ + 1],
                                                              mix[:, i, t, :], ALU.mult, ALU.add)
                    if k_ == 1:
                        link(last)
                last.then_inc(mixed, 1)
            for j in range(halves):
                dve.wait_ge(out_ready, j + 1)
                x = net.x_all[:, 4 * j:4 * j + 4, :]
                nc.vector.scalar_tensor_tensor(x, net.ps[:, 6 + j, :].rearrange("p (t d) -> p t d", d=D), net.row("gain", 0, 1),
                                               x, ALU.mult, ALU.add)
    net.end_phase()



def layer2_experts(net):
    nc = net.nc
    (dve_link, act_link, var_ready, seed_ready, rows_ready, turned, cols_ready, logits_ready, exp_in, exp_out,
     hid_in, hid_copied, stats_taken, rstd_ready, biased, dve_normed, act_normed, hid_turned, hid_ready, out_ready, summed) = net.signals(21)
    m = net.late
    z, hn, zT, hnT, hid, hidT, sums = (m[n] for n in ("z", "hn", "zT", "hnT", "hid_rows", "hidT", "sums"))
    comb = net.comb[:, :, 0:NE2]
    halves = T * P // BANK
    cut = lambda t, e: hid[:, t, e * H2:(e + 1) * H2]
    mine = {e: [(t, k) for t in range(T) for k in range(NE2) if (k < 2 or k == 2 and t % 2 == 1) == (e == "dve")] for e in ("dve", "act")}
    jobs = [(j, c) for j in range(halves) for c in range(2 * NE2)]

    with nc.Block() as block:
        @block.tensor
        def _(pe):
            pe.wait_ge(rows_ready, 1)
            pe_turn_rows(nc, net, z, (6, 7), turned)
            pe.wait_ge(cols_ready, halves)
            for t in range(T):
                if t >= 3:
                    pe.wait_ge(hid_copied, t - 2)
                for half in range(2):
                    last = nc.tensor.matmul(net.ps[:, 2 * (t % 3) + half, :], zT[:, t * P:(t + 1) * P],
                                            net.w2f["in"][:, half * BANK:(half + 1) * BANK], start=True, stop=True)
                last.then_inc(hid_in, 1)
            pe.wait_ge(rows_ready, 2)
            pe_turn_rows(nc, net, hn, (6, 7), turned)
            pe.wait_ge(cols_ready, 2 * halves)
            for t in range(T):
                last = nc.tensor.matmul(net.ps[:, 6, t * NE2:(t + 1) * NE2], hnT[:, t * P:(t + 1) * P], net.router2[:],
                                        start=True, stop=True)
            last.then_inc(logits_ready, 1)
            pe.wait_ge(hid_copied, T)
            for i in range(len(jobs) + 4):
                if i < len(jobs):
                    j, c = jobs[i]
                    if i >= 3:
                        pe.wait_ge(hid_ready, i - 2)
                    for t in range(4 * j, 4 * j + 4):
                        for engine, normed in (("dve", dve_normed), ("act", act_normed)):
                            if (t, c // 2) in mine[engine]:
                                pe.wait_ge(normed, mine[engine].index((t, c // 2)) + 1)
                        last = nc.tensor.transpose(net.ps[:, i % 3, (t % 4) * P:(t % 4 + 1) * P], hid[:, t, c * P:(c + 1) * P], net.ident[:])
                    last.then_inc(hid_turned, 1)
                if i >= 4 and i % 2 == 1:
                    n = (i - 4) // 2
                    j, e = divmod(n, NE2)
                    pe.wait_ge(hid_ready, 2 * n + 2)
                    if n >= 3:
                        pe.wait_ge(summed, n - 2)
                    for t in range(4):
                        for c in range(2):
                            last = nc.tensor.matmul(net.ps[:, 3 + n % 3, t * P:(t + 1) * P],
                                                    hidT[:, 2 * e + c, (4 * j + t) * P:(4 * j + t + 1) * P],
                                                    net.w2f["out"][:, 2 * e + c, :], start=c == 0, stop=c == 1)
                    last.then_inc(out_ready, 1)

        @block.scalar
        def _(act):
            link = linker(act, act_link)
            act_rsqrt_seed(nc, act, link, net, T, var_ready, 1, seed_ready)
            for j in range(halves):
                act.wait_ge(turned, j + 1)
                nc.scalar.copy(zT[:, j * BANK:(j + 1) * BANK], net.ps[:, 6 + j, :]).then_inc(cols_ready, 1)
            act_rsqrt_seed(nc, act, link, net, T, var_ready, 2, seed_ready)
            for t in range(T):
                act.wait_ge(hid_in, t + 1)
                nc.scalar.copy(hid[:, t, :], net.ps[:, 2 * (t % 3):2 * (t % 3) + 2, :].rearrange("p b n -> p (b n)")).then_inc(hid_copied, 1)
            for j in range(halves):
                act.wait_ge(turned, halves + j + 1)
                nc.scalar.activation(hnT[:, j * BANK:(j + 1) * BANK], net.ps[:, 6 + j, :], ACT.Identity, scale=net.col("L2_rn_g", 0),
                                     bias=net.col("L2_rn_b", 0)).then_inc(cols_ready, 1)
            act_rsqrt_seed(nc, act, link, net, T * NE2, var_ready, 3, seed_ready)
            act.wait_ge(rstd_ready, 1)

            def normalise(ts):
                for t, e in mine["act"]:
                    if t in ts:
                        i = t * NE2 + e
                        nc.scalar.activation(cut(t, e), cut(t, e), ACT.Identity, scale=net.rstd[:, i:i + 1],
                                             bias=net.shift[:, i:i + 1]).then_inc(act_normed, 1)
            normalise(range(0, HT))
            for i, (j, c) in enumerate(jobs):
                if i == 4:
                    act.wait_ge(exp_in, 1)
                    e2 = net.small["e"][:, :, 0:NE2]
                    nc.scalar.activation(e2, e2, ACT.Exp).then_inc(exp_out, 1)
                if i == 6:
                    normalise(range(HT, T))
                act.wait_ge(hid_turned, i + 1)
                nc.scalar.activation(hidT[:, c, j * BANK:(j + 1) * BANK], net.ps[:, i % 3, :], ACT.Relu,
                                     scale=net.col("L2_ln_g", c), bias=net.col("L2_ln_b", c)).then_inc(hid_ready, 1)
                if j == 1 and c == 4:
                    act_rsqrt_seed(nc, act, link, net, HT, var_ready, 4, seed_ready)
            act_rsqrt_seed(nc, act, link, net, HT, var_ready, 5, seed_ready)

        @block.gpsimd
        def _(pool):
            pool.wait_ge(rows_ready, 1)
            nc.gpsimd.tensor_tensor(net.x_all, net.x_all, net.row("L2_on_b", 0).unsqueeze(1).to_broadcast([P, T, D]),
                                    ALU.add).then_inc(biased, 1)

        @block.vector
        def _(dve):
            link = linker(dve, dve_link)
            dve_norm_rows(nc, dve, link, net, rows_of(net.x_all), rows_of(z), T, 1e-5, var_ready, seed_ready, 1).then_inc(rows_ready, 1)
            dve.wait_ge(rows_ready, 1)
            dve_norm_rows(nc, dve, link, net, rows_of(z), rows_of(hn), T, 1e-5, var_ready, seed_ready, 2).then_inc(rows_ready, 1)
            dve.wait_ge(rows_ready, 2)
            def aggregate(t):
                dve.wait_ge(stats_taken, t + 1)
                for i in range(t * NE2, (t + 1) * NE2):
                    last = nc.vector.bn_aggr(net.mv[:, i, :], net.stats[:, i, :])
                return last
            for t in range(T):
                dve.wait_ge(hid_copied, t + 1)
                for e in range(NE2):
                    last = nc.vector.bn_stats(net.stats[:, t * NE2 + e, :], cut(t, e))
                last.then_inc(stats_taken, 1)
                if t >= 1:
                    aggregate(t - 1)
            link(aggregate(T - 1))
            nc.vector.tensor_scalar(net.veps[:, 0:T * NE2], net.mv[:, 0:T * NE2, 1], 1e-5, None, ALU.add).then_inc(var_ready, 1)
            dve_rsqrt(nc, dve, link, net, T * NE2, seed_ready, 3, net.rstd[:])
            nc.vector.scalar_tensor_tensor(net.shift[:], net.mv[:, :, 0], -1.0, net.rstd[:], ALU.mult, ALU.mult).then_inc(rstd_ready, 1)
            for t, e in mine["dve"]:
                i = t * NE2 + e
                nc.vector.tensor_scalar(cut(t, e), cut(t, e), net.mv[:, i, 0:1], net.rstd[:, i:i + 1],
                                        ALU.subtract, ALU.mult).then_inc(dve_normed, 1)
            dve.wait_ge(logits_ready, 1)
            dve_top2(nc, dve, link, net, net.ps[:, 6, 0:T * NE2].rearrange("p (t e) -> p t e", t=T), NE2, net.small["p4"],
                     exp_in, exp_out, 1, (1e-8, ALU.add), comb)
            for n in range(halves * NE2):
                j, e = divmod(n, NE2)
                dve.wait_ge(out_ready, n + 1)
                for t in range(4 * j, 4 * j + 4):
                    src = net.ps[:, 3 + n % 3, (t % 4) * P:(t % 4 + 1) * P]
                    if e == 0:
                        last = nc.vector.tensor_scalar(sums[:, t, :], src, comb[:, t, e:e + 1], None, ALU.mult)
                    else:
                        last = nc.vector.scalar_tensor_tensor(sums[:, t, :], src, comb[:, t, e:e + 1], sums[:, t, :], ALU.mult, ALU.add)
                last.then_inc(summed, 1)
                dve.wait_ge(summed, n + 1)
                if e == NE2 - 1:
                    ts = slice(HT * j, HT * j + HT)
                    o, x = hn[:, ts, :], net.x_all[:, ts, :]
                    link(dve_norm_rows(nc, dve, link, net, rows_of(sums[:, ts, :]), rows_of(o), HT, 1e-5, var_ready, seed_ready, 4 + j))
                    link(nc.vector.tensor_tensor(o, o, net.row("L2_on_g", 0).unsqueeze(1).to_broadcast([P, HT, D]), ALU.mult))
                    dve.wait_ge(biased, 1)
                    nc.vector.tensor_tensor(x, x, o, ALU.add)
    net.end_phase()



def layer3_attention(net):
    nc = net.nc
    (dve_link, act_link, var_ready, seed_ready, rows_ready, turned, zT_ready, scores_ready, masked, exped, normed, probs_turned,
     probs_copied, out_ready) = net.signals(14)
    keys = [P, S]
    cols = [0, P]
    blocks = [(0, 0), (1, 0), (1, 1)]
    m = net.late
    z, zT, probs, probsT = m["z"], m["zT"], m["probs3"], m["probsT3"]
    units = [(b, t) for b in range(B) for t in range(NT)]
    halves = T * P // BANK

    with nc.Block() as block:
        @block.sync
        def _(sp):
            d = net.d
            sp.dma_start(net.before, d["before"]).then_inc(net.w3_gate, 16)
            sp.dma_start(net.gate_w, d["gate"]).then_inc(net.w3_gate, 16)
            sp.dma_start(net.w2f["in"][:], d["iota"]).then_inc(net.w3_gate, 16)

        @block.tensor
        def _(pe):
            for u, (b, t) in enumerate(units):
                if u % HT == 0:
                    pe.wait_ge(rows_ready, u // HT + 1)
                    pe_turn_rows(nc, net, z, (6 + u // HT,), turned, (u // HT,))
                    pe.wait_ge(zT_ready, u // 4 + 1)
                nc.tensor.matmul(net.ps[:, b, cols[t]:cols[t] + keys[t]], zT[:, u * P:(u + 1) * P], net.ctxT_all[:, b, 0:keys[t]],
                                 start=True, stop=True).then_inc(scores_ready, 1)
            for b in range(B):
                for j, (t, k) in enumerate(blocks):
                    pe.wait_ge(normed, b * NT + t + 1)
                    last = nc.tensor.transpose(net.ps[:, 4 + b, j * P:(j + 1) * P],
                                               probs[:, b, cols[t] + k * P:cols[t] + (k + 1) * P], net.ident[:])
                last.then_inc(probs_turned, 1)
            pe.wait_ge(masked, T)
            for b in range(B):
                pe.wait_ge(probs_copied, b + 1)
                for j, (t, k) in enumerate(blocks):
                    last = nc.tensor.matmul(net.ps[:, b // 2, ((b % 2) * NT + t) * P:((b % 2) * NT + t + 1) * P],
                                            probsT[:, b, j * P:(j + 1) * P], net.ctx_all[:, b * NT + k, :], start=k == 0, stop=k == t)
                if b % 2 == 1:
                    last.then_inc(out_ready, 1)

        @block.scalar
        def _(act):
            link = linker(act, act_link)
            for j in range(halves):
                act_rsqrt_seed(nc, act, link, net, HT, var_ready, j + 1, seed_ready)
                act.wait_ge(turned, j + 1)
                nc.scalar.copy(zT[:, j * BANK:(j + 1) * BANK], net.ps[:, 6 + j, :]).then_inc(zT_ready, 1)
            for u, (b, t) in enumerate(units):
                act.wait_ge(masked, u + 1)
                x = probs[:, b, cols[t]:cols[t] + keys[t]]
                nc.scalar.activation(x, x, ACT.Exp, bias=net.negmax[:, b, t:t + 1], scale=-1.0,
                                     accum_out=net.sums[:, b, t:t + 1]).then_inc(exped, 1)
            for b in range(B):
                act.wait_ge(probs_turned, b + 1)
                nc.scalar.copy(probsT[:, b, :], net.ps[:, 4 + b, 0:3 * P]).then_inc(probs_copied, 1)

        @block.vector
        def _(dve):
            link = linker(dve, dve_link)
            for j in range(halves):
                dve_norm_half(nc, dve, link, net, net.x_all, z, j, 1e-5, var_ready, seed_ready, j + 1).then_inc(rows_ready, 1)
                dve.wait_ge(rows_ready, j + 1)
            for step in range(T + 2):
                if step < T:
                    b, t = units[step]
                    dve.wait_ge(scores_ready, NT * (b + 1))
                    c = slice(cols[t], cols[t] + keys[t])
                    nc.vector.tensor_tensor_reduce(out=probs[:, b, c], in0=net.ps[:, b, c], in1=net.causal[:, c],
                                                   scale=-D ** -0.5, scalar=-MASKED, op0=ALU.add, op1=ALU.min,
                                                   accum_out=net.negmax[:, b, t:t + 1]).then_inc(masked, 1)
                if step >= 2:
                    b, t = units[step - 2]
                    dve.wait_ge(exped, step - 1)
                    x = probs[:, b, cols[t]:cols[t] + keys[t]]
                    link(nc.vector.reciprocal(net.recip[:, b, t:t + 1], net.sums[:, b, t:t + 1]))
                    nc.vector.tensor_scalar(x, x, net.recip[:, b, t:t + 1], None, ALU.mult).then_inc(normed, 1)
            for j in range(halves):
                dve.wait_ge(out_ready, j + 1)
                x = net.x_all[:, 4 * j:4 * j + 4, :]
                nc.vector.tensor_tensor(x, x, net.ps[:, j, :].rearrange("p (t d) -> p t d", d=D), ALU.add)
    net.end_phase()



def layer3_experts(net, out):
    nc = net.nc
    (dve_link, act_link, pool_link, var_ready, seed_ready, rows_ready, turned, cols_ready, logits_ready, exp_in, exp_out,
     mask_ready, places_ready, slots_ready, diag_ready, spread_ready, spread_copied, hot_ready, take_ready, res_in, res_gelu,
     sent, sent_copied, inter_ready, inter_gelu, expert_ready, expert_copied, mixed, final, written,
     res_out, res_read) = net.signals(32)
    w_res, w_gate, w_experts = net.w3_res, net.w3_gate, net.w3_experts
    at, start = {}, 0
    for name, n in dict(hot=T * NE3 * CAP, take=NE3 * T * P, a=T * D, aT=T * P, z=T * D, res=4 * T * P, sent=NE3 * CAP,
                        eo=NE3 * D, inter=2 * 4 * CAP, slots=T * P, diag=T * P).items():
        at[name] = net.arena[:, start:start + n]
        start += n
    rows = lambda name: at[name].rearrange("p (t d) -> p t d", t=T)
    a_rows, z_rows, eo = rows("a"), rows("z"), rows("eo")
    hot = at["hot"].rearrange("p (t n) -> p t n", t=T)
    take = at["take"].rearrange("p (e s) -> p e s", e=NE3)
    res = at["res"].rearrange("p (c s) -> p c s", c=4)
    inter = at["inter"].rearrange("p (a c s) -> p a c s", a=2, c=4)
    diag = rows("diag")
    wi, wo = net.fc, net.proj
    iota, before, gate_w = net.w2f["in"], net.before, net.gate_w
    r = net.small
    HALF = T * P // BANK

    def residual_rows(pe, j):
        pe.wait_ge(res_gelu, 4 * HALF)
        for t in range(4 * j, 4 * j + 4):
            for c in range(4):
                last = nc.tensor.matmul(net.ps[:, 6 + j, (t % 4) * P:(t % 4 + 1) * P], res[:, c, t * P:(t + 1) * P],
                                        wo[:, NE3, c, :], start=c == 0, stop=c == 3)
        last.then_inc(res_out, 1)

    with nc.Block() as block:
        @block.sync
        def _(sp):
            for t in range(T):
                sp.wait_ge(final, t + 1)
                sp.dma_start(out[t // NT, (t % NT) * P:(t % NT + 1) * P, :], net.x_all[:, t, :]).then_inc(written, 16)
            sp.wait_ge(written, 16 * T)

        @block.tensor
        def _(pe):
            pe.wait_ge(w_gate, 48)
            pe.wait_ge(w_res, 32)
            for i in range(4 * HALF):
                j, c = divmod(i, 4)
                if i in (0, 2):
                    n = i // 2
                    pe.wait_ge(rows_ready, n + 1)
                    pe_turn_rows(nc, net, a_rows, (n,), turned, (n,))
                    pe.wait_ge(cols_ready, n + 1)
                    for t in range(HT * n, HT * n + HT):
                        last = nc.tensor.matmul(net.ps[:, 2, t * 10:(t + 1) * 10], at["aT"][:, t * P:(t + 1) * P], gate_w,
                                                start=True, stop=True)
                    last.then_inc(logits_ready, 1)
                if i >= 4:
                    pe.wait_ge(res_gelu, i - 3)
                nc.tensor.matmul(net.ps[:, 4 + i % 4, :], wi[:, NE3, c * P:(c + 1) * P], at["aT"][:, j * BANK:(j + 1) * BANK],
                                 start=True, stop=True).then_inc(res_in, 1)
            pe.wait_ge(mask_ready, 1)
            mask = r["mask"]
            flat = net.ps[:, 3, 0:T * NE3]
            nc.tensor.matmul(flat, before, mask[:].rearrange("p t e -> p (t e)"), start=True, stop=False)
            for t in range(T - 1):
                last = nc.tensor.matmul(net.ps[:, 3, (t + 1) * NE3:T * NE3].rearrange("p (t e) -> p t e", e=NE3), net.ones[:],
                                        mask[:, t, :].unsqueeze(1).to_broadcast([P, T - 1 - t, NE3]), start=False, stop=t == T - 2)
            last.then_inc(places_ready, 1)
            residual_rows(pe, 0)
            pe.wait_ge(diag_ready, 1)
            for j in range(HALF):
                nc.tensor.matmul(net.ps[:, j, :], net.ones[:], at["diag"][:, j * BANK:(j + 1) * BANK], start=True, stop=True).then_inc(spread_ready, 1)
            residual_rows(pe, 1)
            pe.wait_ge(res_gelu, 4 * HALF)
            for t in range(T):
                pe.wait_ge(hot_ready, t + 1)
                for j in range(2):
                    last = nc.tensor.matmul(net.ps[:, 4 + j, :], a_rows[:, t, :], hot[:, t, j * BANK:(j + 1) * BANK],
                                            start=t == 0, stop=t == T - 1)
            last.then_inc(sent, 1)
            pe.wait_ge(sent_copied, 2)
            pe.wait_ge(w_experts, 32)
            for e in range(NE3 + 1):
                if e < NE3:
                    if e == 0:
                        pe.wait_ge(res_read, HALF)
                    if e >= 2:
                        pe.wait_ge(inter_gelu, 4 * (e - 1))
                    for c in range(4):
                        last = nc.tensor.matmul(net.ps[:, 6 + e % 2, c * CAP:(c + 1) * CAP], wi[:, e, c * P:(c + 1) * P],
                                                at["sent"][:, e * CAP:(e + 1) * CAP], start=True, stop=True)
                    last.then_inc(inter_ready, 1)
                if e >= 1:
                    v = e - 1
                    pe.wait_ge(inter_gelu, 4 * (v + 1))
                    if v >= 2:
                        pe.wait_ge(expert_copied, v - 1)
                    for c in range(4):
                        last = nc.tensor.matmul(net.ps[:, 4 + v % 2, 0:D], inter[:, v % 2, c, :], wo[:, v, c, :], start=c == 0, stop=c == 3)
                    last.then_inc(expert_ready, 1)
            pe.wait_ge(expert_copied, NE3)
            pe.wait_ge(take_ready, NE3)
            for t in range(T):
                if t >= 4:
                    pe.wait_ge(final, t - 3)
                bank = t % 4
                for e in range(NE3):
                    last = nc.tensor.matmul(net.ps[:, bank, 0:D], take[:, e, t * P:(t + 1) * P], eo[:, e, :], start=e == 0, stop=e == NE3 - 1)
                last.then_inc(mixed, 1)

        @block.scalar
        def _(act):
            link = linker(act, act_link)
            for j in range(HALF):
                act_rsqrt_seed(nc, act, link, net, HT, var_ready, 2 * j + 1, seed_ready)
                act_rsqrt_seed(nc, act, link, net, HT, var_ready, 2 * j + 2, seed_ready)
                act.wait_ge(turned, j + 1)
                nc.scalar.activation(at["aT"][:, j * BANK:(j + 1) * BANK], net.ps[:, j, :], ACT.Identity, scale=net.col("L3_nw", 0),
                                     bias=net.col("L3_nb", 0)).then_inc(cols_ready, 1)
            act.wait_ge(exp_in, 1)
            nc.scalar.activation(r["e"][:], r["e"][:], ACT.Exp).then_inc(exp_out, 1)
            for i in range(4 * HALF):
                j, c = divmod(i, 4)
                act.wait_ge(res_in, i + 1)
                nc.scalar.activation(res[:, c, j * BANK:(j + 1) * BANK], net.ps[:, 4 + i % 4, :], ACT.Gelu_apprx_tanh,
                                     bias=net.col("L3_rb", c)).then_inc(res_gelu, 1)
            for j in range(HALF):
                act.wait_ge(spread_ready, j + 1)
                nc.scalar.copy(at["slots"][:, j * BANK:(j + 1) * BANK], net.ps[:, j, :]).then_inc(spread_copied, 1)
            act.wait_ge(sent, 1)
            for j in range(2):
                nc.scalar.activation(at["sent"][:, j * BANK:(j + 1) * BANK], net.ps[:, 4 + j, :], ACT.Identity, scale=net.col("L3_nw", 0),
                                     bias=net.col("L3_nb", 0)).then_inc(sent_copied, 1)
            for e in range(NE3):
                act.wait_ge(inter_ready, e + 1)
                if e >= 2:
                    act.wait_ge(expert_ready, e - 1)
                for c in range(4):
                    nc.scalar.activation(inter[:, e % 2, c, :], net.ps[:, 6 + e % 2, c * CAP:(c + 1) * CAP], ACT.Gelu_apprx_tanh,
                                         bias=net.col("L3_b", 4 * e + c)).then_inc(inter_gelu, 1)

        @block.gpsimd
        def _(pool):
            pool.wait_ge(spread_copied, HALF)
            for e in range(NE3):
                nc.gpsimd.tensor_scalar(take[:, e, :], at["slots"], net.col("L3_slot", e), None, ALU.is_equal).then_inc(take_ready, 1)

        @block.vector
        def _(dve):
            link = linker(dve, dve_link)
            dve.wait_ge(w_gate, 48)
            for j in range(HALF):
                link(dve_norm_half(nc, dve, link, net, net.x_all, z_rows, j, 1e-5, var_ready, seed_ready, 2 * j + 1))
                dve_norm_half(nc, dve, link, net, z_rows, a_rows, j, 1e-12, var_ready, seed_ready, 2 * j + 2).then_inc(rows_ready, 1)
                dve.wait_ge(rows_ready, j + 1)
            link(nc.vector.tensor_tensor(net.x_all, net.x_all, z_rows, ALU.add))
            dve.wait_ge(logits_ready, HALF)
            logits = net.ps[:, 2, 0:T * 10].rearrange("p (t e) -> p t e", t=T)
            sm, mx, e10, top, idx, idxf = r["sm"], r["mx"], r["e"], r["top"], r["idx"], r["idxf"]
            parts = ((slice(0, NE3), slice(0, T)), (slice(NE3, NE3 + 2), slice(T, 2 * T)))
            for e, m in parts:
                last = nc.vector.reduce_max(mx[:, m], logits[:, :, e], AX.X)
            link(last)
            for e, m in parts:
                last = nc.vector.tensor_tensor(e10[:, :, e], logits[:, :, e], spread(mx[:, m], e.stop - e.start), ALU.subtract)
            last.then_inc(exp_in, 1)
            dve.wait_ge(exp_out, 1)
            for e, m in parts:
                last = nc.vector.reduce_sum(sm[:, m], e10[:, :, e], AX.X)
            link(last)
            link(nc.vector.reciprocal(sm[:], sm[:]))
            link(nc.vector.tensor_tensor(e10[:, :, 8:10], e10[:, :, 8:10], spread(sm[:, T:2 * T], 2), ALU.mult))
            link(nc.vector.tensor_tensor(r["p8"][:], e10[:, :, 0:NE3], spread(sm[:, 0:T], NE3), ALU.mult))
            for t in range(T):
                last = nc.vector.max(top[:, t, :], r["p8"][:, t, :])
            link(last)
            for t in range(T):
                last = nc.vector.max_index(idx[:, t, :], top[:, t, :], r["p8"][:, t, :])
            link(last)
            link(nc.vector.tensor_copy(idxf[:, :, 0:1], idx[:, :, 0:1]))
            nc.vector.tensor_tensor(r["mask"][:], net.iota[:, 0:NE3].unsqueeze(1).to_broadcast([P, T, NE3]), spread(idxf[:, :, 0], NE3),
                                    ALU.is_equal).then_inc(mask_ready, 1)
            dve.wait_ge(places_ready, 1)
            link(nc.vector.tensor_tensor(r["place"][:], net.ps[:, 3, 0:T * NE3].rearrange("p (t e) -> p t e", t=T), r["mask"][:], ALU.mult))
            loc, slot = mx[:, 0:T], mx[:, T:2 * T]
            link(nc.vector.reduce_sum(loc, r["place"][:], AX.X))
            link(nc.vector.scalar_tensor_tensor(slot, idxf[:, :, 0], float(CAP), loc, ALU.mult, ALU.add))
            link(nc.vector.tensor_scalar(loc, loc, float(CAP), None, ALU.is_lt))
            link(nc.vector.tensor_scalar(slot, slot, 1.0, None, ALU.add))
            link(nc.vector.tensor_tensor(slot, slot, loc, ALU.mult))
            link(nc.vector.tensor_scalar(slot, slot, -1.0, None, ALU.add))
            for t in range(T):
                last = nc.vector.tensor_scalar(diag[:, t, :], net.ident[:], slot[:, t:t + 1], None, ALU.mult)
            last.then_inc(diag_ready, 1)
            for t in range(T):
                nc.vector.tensor_scalar(hot[:, t, :], iota[:], slot[:, t:t + 1], None, ALU.is_equal).then_inc(hot_ready, 1)
            for j in range(HALF):
                dve.wait_ge(res_out, j + 1)
                link(nc.vector.tensor_tensor(z_rows[:, 4 * j:4 * j + 4, :], net.ps[:, 6 + j, :].rearrange("p (t d) -> p t d", d=D),
                                             net.row("L3_rob", 0).unsqueeze(1).to_broadcast([P, 4, D]), ALU.add))
                dve.sem_inc(res_read, 1)
            for t in range(T):
                last = nc.vector.scalar_tensor_tensor(net.x_all[:, t, :], z_rows[:, t, :], e10[:, t, 8:9], net.x_all[:, t, :], ALU.mult, ALU.add)
            link(last)
            link(nc.vector.tensor_tensor(r["p8"][:, :, 0], top[:, :, 0], e10[:, :, 9], ALU.mult))
            for e in range(NE3):
                dve.wait_ge(expert_ready, e + 1)
                nc.vector.tensor_tensor(eo[:, e, :], net.ps[:, 4 + e % 2, 0:D], net.row("L3_ob", e), ALU.add).then_inc(expert_copied, 1)
            for t in range(T):
                dve.wait_ge(mixed, t + 1)
                nc.vector.scalar_tensor_tensor(net.x_all[:, t, :], net.ps[:, t % 4, 0:D], r["p8"][:, t, 0:1], net.x_all[:, t, :],
                                               ALU.mult, ALU.add).then_inc(final, 1)
    net.end_phase()


def load_local_weights(net, sp, l):
    d, w = net.d, net.wf[l]
    sp.dma_start(w["qkv"][:], d["L0_ffn_wqkv"][l, :, :]).then_inc(net.wf_loaded, 16)
    sp.dma_start(w["o"][:], d["L0_ffn_wo"][l, :, :].rearrange("(c p) n -> p c n", p=P)).then_inc(net.wf_loaded, 16)
    sp.dma_start(w["w1"][:], d["L0_ffn_w1"][l, :, :]).then_inc(net.wf_loaded, 16)
    for c, (c0, cn) in enumerate(HC):
        sp.dma_start(w["w2"][0:cn, c, :], d["L0_ffn_w2"][l, c0:c0 + cn, :]).then_inc(net.wf_loaded, 16)


def start(net):
    nc, d, m = net.nc, net.d, net.first
    dve_link, act_link, loaded, ctx_loaded, var_ready, seed_ready, rows_ready, turned = net.signals(8)
    halves = T * P // BANK
    with nc.Block() as block:
        @block.sync
        def _(sp):
            sp.dma_start(net.x_all, d["x"].rearrange("b (t p) d -> p (b t) d", p=P)).then_inc(loaded, 16)
            sp.dma_start(net.ident[:], d["ident"]).then_inc(loaded, 16)
            sp.dma_start(m["mask0_w"].rearrange("p (t k) -> p t k", t=NT), d["mask0"].rearrange("(t p) k -> p t k", p=P)).then_inc(loaded, 16)
            sp.dma_start(net.ctxT_all[:], d["ctxT"].rearrange("b d s -> d b s")).then_inc(ctx_loaded, 16)
            sp.dma_start(net.cn_all[:], d["ctx"].rearrange("b (t p) d -> p (b t) d", p=P)).then_inc(ctx_loaded, 16)
            for name in "qkv":
                sp.dma_start(net.w0[name][:], d["L0_xattn_w_" + name]).then_inc(net.w0_loaded, 16)
            sp.dma_start(net.w0["o"][:], d["L0_xattn_w_o"].rearrange("(c p) n -> p c n", p=P)).then_inc(net.w0_loaded, 16)
            for dst, name in ((m["band"], "band"), (m["causal"], "causal")):
                sp.dma_start(dst.rearrange("p (t k) -> p t k", t=NT), d[name].rearrange("(t p) k -> p t k", p=P)).then_inc(net.tables_loaded, 16)
            for dst, name in ((net.next_row, "next_row"), (net.next_tile, "next_tile")):
                sp.dma_start(dst[:], d[name]).then_inc(net.tables_loaded, 16)
            sp.dma_start(net.iota[:], d["iota"][:, 0:S]).then_inc(net.tables_loaded, 16)
            sp.dma_start(net.cols[:], d["cols"]).then_inc(net.tables_loaded, 16)
            sp.dma_start(net.rows[:], d["rows"]).then_inc(net.tables_loaded, 16)
            for table, name in ((net.cos_t, "cos"), (net.sin_t, "sin")):
                sp.dma_start(table[:, 0, :, :, :], d[name]).then_inc(net.tables_loaded, 16)
            load_local_weights(net, sp, 0)

        @block.tensor
        def _(pe):
            pe.wait_ge(rows_ready, 1)
            pe_turn_rows(nc, net, m["z"], (0, 1), turned)

        @block.scalar
        def _(act):
            nc.scalar.preload_act_table_set(LN_EXP)
            act_rsqrt_seed(nc, act, linker(act, act_link), net, T, var_ready, 1, seed_ready)
            for j in range(halves):
                act.wait_ge(turned, j + 1)
                nc.scalar.copy(net.zT_all[:, 2 * j:2 * j + 2, :].rearrange("p b s -> p (b s)"), net.ps[:, j, :])

        @block.vector
        def _(dve):
            link = linker(dve, dve_link)
            nc.vector.memset(net.x_padded[:, 0:NT, :], 0.0)
            nc.vector.memset(net.ones[:], 1.0)
            nc.vector.memset(net.ones_b[:], 1.0)
            nc.vector.memset(net.small["p4"][:], -1.0)
            nc.vector.memset(net.kmask[:], 0.0)
            dve.wait_ge(loaded, 48)
            dve_norm_rows(nc, dve, link, net, rows_of(net.x_all), rows_of(m["z"]), T, 1e-5, var_ready, seed_ready, 1).then_inc(rows_ready, 1)
            nc.vector.tensor_scalar(net.mask0[:], m["mask0_w"].bitcast(U8), MASKED, None, ALU.mult)
            dve.wait_ge(ctx_loaded, 32)
    net.end_phase()


def prepare_tables(net):
    nc, d, m = net.nc, net.d, net.first
    table_link, act_link, var_ready, seed_ready, shares_in, shares_out = net.signals(6)
    with nc.Block() as block:
        @block.sync
        def _(sp):
            sp.wait_ge(net.wf_loaded, net.wf_count)
            load_local_weights(net, sp, 1)
            sp.dma_start(net.w1["q"], d["L1_xattn_Wq"]).then_inc(net.w1_loaded, 16)
            sp.dma_start(net.w1["kv"], d["L1_xattn_Wkv"]).then_inc(net.w1_loaded, 16)
            sp.dma_start(net.w1["o"], d["L1_xattn_Wout"].rearrange("(c p) n -> p c n", p=P)).then_inc(net.w1_loaded, 16)

        @block.scalar
        def _(act):
            act_rsqrt_seed(nc, act, linker(act, act_link), net, NT, var_ready, 1, seed_ready)
            act.wait_ge(shares_in, 1)
            nc.scalar.activation(net.share[:], net.share[:], ACT.Exp).then_inc(shares_out, 1)

        @block.vector
        def _(dve):
            link = linker(dve, table_link)
            last = slice((B - 1) * NT, B * NT)
            dve_norm_rows(nc, dve, link, net, rows_of(net.x_all[:, last, :]), rows_of(net.z_padded[:, B * NT:(B + 1) * NT, :]), NT, 1e-5,
                          var_ready, seed_ready, 1)
            dve.wait_ge(net.tables_loaded, net.tables_count)
            link(nc.vector.reduce_max(net.recip[:, 0, 0:1], net.row("council", 0, 2), AX.X))
            nc.vector.tensor_scalar(net.share[:], net.row("council", 0, 2), net.recip[:, 0, 0:1], None, ALU.subtract).then_inc(shares_in, 1)
            for mask, src in ((net.causal, m["causal"]), (net.band, m["band"])):
                nc.vector.tensor_scalar(mask[:, 0:P], src[:, 0:P], MASKED, None, ALU.mult)
                nc.vector.tensor_scalar(mask[:, P:P + S], src[:, S:2 * S], MASKED, None, ALU.mult)
            for l in (1, 0):
                for a, name in enumerate(("q_scale", "k_scale")):
                    row = net.row(name, l, DH).unsqueeze(1).to_broadcast([P, NT, DH])
                    cos, sin, cos0, sin0 = (table[:, n, :, a, :] for n in (l, 0) for table in (net.cos_t, net.sin_t))
                    nc.vector.tensor_tensor(cos, cos0, row, ALU.mult)
                    nc.vector.tensor_tensor(sin[:, :, 0:32], sin0[:, :, 0:32], row[:, :, 32:64], ALU.mult)
                    nc.vector.tensor_tensor(sin[:, :, 32:64], sin0[:, :, 32:64], row[:, :, 0:32], ALU.mult)
            dve.wait_ge(shares_out, 1)
            link(nc.vector.reduce_sum(net.recip[:, 1, 0:1], net.share[:], AX.X))
            link(nc.vector.reciprocal(net.recip[:, 2, 0:1], net.recip[:, 1, 0:1]))
            nc.vector.tensor_scalar(net.share[:], net.share[:], net.recip[:, 2, 0:1], None, ALU.mult)
    net.end_phase()


def carve(region, sizes):
    at, start = {}, 0
    for name, size in sizes.items():
        assert start + size <= region.shape[1], (name, start + size, region.shape[1])
        at[name] = region[:, start:start + size]
        start += size
    return at


def program(nc, d, out):
    es = ExitStack()
    with es:
        net = Net(nc, es)
        net.d = d
        sb, sem = net.sb, net.sem
        weights = dict(wf_qkv0=1536, wf_o0=512, wf_10=2 * HID, wf_20=384, wf_qkv1=1536, wf_o1=512, wf_11=2 * HID, wf_21=384,
                       w1q=1024, w1kv=2048, w1o=1024)
        W0, WORK = 4096, 8 * S + 16 * S + 4096 + 8 * BANK
        n_weights = sum(weights.values())
        arena = sb("arena", [P, n_weights + W0 + WORK])
        net.arena = arena
        at = carve(arena[:, 0:n_weights], weights)
        cut = lambda ap, c: ap.rearrange("p (c n) -> p c n", c=c)
        net.wf = [dict(qkv=at[f"wf_qkv{l}"], o=cut(at[f"wf_o{l}"], 4), w1=at[f"wf_1{l}"], w2=cut(at[f"wf_2{l}"], 3)) for l in range(2)]
        net.w1 = dict(q=at["w1q"], kv=at["w1kv"], o=cut(at["w1o"], 8))
        w0_region, work = arena[:, n_weights:n_weights + W0], arena[:, n_weights + W0:n_weights + W0 + WORK]
        w0 = carve(w0_region, dict(q=1024, k=1024, v=1024, o=1024))
        net.w0 = dict(q=w0["q"], k=w0["k"], v=w0["v"], o=cut(w0["o"], 8))
        att = carve(work, dict(probs=4 * BANK, probsT=4 * BANK, qT=8 * S, kT=16 * S, v=4096))
        net.qT, net.kT, net.v = cut(att["qT"], 8), cut(att["kT"], 8), cut(att["v"], 4)
        net.probs, net.probsT = cut(att["probs"], 4), cut(att["probsT"], 4)
        first = carve(att["v"][:, 2048:4096], dict(zT=T * P, band=NT * S, causal=NT * S))
        net.zT_all = cut(first["zT"], B)
        net.first = dict(z=cut(att["probs"][:, 0:T * D], T), band=first["band"], causal=first["causal"],
                         mask0_w=att["probsT"][:, 0:NT * S // 4].bitcast(I32))
        behind = carve(w0_region, dict(ctx=T * D, kv=B * 2 * S, kmask=B * S))
        net.ctx_all, net.kv_all, net.kmask_f = cut(behind["ctx"], T), cut(behind["kv"], B), cut(behind["kmask"], B)[0:1]
        norms = carve(att["kT"], dict(z=T * D, hn=T * D))
        net.prep1 = dict(kmask=att["qT"][0:1, 0:B * S // 4].bitcast(I32), **{n: cut(ap, T) for n, ap in norms.items()})
        both = sb("experts", [P, 2 * (NE1 + 1) * FF])
        experts = carve(both[:], dict(fc=(NE1 + 1) * FF, proj=(NE1 + 1) * 4 * D))
        net.fc, net.proj = cut(experts["fc"], NE1 + 1), experts["proj"].rearrange("p (e c d) -> p e c d", e=NE1 + 1, c=4)
        early = carve(both[:], dict(sin=LT * 2 * BANK, squares=LT * 2 * BANK, cn=T * D))
        net.cn_all = cut(early["cn"], T)
        net.kv_in = sb("kv_in", [P, 2 * S])
        local = carve(w0_region, dict(kT=4 * LB * S, v=LT * BANK))
        mlp = carve(att["kT"], dict(hn=LT * D, hnT=LT * P))
        net.local = dict(qT=cut(att["qT"], 4), kT=cut(local["kT"], 4), v=cut(local["v"], LT), qk=cut(att["kT"], LT), rot=cut(att["v"], LT),
                         sin=cut(early["sin"], LT), squares=cut(early["squares"], LT), hT=net.kv_in[:],
                         hn=cut(mlp["hn"], LT), hnT=mlp["hnT"],
                         gate=cut(att["probsT"][:, 0:3 * LT * P], 3), hid=cut(att["probs"][:, 0:3 * LT * P], 3))
        front, back = arena[:, 0:n_weights], arena[:, n_weights + T * D:n_weights + W0 + WORK]
        l1 = carve(back, dict(z=T * D, zT=T * P, relu=4 * BANK, hid=8 * BANK))
        l2_front = carve(front, dict(ids_i=B * S, ids_f=B * S, mix=8 * BANK, mixT=8 * BANK))
        l2_back = carve(back, dict(z=T * D, zT=T * P, q=2 * T * P, k=2 * T * P, v=T * 2 * D, hot=3 * T * S, junk=12 * S))
        f2 = carve(back, dict(z=T * D, zT=T * P, hn=T * D, hnT=T * P, sums=T * D, hidT=8 * T * P))
        l3 = carve(front, dict(probs=B * 3 * P, probsT=B * 3 * P))
        net.late = dict(z=cut(l1["z"], T), zT=l1["zT"], relu=cut(l1["relu"], 4), hid=l1["hid"].rearrange("p (a m s) -> p a m s", a=2, m=4),
                        ids_i=l2_front["ids_i"][0:1].bitcast(I32), ids_f=l2_front["ids_f"][0:1],
                        mix=l2_front["mix"].rearrange("p (a t l) -> p a t l", a=8, t=NT), mixT=cut(l2_front["mixT"], 8),
                        q=cut(l2_back["q"], 2), k=cut(l2_back["k"], 2), v=cut(l2_back["v"], T), junk=cut(l2_back["junk"], 12),
                        hot=l2_back["hot"].rearrange("p (w t l) -> p w t l", w=3, t=T), meanT=l2_back["z"],
                        hn=cut(f2["hn"], T), hnT=f2["hnT"], sums=cut(f2["sums"], T), hidT=cut(f2["hidT"], 8),
                        hid_rows=cut(front[:, 0:T * NE2 * H2], T), probs3=cut(l3["probs"], B), probsT3=cut(l3["probsT"], B))
        net.router1, net.router2 = sb("router1", [P, NE1]), sb("router2", [P, NE2])
        net.w2x = dict(q=sb("w2q", [P, 2, D]), k=sb("w2k", [P, 2, D]), v=sb("w2v", [P, 2 * D]), o=sb("w2o", [P, D]))
        net.w2f = dict([("in", sb("w2in", [P, NE2 * H2])), ("out", sb("w2out", [P, 2 * NE2, D]))])
        net.before, net.gate_w = net.w2f["out"][:, 0, :], net.w2f["out"][:, 1, 0:NE3 + 2]
        net.cols, net.rows = sb("cols", [P, d["cols"].shape[1]]), sb("rows", [P, d["rows"].shape[1]])
        net.col = lambda name, i: net.cols[:, COLS[name] + i:COLS[name] + i + 1]
        net.row = lambda name, i, n=D: net.rows[:, ROWS[name] + i * n:ROWS[name] + (i + 1) * n]
        net.band, net.causal, net.mask0 = (sb(n, [P, NT * S], BF16) for n in ("band", "causal", "mask0"))
        net.cos_t, net.sin_t = sb("cos_t", [P, 2, NT, 2, DH]), sb("sin_t", [P, 2, NT, 2, DH])
        net.ones, net.ones_b, net.iota = sb("ones", [P, P]), sb("ones_b", [P, P], BF16), sb("iota", [P, S])
        net.share, net.ident = sb("share", [P, 2]), sb("ident", [P, P])
        net.next_row, net.next_tile = sb("next_row", [P, P]), sb("next_tile", [P, P])
        net.x_padded, net.z_padded = sb("x_padded", [P, NT + T, D]), sb("z_padded", [P, NT + T, D])
        net.x_all, net.ctxT_all, net.z = net.x_padded[:, NT:NT + T, :], sb("ctxT_all", [P, B, S]), sb("z", [P, LT, D])
        net.ptr_i = sb("ptr_i", [P, T], I32)
        net.ctxT, net.zT = net.kv_in[:, 0:S], net.kv_in[:, S:2 * S]
        net.kmask, net.kmask_all = sb("kmask", [1, 2 * S], BF16), sb("kmask_all", [P, 2 * S], BF16)
        net.stats, net.mv = sb("stats", [P, 32, 6]), sb("mv", [P, 32, 2])
        net.veps, net.lnv, net.seed, net.nwt = (sb(n, [P, LT * 16]) for n in ("veps", "lnv", "seed", "nwt"))
        net.rstd, net.shift = sb("rstd", [P, 32]), sb("shift", [P, 32])
        net.negmax, net.sums, net.recip = (sb(n, [P, 4, 2]) for n in ("negmax", "sums", "recip"))
        net.ssq, net.rnorm = sb("ssq", [P, LT, 16]), sb("rnorm", [P, LT, 16])
        net.s6, net.comb = sb("s6", [P, 2, T, 3]), sb("comb", [P, T, 8])
        net.small = dict(mx=sb("r_mx", [P, 16]), sm=sb("r_sm", [P, 16]), top=sb("r_top", [P, 8, 8]), idx=sb("r_idx", [P, 8, 8], U32),
                         idxf=sb("r_idxf", [P, 8, 8]), e=sb("r_e", [P, 8, 10]), p8=sb("r_p8", [P, 8, 8]), p4=sb("r_p4", [P, T, 8]),
                         w2=sb("r_w2", [P, T, 2])[:], eq=sb("r_eq", [P, 2, T, 8]), ptr=sb("r_ptr", [P, 4, T]), rel=sb("r_rel", [P, T]),
                         val=sb("r_val", [P, 6, T]), new=sb("r_new", [P, T]), any=sb("r_any", [P, T]), mask=sb("r_mask", [P, 8, 8]),
                         place=sb("r_place", [P, 8, 8]), **{"is": sb("r_is", [P, 5, T])})
        net.ps = es.enter_context(nc.psum_tensor("ps", [P, 8, BANK], F32))

        net.w0_loaded, net.w0_count = sem("w0_loaded"), 16 * 4
        net.tables_loaded, net.tables_count = sem("tables_loaded"), 16 * 9
        net.wf_loaded, net.wf_count = sem("wf_loaded"), 16 * 6
        net.w1_loaded, net.w1_count = sem("w1_loaded"), 16 * 3
        net.w1f_loaded, net.w1f_count = sem("w1f_loaded"), 16 * 3
        net.w2_loaded, net.w2_count = sem("w2_loaded"), 16 * 7
        net.w3_res, net.w3_gate, net.w3_experts = sem("w3_res"), sem("w3_gate"), sem("w3_experts")

        start(net)
        with nc.Fori(0, B) as batch:
            net.batch = batch
            layer0_attention(net)
        prepare_tables(net)
        with nc.Fori(0, B // LB) as turn:
            net.turn = turn
            for l in range(2):
                local_block(net, l)
        prepare_layer1(net)
        with nc.Fori(0, B) as batch:
            net.batch = batch
            layer1_attention(net)
        layer1_experts(net)
        layer2_attention(net)
        layer2_experts(net)
        layer3_attention(net)
        layer3_experts(net, out)


def rotary_tables():
    half = np.arange(0, DH, 2, dtype=np.float32)
    t = np.arange(S, dtype=np.float32)
    angle = t[:, None] * (1.0 / 10000.0 ** (half / DH)).astype(np.float32)[None, :]
    base = (half + 0.4 * DH) / (1.4 * DH)
    scale = base[None, :] ** ((t - S // 2) / 32.0)[:, None]
    scale = np.concatenate([scale, scale], -1)
    cos = np.concatenate([np.cos(angle), np.cos(angle)], -1)
    sin = np.concatenate([-np.sin(angle), np.sin(angle)], -1)
    return [np.ascontiguousarray(np.stack([m * scale, m / scale], 1).reshape(NT, P, 2, DH).transpose(1, 0, 2, 3), dtype=np.float32)
            for m in (cos, sin)]


COLS = dict(L0_ln_g=0, L0_ln_b=2, L0_b1=4, L1_g_x=16, L1_b_x=17, L1_g_l=18, L1_b_l=19, L2_rn_g=20, L2_rn_b=21,
            L2_ln_g=22, L2_ln_b=30, L3_b=38, L3_rb=70, L3_slot=74, L3_nw=82, L3_nb=83, end=84)
ROWS = dict(q_scale=0, k_scale=128, L0_b2=256, L1_g_o=512, L1_b_o=640, L2_on_g=768, L2_on_b=896, council=1024, gain=1026,
            L3_ob=1028, L3_rob=1028 + 1024, end=1028 + 1152)


def packed_columns(a):
    cols = np.zeros((P, COLS["end"]), np.float32)
    for l in range(2):
        cols[:, COLS["L0_ln_g"] + l] = a["L0_ffn_ln_g"][l]
        cols[:, COLS["L0_ln_b"] + l] = a["L0_ffn_ln_b"][l]
        for part in range(2):
            for c, (c0, cn) in enumerate(HC):
                cols[0:cn, COLS["L0_b1"] + 6 * l + 3 * part + c] = a["L0_ffn_b1"][l, part * HID + c0:part * HID + c0 + cn]
    cols[:, COLS["L3_slot"]:COLS["L3_slot"] + NE3] = np.arange(P)[:, None] + CAP * np.arange(NE3)[None, :]
    for name, src in (("L1_g_x", "L1_xattn_g_x"), ("L1_b_x", "L1_xattn_b_x"), ("L1_g_l", "L1_xattn_g_l"), ("L1_b_l", "L1_xattn_b_l"),
                      ("L2_rn_g", "L2_ffn_rn_g"), ("L2_rn_b", "L2_ffn_rn_b"), ("L2_ln_g", "L2_ffn_ln_g"), ("L2_ln_b", "L2_ffn_ln_b"),
                      ("L3_nw", "L3_ffn_attn_nw"), ("L3_nb", "L3_ffn_attn_nb"), ("L3_b", "L3_ffn_inter_b"), ("L3_rb", "L3_ffn_res_inter_b")):
        n = a[src].size // P
        cols[:, COLS[name]:COLS[name] + n] = a[src].reshape(n, P).T
    return cols


def packed_rows(a):
    row = np.zeros(ROWS["end"], np.float32)
    for name, src in (("q_scale", "L0_ffn_q_scale"), ("k_scale", "L0_ffn_k_scale"), ("L0_b2", "L0_ffn_b2"), ("L1_g_o", "L1_xattn_g_o"),
                      ("L1_b_o", "L1_xattn_b_o"), ("L2_on_g", "L2_ffn_on_g"), ("L2_on_b", "L2_ffn_on_b"),
                      ("council", "L2_xattn_council_weights"), ("gain", "L2_xattn_gain"), ("L3_ob", "L3_ffn_output_b"), ("L3_rob", "L3_ffn_res_output_b")):
        row[ROWS[name]:ROWS[name] + a[src].size] = a[src].reshape(-1)
    return np.ascontiguousarray(np.broadcast_to(row, (P, row.size)))


def laid_out(inputs):
    a = {k: np.asarray(v) for k, v in inputs.items()}
    c = np.ascontiguousarray
    cos, sin = rotary_tables()
    far = np.arange(S)[:, None] - np.arange(S)[None, :]
    return {
        "x": a["x"], "ctx": a["ctx_1024"], "ctxT": c(a["ctx_1024"].transpose(0, 2, 1)),
        "ids": a["itok_BxS_0_7"], "ptr": c(a["itok_BxS_0_4092"].reshape(B, NT, P).transpose(0, 2, 1)),
        "mask0": c(a["mask_1x1xSxS2_bk1"].reshape(S, S)).view(np.int32), "kmask": c(a["mask_BxS2_bf1"]).view(np.int32),
        **{k: a[k] for k in ("L0_xattn_w_q", "L0_xattn_w_k", "L0_xattn_w_v", "L0_xattn_w_o")},
        **{k: a[k] for k in ("L0_ffn_wqkv", "L0_ffn_wo", "L0_ffn_w1", "L0_ffn_w2")},
        "cols": packed_columns(a), "rows": packed_rows(a), "cos": cos, "sin": sin,
        "band": ((far < 0) | (far > 64)).astype(np.float32),
        "causal": (far < 0).astype(np.float32),
        "iota": np.ascontiguousarray(np.broadcast_to(np.arange(NE3 * CAP, dtype=np.float32), (P, NE3 * CAP))),
        **{k: a[k] for k in ("L1_xattn_Wq", "L1_xattn_Wkv", "L1_xattn_Wout")},
        "fc": c(np.concatenate([a["L1_ffn_w_fc"], a["L1_ffn_shared_fc"][None]]).transpose(2, 0, 1)),
        "proj": c(np.concatenate([a["L1_ffn_w_proj"], a["L1_ffn_shared_proj"][None]]).reshape(NE1 + 1, D, 4, P).transpose(3, 0, 2, 1)),
        "router1": c(a["L1_ffn_router_w"].T), "router2": c(a["L2_ffn_router_w"].T),
        "w2q": c(np.stack([a["L2_xattn_Wqj"].T, a["L2_xattn_Wqi"].T], 1)), "w2k": c(np.stack([a["L2_xattn_Wkj"].T, a["L2_xattn_Wki"].T], 1)),
        "w2v": c(np.concatenate([a["L2_xattn_Wvj"].T, a["L2_xattn_Wvi"].T], 1)), "w2o": c(a["L2_xattn_Wout"].T),
        "w2in": c(a["L2_ffn_w1"].transpose(1, 0, 2).reshape(D, NE2 * H2)),
        "w2out": c(a["L2_ffn_w2"].reshape(2 * NE2, P, D).transpose(1, 0, 2)),
        "before": c((far[0:P, 0:P] < 0).astype(np.float32)), "gate": c(np.concatenate([a["L3_ffn_wg"], a["L3_ffn_res_coef"]], 1)),
        "res_in": a["L3_ffn_res_inter_w"], "res_out": c(a["L3_ffn_res_output_w"].reshape(4, P, D).transpose(1, 0, 2)),
        "inter": c(a["L3_ffn_inter_w"].transpose(1, 0, 2)),
        "output": c(a["L3_ffn_output_w"].reshape(NE3, 4, P, D).transpose(2, 0, 1, 3)),
        "ident": np.eye(P, dtype=np.float32),
        "next_row": np.eye(P, k=1, dtype=np.float32), "next_tile": np.eye(P, k=P - 1, dtype=np.float32).T.copy(),
    }


def kernel(**inputs):
    import concourse.bacc as bacc
    from concourse.bass_utils import run_bass_kernel_spmd

    nc = bacc.Bacc("TRN2", target_bir_lowering=False, num_devices=1)
    arrays = {f"in_{k}": v for k, v in laid_out(inputs).items()}
    d = {k[3:]: nc.dram_tensor(k, v.shape, mybir.dt.from_np(v.dtype), kind="ExternalInput").ap() for k, v in arrays.items()}
    out = nc.dram_tensor("out", (B, S, D), F32, kind="ExternalOutput").ap()
    program(nc, d, out)
    return run_bass_kernel_spmd(nc, [arrays], core_ids=[0]).results[0]["out"]
```
